# Optimizing a Trainium2 kernel written in Bass

```python
import numpy as np
import jax
import jax.numpy as jnp

def _softmax(x, axis=-1):
    return jax.nn.softmax(x, axis=axis)

def _gelu(x):
    return jax.nn.gelu(x, approximate=True)

def _silu(x):
    return jax.nn.silu(x)

def _sigmoid(x):
    return jax.nn.sigmoid(x)

def _layernorm(x, axis=-1, eps=1e-05):
    m = jnp.mean(x, axis=axis, keepdims=True)
    v = jnp.var(x, axis=axis, keepdims=True)
    return (x - m) / jnp.sqrt(v + eps)

def _scatter_add(tgt, idx, src, axis=0):
    return tgt.at[idx].add(src)

def _segment_sum(src, seg, n):
    return jax.ops.segment_sum(src, seg, n)
kernel_name = 'mk_decoder_preln_d2_seqx_r8_57b235'

def setup_inputs(seed: int=0):
    np.random.seed(seed)
    _w = jnp.asarray

    def _rec_inputs():
        import jax
        import jax.numpy as jnp
        _rk = jax.random.key(seed)
        x = -0.0002928 + 1 * jax.random.normal(jax.random.fold_in(_rk, 1), (64, 64, 128), jnp.float32)
        _lenS = 64 - jax.random.randint(jax.random.fold_in(_rk, 7), (64,), 0, max(1, 64 // 4) + 1, jnp.int32)
        _lenS2 = 64 - jax.random.randint(jax.random.fold_in(_rk, 8), (64,), 0, max(1, 64 // 4) + 1, jnp.int32)
        _ctx_1024P = jax.random.normal(jax.random.fold_in(_rk, 11), (64, 16, 128), jnp.float32)
        _ctx_1024c = jax.random.dirichlet(jax.random.fold_in(_rk, 511), 0.3 * jnp.ones((16,), jnp.float32), (64, 64))
        _ctx_1024t = jnp.einsum('bsk,bkd->bsd', _ctx_1024c, _ctx_1024P)
        _ctx_1024t = _ctx_1024t * jax.lax.rsqrt(jnp.mean(jnp.square(_ctx_1024t)) + 1e-12) * 0.953939
        ctx_1024 = -1.39393e-06 + 0.999914 * (_ctx_1024t + 0.3 * jax.random.normal(jax.random.fold_in(_rk, 611), (64, 64, 128), jnp.float32))
        return (x, ctx_1024)
    x, ctx_1024 = _rec_inputs()

    def _L0_attn_setup():
        import jax, jax.numpy as jnp
        import numpy as np
        D_MODEL = 128
        NUM_HEADS = 16
        HEAD_DIM = D_MODEL // NUM_HEADS
        key = jax.random.key(seed)
        ks = jax.random.split(key, 7)
        B, T, C = (4, 256, D_MODEL)
        s = 1.0 / np.sqrt(C)
        return {'x': jax.random.normal(ks[0], (B, T, C), dtype=jnp.float32), 'ln_gamma': jnp.ones((C,), dtype=jnp.float32), 'ln_beta': jnp.zeros((C,), dtype=jnp.float32), 'w_qkv': jax.random.normal(ks[1], (C, 3 * C), dtype=jnp.float32) * s, 'b_qkv': jnp.zeros((3 * C,), dtype=jnp.float32), 'w_out': jax.random.normal(ks[2], (C, C), dtype=jnp.float32) * s, 'b_out': jnp.zeros((C,), dtype=jnp.float32)}
    _L0_attn_all = _L0_attn_setup()
    _L0_attn_in = {k: v for k, v in _L0_attn_all.items() if k in ('ln_gamma', 'ln_beta', 'w_qkv', 'b_qkv', 'w_out', 'b_out')}
    del _L0_attn_all

    def _L0_xattn_setup():
        import jax, jax.numpy as jnp
        import numpy as np
        B, S, D, H = (2, 256, 128, 16)
        DH = D // H

        def _split(x):
            b, s, d = x.shape
            return x.reshape(b, s, H, DH).transpose(0, 2, 1, 3)
        key = jax.random.key(seed)
        ks = jax.random.split(key, 11)
        sc = 1.0 / np.sqrt(D)
        return {'q': jax.random.normal(ks[0], (B, S, D), jnp.float32), 'k': jax.random.normal(ks[1], (B, S, D), jnp.float32), 'v': jax.random.normal(ks[2], (B, S, D), jnp.float32), 'Wq': jax.random.normal(ks[3], (D, D), jnp.float32) * sc, 'bq': jnp.zeros((D,), jnp.float32), 'Wk': jax.random.normal(ks[4], (D, D), jnp.float32) * sc, 'bk': jnp.zeros((D,), jnp.float32), 'Wv': jax.random.normal(ks[5], (D, D), jnp.float32) * sc, 'bv': jnp.zeros((D,), jnp.float32), 'Wo': jax.random.normal(ks[6], (D, D), jnp.float32) * sc, 'bo': jnp.zeros((D,), jnp.float32)}
    _L0_xattn_all = _L0_xattn_setup()
    _L0_xattn_in = {k: v for k, v in _L0_xattn_all.items() if k in ('Wq', 'bq', 'Wk', 'bk', 'Wv', 'bv', 'Wo', 'bo')}
    del _L0_xattn_all

    def _L0_ffn_setup():
        import jax, jax.numpy as jnp
        import numpy as np
        B, T, C, H, E, K, F = (2, 256, 128, 16, 8, 2, 256)
        EPS = 1e-05

        def layernorm(x, w):
            m = x.mean(-1, keepdims=True)
            v = x.var(-1, keepdims=True)
            return (x - m) * jax.lax.rsqrt(v + EPS) * w

        def attention(x, c_attn_w, c_proj_w):
            b, t, c = x.shape
            hd = c // H
            q, k, v = jnp.split(x @ c_attn_w, 3, axis=-1)
            q = q.reshape(b, t, H, hd).transpose(0, 2, 1, 3)
            k = k.reshape(b, t, H, hd).transpose(0, 2, 1, 3)
            v = v.reshape(b, t, H, hd).transpose(0, 2, 1, 3)
            att = jnp.einsum('bhqd,bhkd->bhqk', q, k) / jnp.sqrt(jnp.asarray(hd, x.dtype))
            causal = jnp.tril(jnp.ones((t, t), bool))
            att = jnp.where(causal, att, jnp.asarray(-jnp.inf, att.dtype))
            att = jax.nn.softmax(att, axis=-1)
            y = jnp.einsum('bhqk,bhkd->bhqd', att, v)
            y = y.transpose(0, 2, 1, 3).reshape(b, t, c)
            return y @ c_proj_w

        def moe_mlp(x, router_w, w1, w2):
            b, t, c = x.shape
            xf = x.reshape(-1, c)
            router_logits = xf @ router_w
            probs = jax.nn.softmax(router_logits.astype(jnp.float32), axis=-1)
            rw, sel = jax.lax.top_k(probs, K)
            rw = rw / rw.sum(axis=-1, keepdims=True)
            rw = rw.astype(x.dtype)
            w1e = w1.reshape(c, E, F).transpose(1, 0, 2)
            w2e = w2.reshape(E, F, c)
            h = jax.nn.gelu(jnp.einsum('nc,ecf->enf', xf, w1e), approximate=False)
            y_all = jnp.einsum('enf,efc->nec', h, w2e)
            y_sel = jnp.take_along_axis(y_all, sel[:, :, None], axis=1)
            y = (y_sel * rw[:, :, None]).sum(axis=1)
            return y.reshape(b, t, c)
        key = jax.random.key(seed)
        ks = jax.random.split(key, 6)
        s = 0.02
        return {'x': jax.random.normal(ks[0], (B, T, C), jnp.float32), 'ln1_w': jnp.ones((C,), jnp.float32), 'c_attn_w': jax.random.normal(ks[1], (C, 3 * C), jnp.float32) * s, 'c_proj_w': jax.random.normal(ks[2], (C, C), jnp.float32) * s, 'ln2_w': jnp.ones((C,), jnp.float32), 'router_w': jax.random.normal(ks[3], (C, E), jnp.float32) * s, 'w1': jnp.clip(jax.random.normal(ks[4], (C, E * F), jnp.float32) * s, -0.06, 0.06), 'w2': jnp.clip(jax.random.normal(ks[5], (E * F, C), jnp.float32) * s, -0.06, 0.06)}
    _L0_ffn_all = _L0_ffn_setup()
    _L0_ffn_in = {k: v for k, v in _L0_ffn_all.items() if k in ('ln1_w', 'c_attn_w', 'c_proj_w', 'ln2_w', 'router_w', 'w1', 'w2')}
    del _L0_ffn_all

    def _L1_attn_setup():
        import jax, jax.numpy as jnp
        import numpy as np
        N_HEAD = 16
        N_KV = 4
        BITS = 8
        EPS = 1e-06

        def fake_quant(x, bits=BITS):
            qmax = 2.0 ** bits - 1.0
            mn, mx = (jnp.min(x), jnp.max(x))
            scale = (mx - mn) / qmax + 1e-12
            zp = jnp.round(-mn / scale)
            dq = (jnp.clip(jnp.round(x / scale) + zp, 0.0, qmax) - zp) * scale
            return x + jax.lax.stop_gradient(dq - x)

        def rope(x):
            D, T = (x.shape[-1], x.shape[-2])
            inv_freq = 1.0 / 10000.0 ** (jnp.arange(0, D, 2, dtype=jnp.float32) / D)
            freqs = jnp.arange(T, dtype=jnp.float32)[:, None] * inv_freq[None, :]
            cos = jnp.concatenate([jnp.cos(freqs)] * 2, axis=-1)
            sin = jnp.concatenate([jnp.sin(freqs)] * 2, axis=-1)
            x1, x2 = jnp.split(x, 2, axis=-1)
            rot = jnp.concatenate([-x2, x1], axis=-1)
            return x * cos + rot * sin

        def fire_bias(T, w1, b1, w2, b2, c, L):
            pos = jnp.arange(T, dtype=jnp.float32)
            rel = pos[:, None] - pos[None, :]
            thresh = jnp.abs(L)
            pos_norm = jnp.maximum(pos, thresh)[:, None]
            rd = jnp.log(jnp.abs(c * rel) + 1.0)
            pn = jnp.log(jnp.abs(c * pos_norm) + 1.0) + EPS
            nd = rd / pn
            h = jax.nn.relu(nd[..., None] @ w1 + b1)
            bias = h @ w2 + b2
            return jnp.transpose(bias, (2, 0, 1))[None]
        key = jax.random.key(seed)
        ks = jax.random.split(key, 8)
        B, T, C = (1, 256, 128)
        kv_dim = C // N_HEAD * N_KV
        s = 0.02
        return {'x': jax.random.normal(ks[0], (B, T, C), jnp.float32), 'Wq': jax.random.normal(ks[1], (C, C), jnp.float32) * s, 'Wk': jax.random.normal(ks[2], (C, kv_dim), jnp.float32) * s, 'Wv': jax.random.normal(ks[3], (C, kv_dim), jnp.float32) * s, 'Wproj': jax.random.normal(ks[4], (C, C), jnp.float32) * s, 'fire_w1': jax.random.normal(ks[5], (1, 32), jnp.float32) * 0.1, 'fire_b1': jnp.zeros((32,), jnp.float32), 'fire_w2': jax.random.normal(ks[6], (32, N_HEAD), jnp.float32) * 0.1, 'fire_b2': jnp.zeros((N_HEAD,), jnp.float32), 'fire_c': jnp.full((1,), 0.1, jnp.float32), 'fire_L': jnp.full((1,), 512.0, jnp.float32)}
    _L1_attn_all = _L1_attn_setup()
    _L1_attn_in = {k: v for k, v in _L1_attn_all.items() if k in ('Wq', 'Wk', 'Wv', 'Wproj', 'fire_w1', 'fire_b1', 'fire_w2', 'fire_b2', 'fire_c', 'fire_L')}
    del _L1_attn_all

    def _L1_xattn_setup():
        import jax, jax.numpy as jnp
        import numpy as np
        NUM_HEADS = 8

        def _split_heads(x, h):
            b, n, c = x.shape
            return x.reshape(b, n, h, c // h).transpose(0, 2, 1, 3)
        key = jax.random.key(seed)
        ks = jax.random.split(key, 5)
        B, N, K, C = (16, 512, 64, 128)
        return {'img_fea': jax.random.normal(ks[0], (B, N, C), dtype=jnp.float32), 'aud_fea': jax.random.normal(ks[1], (B, K, C), dtype=jnp.float32), 'Wq': jax.random.normal(ks[2], (C, C), dtype=jnp.float32) * 0.02, 'Wk': jax.random.normal(ks[3], (C, C), dtype=jnp.float32) * 0.02, 'Wv': jax.random.normal(ks[4], (C, C), dtype=jnp.float32) * 0.02, 'aq': 1, 'sigmoid': 0, 'softmax': 1}
    _L1_xattn_all = _L1_xattn_setup()
    _L1_xattn_in = {k: v for k, v in _L1_xattn_all.items() if k in ('Wq', 'Wk', 'Wv')}
    del _L1_xattn_all

    def _L1_ffn_setup():
        import jax, jax.numpy as jnp
        import numpy as np
        EPS = 1e-05

        def _layernorm(x, w, b):
            mu = jnp.mean(x, axis=-1, keepdims=True)
            var = jnp.mean((x - mu) ** 2, axis=-1, keepdims=True)
            return (x - mu) * jax.lax.rsqrt(var + EPS) * w + b

        def _rope_tables(T, D, base=10000.0):
            inv_freq = 1.0 / base ** (jnp.arange(0, D, 2, dtype=jnp.float32) / D)
            t = jnp.arange(T, dtype=jnp.float32)
            freqs = jnp.einsum('i,j->ij', t, inv_freq)
            emb = jnp.concatenate([freqs, freqs], axis=-1)
            return (jnp.cos(emb), jnp.sin(emb))

        def _rotate_half(x):
            x1, x2 = (x[..., :x.shape[-1] // 2], x[..., x.shape[-1] // 2:])
            return jnp.concatenate([-x2, x1], axis=-1)

        def _attn(x, ln_w, ln_b, conv_w, attn_w, proj_w, n_head):
            B, T, C = x.shape
            D = C // n_head
            h = _layernorm(x, ln_w, ln_b)
            hc = jnp.transpose(h, (0, 2, 1))
            hc = jnp.pad(hc, ((0, 0), (0, 0), (2, 0)))
            hc = jax.lax.conv_general_dilated(hc, conv_w, window_strides=(1,), padding='VALID', dimension_numbers=('NCH', 'OIH', 'NCH'), feature_group_count=C)
            h = jnp.transpose(hc, (0, 2, 1))
            qkv = h @ attn_w
            q, k, v = jnp.split(qkv, 3, axis=-1)
            q = q.reshape(B, T, n_head, D)
            k = k.reshape(B, T, n_head, D)
            v = v.reshape(B, T, n_head, D)
            cos, sin = _rope_tables(T, D)
            cos = cos[None, :, None, :]
            sin = sin[None, :, None, :]
            q = q * cos + _rotate_half(q) * sin
            k = k * cos + _rotate_half(k) * sin
            scores = jnp.einsum('bqhd,bkhd->bhqk', q, k) / jnp.sqrt(jnp.float32(D))
            causal = jnp.tril(jnp.ones((T, T), dtype=bool))
            scores = jnp.where(causal, scores, jnp.float32(-1e+30))
            p = jax.nn.softmax(scores, axis=-1)
            y = jnp.einsum('bhqk,bkhd->bqhd', p, v).reshape(B, T, C)
            return y @ proj_w

        def _moe(x, ln_w, ln_b, router_w, expert_wv, expert_proj):
            h = _layernorm(x, ln_w, ln_b)
            logits = h @ router_w
            expert_idx = jnp.argmax(logits, axis=-1)
            E = router_w.shape[-1]
            out = jnp.zeros_like(x)
            for e in range(E):
                gv = h @ expert_wv[e]
                gate_raw, value = jnp.split(gv, 2, axis=-1)
                y = gate_raw * jax.nn.sigmoid(gate_raw) * value @ expert_proj[e]
                out = out + jnp.where((expert_idx == e)[..., None], y, 0.0)
            return out
        C, H, E, B, T = (128, 16, 4, 4, 128)
        Dff = 4 * C
        key = jax.random.key(seed)
        ks = jax.random.split(key, 8)
        s = 0.02
        return {'x': jax.random.normal(ks[0], (B, T, C), dtype=jnp.float32), 'ln1_w': jnp.ones((C,), jnp.float32), 'ln1_b': jnp.zeros((C,), jnp.float32), 'ln2_w': jnp.ones((C,), jnp.float32), 'ln2_b': jnp.zeros((C,), jnp.float32), 'conv_w': jax.random.normal(ks[1], (C, 1, 3), dtype=jnp.float32) * 0.1, 'attn_w': jax.random.normal(ks[2], (C, 3 * C), dtype=jnp.float32) * s, 'proj_w': jax.random.normal(ks[3], (C, C), dtype=jnp.float32) * s, 'router_w': jax.random.normal(ks[4], (C, E), dtype=jnp.float32) * s, 'expert_wv': jax.random.normal(ks[5], (E, C, 2 * Dff), dtype=jnp.float32) * s, 'expert_proj': jax.random.normal(ks[6], (E, Dff, C), dtype=jnp.float32) * s}
    _L1_ffn_all = _L1_ffn_setup()
    _L1_ffn_in = {k: v for k, v in _L1_ffn_all.items() if k in ('ln1_w', 'ln1_b', 'ln2_w', 'ln2_b', 'conv_w', 'attn_w', 'proj_w', 'router_w', 'expert_wv', 'expert_proj')}
    del _L1_ffn_all
    return {'x': x, 'ctx_1024': ctx_1024, 'L0_attn_ln_gamma': _L0_attn_in['ln_gamma'], 'L0_attn_ln_beta': _L0_attn_in['ln_beta'], 'L0_attn_w_qkv': _L0_attn_in['w_qkv'], 'L0_attn_b_qkv': _L0_attn_in['b_qkv'], 'L0_attn_w_out': _L0_attn_in['w_out'], 'L0_attn_b_out': _L0_attn_in['b_out'], 'L0_xattn_Wq': _L0_xattn_in['Wq'], 'L0_xattn_bq': _L0_xattn_in['bq'], 'L0_xattn_Wk': _L0_xattn_in['Wk'], 'L0_xattn_bk': _L0_xattn_in['bk'], 'L0_xattn_Wv': _L0_xattn_in['Wv'], 'L0_xattn_bv': _L0_xattn_in['bv'], 'L0_xattn_Wo': _L0_xattn_in['Wo'], 'L0_xattn_bo': _L0_xattn_in['bo'], 'L0_ffn_ln1_w': _L0_ffn_in['ln1_w'], 'L0_ffn_c_attn_w': _L0_ffn_in['c_attn_w'], 'L0_ffn_c_proj_w': _L0_ffn_in['c_proj_w'], 'L0_ffn_ln2_w': _L0_ffn_in['ln2_w'], 'L0_ffn_router_w': _L0_ffn_in['router_w'], 'L0_ffn_w1': _L0_ffn_in['w1'], 'L0_ffn_w2': _L0_ffn_in['w2'], 'L1_attn_Wq': _L1_attn_in['Wq'], 'L1_attn_Wk': _L1_attn_in['Wk'], 'L1_attn_Wv': _L1_attn_in['Wv'], 'L1_attn_Wproj': _L1_attn_in['Wproj'], 'L1_attn_fire_w1': _L1_attn_in['fire_w1'], 'L1_attn_fire_b1': _L1_attn_in['fire_b1'], 'L1_attn_fire_w2': _L1_attn_in['fire_w2'], 'L1_attn_fire_b2': _L1_attn_in['fire_b2'], 'L1_attn_fire_c': _L1_attn_in['fire_c'], 'L1_attn_fire_L': _L1_attn_in['fire_L'], 'L1_xattn_Wq': _L1_xattn_in['Wq'], 'L1_xattn_Wk': _L1_xattn_in['Wk'], 'L1_xattn_Wv': _L1_xattn_in['Wv'], 'L1_ffn_ln1_w': _L1_ffn_in['ln1_w'], 'L1_ffn_ln1_b': _L1_ffn_in['ln1_b'], 'L1_ffn_ln2_w': _L1_ffn_in['ln2_w'], 'L1_ffn_ln2_b': _L1_ffn_in['ln2_b'], 'L1_ffn_conv_w': _L1_ffn_in['conv_w'], 'L1_ffn_attn_w': _L1_ffn_in['attn_w'], 'L1_ffn_proj_w': _L1_ffn_in['proj_w'], 'L1_ffn_router_w': _L1_ffn_in['router_w'], 'L1_ffn_expert_wv': _L1_ffn_in['expert_wv'], 'L1_ffn_expert_proj': _L1_ffn_in['expert_proj']}

def reference(x, ctx_1024, L0_attn_ln_gamma, L0_attn_ln_beta, L0_attn_w_qkv, L0_attn_b_qkv, L0_attn_w_out, L0_attn_b_out, L0_xattn_Wq, L0_xattn_bq, L0_xattn_Wk, L0_xattn_bk, L0_xattn_Wv, L0_xattn_bv, L0_xattn_Wo, L0_xattn_bo, L0_ffn_ln1_w, L0_ffn_c_attn_w, L0_ffn_c_proj_w, L0_ffn_ln2_w, L0_ffn_router_w, L0_ffn_w1, L0_ffn_w2, L1_attn_Wq, L1_attn_Wk, L1_attn_Wv, L1_attn_Wproj, L1_attn_fire_w1, L1_attn_fire_b1, L1_attn_fire_w2, L1_attn_fire_b2, L1_attn_fire_c, L1_attn_fire_L, L1_xattn_Wq, L1_xattn_Wk, L1_xattn_Wv, L1_ffn_ln1_w, L1_ffn_ln1_b, L1_ffn_ln2_w, L1_ffn_ln2_b, L1_ffn_conv_w, L1_ffn_attn_w, L1_ffn_proj_w, L1_ffn_router_w, L1_ffn_expert_wv, L1_ffn_expert_proj):
    import jax
    import jax.numpy as jnp

    def _L0_attn_ref(x, ln_gamma, ln_beta, w_qkv, b_qkv, w_out, b_out):
        import jax, jax.numpy as jnp
        import numpy as np
        D_MODEL = 128
        NUM_HEADS = 16
        HEAD_DIM = D_MODEL // NUM_HEADS
        B, T, C = x.shape
        residual = x
        mu = jnp.mean(x, axis=-1, keepdims=True)
        var = jnp.var(x, axis=-1, keepdims=True)
        h = (x - mu) * jax.lax.rsqrt(var + 1e-05) * ln_gamma + ln_beta
        qkv = (h @ w_qkv + b_qkv).reshape(B, T, 3, NUM_HEADS, HEAD_DIM)
        qkv = jnp.transpose(qkv, (2, 0, 3, 1, 4))
        q, k, v = (qkv[0], qkv[1], qkv[2])
        scores = jnp.einsum('bhqd,bhkd->bhqk', q, k) / np.sqrt(HEAD_DIM)
        attn = jax.nn.softmax(scores, axis=-1)
        out = jnp.einsum('bhqk,bhkd->bhqd', attn, v)
        out = jnp.transpose(out, (0, 2, 1, 3)).reshape(B, T, C)
        out = out @ w_out + b_out
        return residual + out

    def _L0_xattn_ref(q, k, v, Wq, bq, Wk, bk, Wv, bv, Wo, bo):
        import jax, jax.numpy as jnp
        import numpy as np
        B, S, D, H = (2, 256, 128, 16)
        DH = D // H

        def _split(x):
            b, s, d = x.shape
            return x.reshape(b, s, H, DH).transpose(0, 2, 1, 3)
        qh = _split(q @ Wq + bq)
        kh = _split(k @ Wk + bk)
        vh = _split(v @ Wv + bv)
        scale = 1.0 / jnp.sqrt(jnp.asarray(DH, qh.dtype))
        scores = jnp.einsum('bhqd,bhkd->bhqk', qh, kh) * scale
        attn = jax.nn.softmax(scores, axis=-1)
        ctx = jnp.einsum('bhqk,bhkd->bhqd', attn, vh)
        ctx = ctx.transpose(0, 2, 1, 3).reshape(q.shape[0], q.shape[1], D)
        return ctx @ Wo + bo

    def _L0_ffn_ref(x, ln1_w, c_attn_w, c_proj_w, ln2_w, router_w, w1, w2):
        import jax, jax.numpy as jnp
        import numpy as np
        B, T, C, H, E, K, F = (2, 256, 128, 16, 8, 2, 256)
        EPS = 1e-05

        def layernorm(x, w):
            m = x.mean(-1, keepdims=True)
            v = x.var(-1, keepdims=True)
            return (x - m) * jax.lax.rsqrt(v + EPS) * w

        def attention(x, c_attn_w, c_proj_w):
            b, t, c = x.shape
            hd = c // H
            q, k, v = jnp.split(x @ c_attn_w, 3, axis=-1)
            q = q.reshape(b, t, H, hd).transpose(0, 2, 1, 3)
            k = k.reshape(b, t, H, hd).transpose(0, 2, 1, 3)
            v = v.reshape(b, t, H, hd).transpose(0, 2, 1, 3)
            att = jnp.einsum('bhqd,bhkd->bhqk', q, k) / jnp.sqrt(jnp.asarray(hd, x.dtype))
            causal = jnp.tril(jnp.ones((t, t), bool))
            att = jnp.where(causal, att, jnp.asarray(-jnp.inf, att.dtype))
            att = jax.nn.softmax(att, axis=-1)
            y = jnp.einsum('bhqk,bhkd->bhqd', att, v)
            y = y.transpose(0, 2, 1, 3).reshape(b, t, c)
            return y @ c_proj_w

        def moe_mlp(x, router_w, w1, w2):
            b, t, c = x.shape
            xf = x.reshape(-1, c)
            router_logits = xf @ router_w
            probs = jax.nn.softmax(router_logits.astype(jnp.float32), axis=-1)
            rw, sel = jax.lax.top_k(probs, K)
            rw = rw / rw.sum(axis=-1, keepdims=True)
            rw = rw.astype(x.dtype)
            w1e = w1.reshape(c, E, F).transpose(1, 0, 2)
            w2e = w2.reshape(E, F, c)
            h = jax.nn.gelu(jnp.einsum('nc,ecf->enf', xf, w1e), approximate=False)
            y_all = jnp.einsum('enf,efc->nec', h, w2e)
            y_sel = jnp.take_along_axis(y_all, sel[:, :, None], axis=1)
            y = (y_sel * rw[:, :, None]).sum(axis=1)
            return y.reshape(b, t, c)
        x = x + attention(layernorm(x, ln1_w), c_attn_w, c_proj_w)
        x = x + moe_mlp(layernorm(x, ln2_w), router_w, w1, w2)
        return x

    def _L1_attn_ref(x, Wq, Wk, Wv, Wproj, fire_w1, fire_b1, fire_w2, fire_b2, fire_c, fire_L):
        import jax, jax.numpy as jnp
        import numpy as np
        N_HEAD = 16
        N_KV = 4
        BITS = 8
        EPS = 1e-06

        def fake_quant(x, bits=BITS):
            qmax = 2.0 ** bits - 1.0
            mn, mx = (jnp.min(x), jnp.max(x))
            scale = (mx - mn) / qmax + 1e-12
            zp = jnp.round(-mn / scale)
            dq = (jnp.clip(jnp.round(x / scale) + zp, 0.0, qmax) - zp) * scale
            return x + jax.lax.stop_gradient(dq - x)

        def rope(x):
            D, T = (x.shape[-1], x.shape[-2])
            inv_freq = 1.0 / 10000.0 ** (jnp.arange(0, D, 2, dtype=jnp.float32) / D)
            freqs = jnp.arange(T, dtype=jnp.float32)[:, None] * inv_freq[None, :]
            cos = jnp.concatenate([jnp.cos(freqs)] * 2, axis=-1)
            sin = jnp.concatenate([jnp.sin(freqs)] * 2, axis=-1)
            x1, x2 = jnp.split(x, 2, axis=-1)
            rot = jnp.concatenate([-x2, x1], axis=-1)
            return x * cos + rot * sin

        def fire_bias(T, w1, b1, w2, b2, c, L):
            pos = jnp.arange(T, dtype=jnp.float32)
            rel = pos[:, None] - pos[None, :]
            thresh = jnp.abs(L)
            pos_norm = jnp.maximum(pos, thresh)[:, None]
            rd = jnp.log(jnp.abs(c * rel) + 1.0)
            pn = jnp.log(jnp.abs(c * pos_norm) + 1.0) + EPS
            nd = rd / pn
            h = jax.nn.relu(nd[..., None] @ w1 + b1)
            bias = h @ w2 + b2
            return jnp.transpose(bias, (2, 0, 1))[None]
        B, T, C = x.shape
        H, G = (N_HEAD, N_KV)
        hs = C // H
        q = jnp.transpose((x @ Wq).reshape(B, T, H, hs), (0, 2, 1, 3))
        k = jnp.transpose((x @ Wk).reshape(B, T, G, hs), (0, 2, 1, 3))
        v = jnp.transpose((x @ Wv).reshape(B, T, G, hs), (0, 2, 1, 3))
        q, k = (rope(q), rope(k))
        q = fake_quant(q)
        k = fake_quant(k)
        kr = jnp.repeat(k, H // G, axis=1)
        att = jnp.einsum('bhqd,bhkd->bhqk', q, kr) / jnp.sqrt(jnp.float32(hs))
        att = att + fire_bias(T, fire_w1, fire_b1, fire_w2, fire_b2, fire_c, fire_L)
        causal = jnp.tril(jnp.ones((T, T), bool))
        att = jnp.where(causal, att, -jnp.inf)
        att = jax.nn.softmax(att, axis=-1)
        att = fake_quant(att)
        vr = jnp.repeat(fake_quant(v), H // G, axis=1)
        y = jnp.einsum('bhqk,bhkd->bhqd', att, vr)
        y = fake_quant(y)
        y = jnp.transpose(y, (0, 2, 1, 3)).reshape(B, T, C)
        return y @ Wproj

    def _L1_xattn_ref(img_fea, aud_fea, Wq, Wk, Wv, aq, sigmoid, softmax):
        import jax, jax.numpy as jnp
        import numpy as np
        NUM_HEADS = 8

        def _split_heads(x, h):
            b, n, c = x.shape
            return x.reshape(b, n, h, c // h).transpose(0, 2, 1, 3)
        if aq:
            query, key, value = (aud_fea, img_fea, img_fea)
        else:
            query, key, value = (img_fea, aud_fea, aud_fea)
        B, Nq, C = query.shape
        h = NUM_HEADS
        scale = (C // h) ** (-0.5)
        q = _split_heads(query @ Wq.T, h)
        k = _split_heads(key @ Wk.T, h)
        v = _split_heads(value @ Wv.T, h)
        attn = jnp.einsum('bhnd,bhmd->bhnm', q, k) * scale
        if sigmoid:
            attn = jax.nn.sigmoid(attn)
        if softmax:
            attn = jax.nn.softmax(attn, axis=-1)
        x = jnp.einsum('bhnm,bhmd->bhnd', attn, v)
        return x.transpose(0, 2, 1, 3).reshape(B, Nq, C)

    def _L1_ffn_ref(x, ln1_w, ln1_b, ln2_w, ln2_b, conv_w, attn_w, proj_w, router_w, expert_wv, expert_proj):
        import jax, jax.numpy as jnp
        import numpy as np
        EPS = 1e-05

        def _layernorm(x, w, b):
            mu = jnp.mean(x, axis=-1, keepdims=True)
            var = jnp.mean((x - mu) ** 2, axis=-1, keepdims=True)
            return (x - mu) * jax.lax.rsqrt(var + EPS) * w + b

        def _rope_tables(T, D, base=10000.0):
            inv_freq = 1.0 / base ** (jnp.arange(0, D, 2, dtype=jnp.float32) / D)
            t = jnp.arange(T, dtype=jnp.float32)
            freqs = jnp.einsum('i,j->ij', t, inv_freq)
            emb = jnp.concatenate([freqs, freqs], axis=-1)
            return (jnp.cos(emb), jnp.sin(emb))

        def _rotate_half(x):
            x1, x2 = (x[..., :x.shape[-1] // 2], x[..., x.shape[-1] // 2:])
            return jnp.concatenate([-x2, x1], axis=-1)

        def _attn(x, ln_w, ln_b, conv_w, attn_w, proj_w, n_head):
            B, T, C = x.shape
            D = C // n_head
            h = _layernorm(x, ln_w, ln_b)
            hc = jnp.transpose(h, (0, 2, 1))
            hc = jnp.pad(hc, ((0, 0), (0, 0), (2, 0)))
            hc = jax.lax.conv_general_dilated(hc, conv_w, window_strides=(1,), padding='VALID', dimension_numbers=('NCH', 'OIH', 'NCH'), feature_group_count=C)
            h = jnp.transpose(hc, (0, 2, 1))
            qkv = h @ attn_w
            q, k, v = jnp.split(qkv, 3, axis=-1)
            q = q.reshape(B, T, n_head, D)
            k = k.reshape(B, T, n_head, D)
            v = v.reshape(B, T, n_head, D)
            cos, sin = _rope_tables(T, D)
            cos = cos[None, :, None, :]
            sin = sin[None, :, None, :]
            q = q * cos + _rotate_half(q) * sin
            k = k * cos + _rotate_half(k) * sin
            scores = jnp.einsum('bqhd,bkhd->bhqk', q, k) / jnp.sqrt(jnp.float32(D))
            causal = jnp.tril(jnp.ones((T, T), dtype=bool))
            scores = jnp.where(causal, scores, jnp.float32(-1e+30))
            p = jax.nn.softmax(scores, axis=-1)
            y = jnp.einsum('bhqk,bkhd->bqhd', p, v).reshape(B, T, C)
            return y @ proj_w

        def _moe(x, ln_w, ln_b, router_w, expert_wv, expert_proj):
            h = _layernorm(x, ln_w, ln_b)
            logits = h @ router_w
            expert_idx = jnp.argmax(logits, axis=-1)
            E = router_w.shape[-1]
            out = jnp.zeros_like(x)
            for e in range(E):
                gv = h @ expert_wv[e]
                gate_raw, value = jnp.split(gv, 2, axis=-1)
                y = gate_raw * jax.nn.sigmoid(gate_raw) * value @ expert_proj[e]
                out = out + jnp.where((expert_idx == e)[..., None], y, 0.0)
            return out
        n_head = 16
        x = x + _attn(x, ln1_w, ln1_b, conv_w, attn_w, proj_w, n_head)
        x = x + _moe(x, ln2_w, ln2_b, router_w, expert_wv, expert_proj)
        return x
    x = x + _L0_attn_ref(_layernorm(x, axis=-1), L0_attn_ln_gamma, L0_attn_ln_beta, L0_attn_w_qkv, L0_attn_b_qkv, L0_attn_w_out, L0_attn_b_out)
    x = x + _L0_xattn_ref(_layernorm(x, axis=-1), ctx_1024, ctx_1024, L0_xattn_Wq, L0_xattn_bq, L0_xattn_Wk, L0_xattn_bk, L0_xattn_Wv, L0_xattn_bv, L0_xattn_Wo, L0_xattn_bo)
    x = x + _L0_ffn_ref(_layernorm(x, axis=-1), L0_ffn_ln1_w, L0_ffn_c_attn_w, L0_ffn_c_proj_w, L0_ffn_ln2_w, L0_ffn_router_w, L0_ffn_w1, L0_ffn_w2)
    x = x + _L1_attn_ref(_layernorm(x, axis=-1), L1_attn_Wq, L1_attn_Wk, L1_attn_Wv, L1_attn_Wproj, L1_attn_fire_w1, L1_attn_fire_b1, L1_attn_fire_w2, L1_attn_fire_b2, L1_attn_fire_c, L1_attn_fire_L)
    x = x + _L1_xattn_ref(ctx_1024, _layernorm(x, axis=-1), L1_xattn_Wq, L1_xattn_Wk, L1_xattn_Wv, 1, 0, 1)
    x = x + _L1_ffn_ref(_layernorm(x, axis=-1), L1_ffn_ln1_w, L1_ffn_ln1_b, L1_ffn_ln2_w, L1_ffn_ln2_b, L1_ffn_conv_w, L1_ffn_attn_w, L1_ffn_proj_w, L1_ffn_router_w, L1_ffn_expert_wv, L1_ffn_expert_proj)
    return x

_drawn_inputs = setup_inputs


def setup_inputs(seed=0):
    import zlib

    import numpy as np

    out = dict(_drawn_inputs(seed))
    spreads = {'L0_attn_ln_gamma': (1.0, 0.2),
     'L0_attn_ln_beta': (0.0, 0.1),
     'L0_attn_b_qkv': (0.0, 0.1),
     'L0_attn_b_out': (0.0, 0.1),
     'L0_xattn_bq': (0.0, 0.592),
     'L0_xattn_bk': (0.0, 0.8),
     'L0_xattn_bv': (0.0, 0.1),
     'L0_xattn_bo': (0.0, 0.1),
     'L0_ffn_ln1_w': (1.0, 0.6),
     'L0_ffn_ln2_w': (1.0, 0.6),
     'L1_attn_fire_b1': (0.0, 0.8),
     'L1_attn_fire_b2': (0.0, 0.1),
     'L1_ffn_ln1_w': (1.0, 0.6),
     'L1_ffn_ln1_b': (0.0, 0.8),
     'L1_ffn_ln2_w': (1.0, 0.6),
     'L1_ffn_ln2_b': (0.0, 0.8)}
    factors = {'L0_ffn_c_attn_w': 8.0,
     'L0_ffn_c_proj_w': 8.0,
     'L0_ffn_router_w': 7.309,
     'L0_ffn_w1': 6.349,
     'L0_ffn_w2': 6.243,
     'L1_attn_Wq': 8.0,
     'L1_attn_Wk': 8.0,
     'L1_attn_Wv': 8.0,
     'L1_attn_Wproj': 8.0,
     'L1_attn_fire_w1': 8.0,
     'L1_attn_fire_w2': 8.0,
     'L1_xattn_Wq': 8.0,
     'L1_xattn_Wk': 8.0,
     'L1_ffn_conv_w': 8.0,
     'L1_ffn_attn_w': 8.0,
     'L1_ffn_proj_w': 8.0,
     'L1_ffn_router_w': 8.0,
     'L1_ffn_expert_wv': 8.0,
     'L1_ffn_expert_proj': 8.0}
    for name, (base, spread) in spreads.items():
        noise = np.random.default_rng([zlib.crc32(name.encode()), seed]).standard_normal(out[name].shape)
        drawn = base * np.exp(spread * noise) if base else spread * noise
        out[name] = jnp.asarray(drawn.astype(out[name].dtype))
    for name, factor in factors.items():
        out[name] = (out[name] * factor).astype(out[name].dtype)
    return out
```

```python
from contextlib import ExitStack

import concourse.bass as bass
from concourse import mybir

F32 = mybir.dt.float32
BF16 = mybir.dt.bfloat16
I32 = mybir.dt.int32
ALU = mybir.AluOpType
ACT = mybir.ActivationFunctionType
AX = mybir.AxisListType

P = 128
C = 128
T = 64
B = 64
NT = B * T // P
G = 4
R = NT // G
GT = G * P
E0, F0 = 8, 256
E1, F1 = 4, 512
NF = 32
EPS = 1e-5
MAGIC = 12582912.0
QMAX = 255.0
NEG = -1e30

USES = {
    "ln_stats": (7, 0, 4),
    "ln_aggr": (7, 0, 4),
    "ln_eps": (7, 0, 4),
    "ln_rstd": (7, 0, 4),
    "ln_done": (7, 0, 4),
    "hT_ps": (5, 0, 4),
    "hT_ready": (5, 0, 4),
    "ctxT_ps": (1, 0, 1),
    "ctxT_ready": (1, 0, 1),
    "conv_mid": (0, 0, 1),
    "conv_mid2": (0, 0, 1),
    "conv_done": (0, 0, 1),
    "proj_ps": (4, 1, 2),
    "q_ready": (3, 0, 1),
    "k_ready": (3, 0, 1),
    "v1_ready": (1, 0, 0),
    "rope_cos": (1, 0, 1),
    "rope_sin": (1, 0, 1),
    "rope_done": (1, 0, 1),
    "v_ready": (3, 1, 2),
    "kblk_ready": (3, 1, 2),
    "scores_ps": (3, 1, 2),
    "biased": (0, 1, 0),
    "rowmax": (3, 1, 2),
    "shifted": (3, 1, 2),
    "probs": (3, 1, 2),
    "rowsum": (0, 1, 0),
    "rowinv": (0, 1, 0),
    "normed": (0, 1, 0),
    "rounded": (0, 1, 0),
    "pT_ps": (3, 1, 2),
    "pT_ready": (3, 1, 2),
    "o_ps": (3, 1, 2),
    "o_inv": (3, 0, 2),
    "o_ready": (3, 1, 2),
    "oT_ps": (3, 0, 1),
    "oT_ready": (3, 0, 1),
    "out_ps": (3, 0, 2),
    "x_added": (3, 0, 3),
    "pool_x": (4, 0, 1),
}
GROUP_USES = {
    "router_ps": (1, 0, 1),
    "route": (18, 0, 7),
    "route_exp": (1, 0, 0),
    "up_ps": (2 * E0, 0, 2 * E1 * F1 // P),
    "act_ready": (2 * E0, 0, E1 * F1 // P),
    "hid_ready": (0, 0, E1 * F1 // P),
    "down_ps": (E0 * G, 0, E1 * G),
    "y_added": (E0 * G, 0, E1 * G),
    "quant_a": (0, 3, 1),
    "quant_b": (0, 3, 1),
    "quant_c": (0, 3, 1),
    "x_free": (1, 0, 1),
    "x_loaded": (16, 0, 16),
    "ctx_loaded": (16, 0, 16),
    "x_stored": (16, 0, 16),
}
PH_A, PH_B, PH_C = range(3)
STAT_Y = 18


def counter(phase, r):
    def at(name, n, lane=None):
        per = [u * G for u in USES[name]] if name in USES else list(GROUP_USES[name])
        if lane is not None:
            n = n * G + lane
        return r * per[phase] + (sum(R * per[p] for p in range(phase)) + n + 1)
    return at


def total(name, phase):
    per = [u * G for u in USES[name]] if name in USES else list(GROUP_USES[name])
    return sum(R * per[p] for p in range(phase + 1))


def decoder_kernel(nc, a, out):
    ctx = ExitStack()
    with ctx:
        def sb(name, shape, dt=F32):
            return ctx.enter_context(nc.sbuf_tensor(name, shape, dt))

        def sem(name):
            return ctx.enter_context(nc.semaphore(name))

        S = {name: sem(name) for name in (*USES, *GROUP_USES)}
        w_attn0 = sem("w_attn0")
        w_moe0 = sem("w_moe0")
        w_layer1 = sem("w_layer1")
        const_ready = sem("const_ready")
        const_step = sem("const_step")
        fire_pe = sem("fire_pe")
        fire_act = sem("fire_act")
        fire_dve = sem("fire_dve")
        stat_dve = sem("stat_dve")
        stat_all = sem("stat_all")

        w = {n: sb("w_" + n, list(a[n].shape)) for n in a if n not in ("x", "ctx", "xmid")}
        moe0 = [n for n in w if n in ("f0_w1", "f0_w2")]
        layer1 = [n for n in w if n[:2] in ("a1", "x1", "f1") or n in ("cosT", "sinT")]
        attn0 = [n for n in w if n not in moe0 + layer1]

        ident = sb("ident", [P, P])
        ident_bf = sb("ident_bf", [P, P], BF16)
        causal_bf = sb("causal_bf", [P, T], BF16)
        causal = sb("causal", [P, T])
        blk16 = sb("blk16", [P, 16])
        blk8 = sb("blk8", [P, 8])
        minus_half = sb("minus_half", [P, 1])
        eps = sb("eps", [P, 1])
        unused = sb("unused", [P, 1])
        first8 = sb("first8", [P, E0])
        xin = sb("xin", [P, G, C])
        ctxin = sb("ctxin", [P, G, C])
        x = sb("xres", [P, G, C])
        h = sb("h", [P, G, C])
        h2 = sb("h2", [P, G, C])
        hT = sb("hT", [P, G, P])
        ctxT = sb("ctxT", [P, G, P])
        qk = sb("qk", [P, G, 2, P])
        big = sb("big", [P, G, 2048])
        vb16 = sb("vb16", [P, G, 2, 8, 18])
        vb8 = sb("vb8", [P, G, 2, 4, 34])
        o = sb("o", [P, G, C])
        oT = sb("oT", [P, G, P])
        st6 = sb("st6", [P, G, 6])
        mv = sb("mv", [P, G, 2])
        veps = sb("veps", [P, G])
        rstd = sb("rstd", [P, G])
        rmax = sb("rmax", [P, G, 16])
        rsum = sb("rsum", [P, G, 16])
        rinv = sb("rinv", [P, G, 16])
        lg = sb("lg", [P, G, E0])
        le = sb("le", [P, G, E0])
        l2 = sb("l2", [P, G, E0])
        sel1 = sb("sel1", [P, G, E0])
        sel2 = sb("sel2", [P, G, E0])
        key = sb("key", [P, G, E0])
        top = sb("top", [P, G, 1])
        rw = sb("rw", [P, G, E0])
        qkv = sb("qkv", [P, 3, B * T])
        qkvq = sb("qkvq", [P, 3, GT])
        bias = sb("bias", [P, 16, T])
        stats = sb("stats", [P, 8])
        gstats = sb("gstats", [P, 8])
        qstep = sb("qstep", [P, 4])
        qinv = sb("qinv", [P, 4])
        qzero = sb("qzero", [P, 4])
        qmagic = sb("qmagic", [P, 4])
        sS = sb("sS", [P, 1])
        sY = sb("sY", [P, 1])

        bank = [ctx.enter_context(nc.psum_tensor(f"bank{i}", [P, 512], F32)) for i in range(2 * G)]

        def lo(t):
            return bank[2 * t]

        def hi(t):
            return bank[2 * t + 1]

        block = ctx.enter_context(nc.Block())

        P_ = lambda t: big[:, t, 0:1024]
        PT = lambda t: big[:, t, 1024:2048]
        hid = big[:, :, :].rearrange("p g (c n) -> p (g c) n", n=GT)
        yst = qkv[:, 0, :]

        x_t = a["x"].rearrange("(r g p) c -> r p g c", g=G, p=P)
        ctx_t = a["ctx"].rearrange("(r g p) c -> r p g c", g=G, p=P)
        xmid_t = a["xmid"].rearrange("(r g p) c -> r p g c", g=G, p=P)
        out_t = out.rearrange("(r g p) c -> r p g c", g=G, p=P)

        att_a = [dict(q=w["a0_wqkv"][:, 0:128], k=w["a0_wqkv"][:, 128:256], v=w["a0_wqkv"][:, 256:384],
                      o=w["a0_wout"][:, :], kv="h", causal=False),
                 dict(q=w["x0_wq"][:, :], k=w["x0_wk"][:, :], v=w["x0_wv"][:, :],
                      o=w["x0_wo"][:, :], kv="ctx", causal=False),
                 dict(q=w["f0_wqkv"][:, 0:128], k=w["f0_wqkv"][:, 128:256], v=w["f0_wqkv"][:, 256:384],
                      o=w["f0_wo"][:, :], kv="h", causal=True)]

        def vblocks(t, heads):
            return (vb16 if heads == 16 else vb8)[:, t]

        @block.sync
        def _(sp):
            for names, done in ((attn0, w_attn0), (moe0, w_moe0), (layer1, w_layer1)):
                for n in names:
                    sp.dma_start(w[n][:], a[n]).then_inc(done, 16)
            sp.nop().then_inc(S["x_free"], 1)
            for phase, src, dst in ((PH_A, x_t, xmid_t), (PH_C, xmid_t, out_t)):
                if phase == PH_C:
                    sp.wait_ge(S["x_stored"], total("x_stored", PH_A))
                sp.dma_start(xin[:, :, :], src[0]).then_inc(S["x_loaded"], 16)
                sp.dma_start(ctxin[:, :, :], ctx_t[0]).then_inc(S["ctx_loaded"], 16)

                def store(at, r):
                    n = (E0 if phase == PH_A else E1) * G - 1
                    sp.wait_ge(S["y_added"], at("y_added", n))
                    sp.dma_start(dst[r], x[:, :, :]).then_inc(S["x_stored"], 16)
                    sp.wait_ge(S["x_stored"], at("x_stored", 15))
                    sp.nop().then_inc(S["x_free"], 1)

                with sp.Fori(0, R - 1) as r:
                    at = counter(phase, r)
                    if phase == PH_A:
                        sp.wait_ge(S["pool_x"], at("pool_x", 0, G - 1))
                    else:
                        sp.wait_ge(S["x_added"], at("x_added", 0, G - 1))
                    sp.dma_start(xin[:, :, :], src[r + 1]).then_inc(S["x_loaded"], 16)
                    sp.wait_ge(S["ctxT_ps"], at("ctxT_ps", 0, G - 1))
                    sp.dma_start(ctxin[:, :, :], ctx_t[r + 1]).then_inc(S["ctx_loaded"], 16)
                    store(at, r)
                store(counter(phase, R - 1), R - 1)

        @block.gpsimd
        def _(pool):
            step = [0]

            def link(ins):
                step[0] += 1
                ins.then_inc(const_step, 1)
                pool.wait_ge(const_step, step[0])

            link(nc.gpsimd.memset(ident[:, :], 0.0))
            link(nc.gpsimd.affine_select(out=ident[:, :], in_=ident[:, :], compare_op=ALU.not_equal, fill=1.0,
                                         base=0, pattern=[[-1, P]], channel_multiplier=1))
            link(nc.gpsimd.tensor_copy(ident_bf[:, :], ident[:, :]))
            link(nc.gpsimd.memset(causal[:, :], 0.0))
            for half in (0, 64):
                link(nc.gpsimd.affine_select(out=causal[half:half + 64, :], in_=causal[half:half + 64, :],
                                             compare_op=ALU.is_ge, fill=NEG, base=0,
                                             pattern=[[-1, T]], channel_multiplier=1))
            link(nc.gpsimd.tensor_copy(causal_bf[:, :], causal[:, :]))
            for t_, heads in ((blk16, 16), (blk8, 8)):
                D = C // heads
                link(nc.gpsimd.memset(t_[:, :], 1.0))
                link(nc.gpsimd.affine_select(out=t_[:, :], in_=t_[:, :], compare_op=ALU.is_ge, fill=0.0,
                                             base=0, pattern=[[-D, heads]], channel_multiplier=1))
                link(nc.gpsimd.affine_select(out=t_[:, :], in_=t_[:, :], compare_op=ALU.is_ge, fill=0.0,
                                             base=D - 1, pattern=[[D, heads]], channel_multiplier=-1))
            link(nc.gpsimd.memset(minus_half[:, :], -0.5))
            link(nc.gpsimd.memset(eps[:, :], EPS))
            link(nc.gpsimd.iota(first8[:, :], pattern=[[-1, E0]], base=E0, channel_multiplier=0,
                                allow_small_or_imprecise_dtypes=True))
            link(nc.gpsimd.memset(vb16[:, :, :, :, :], 0.0))
            link(nc.gpsimd.memset(vb8[:, :, :, :, :], 0.0))
            for half in (0, 1):
                for vb, D in ((vb16, 8), (vb8, 16)):
                    col = half * (D + 1) + D
                    for t in range(G):
                        link(nc.gpsimd.memset(vb[64 * half:64 * half + 64, t, :, :, col:col + 1], 1.0))
            link(nc.gpsimd.iota(qkv[0:NF, 0, :].rearrange("p (i j) -> p i j", j=T), pattern=[[1, T], [-1, T]],
                                base=0, channel_multiplier=0, allow_small_or_imprecise_dtypes=True))
            nc.gpsimd.iota(qkv[0:NF, 1, 0:T], pattern=[[1, T]], base=0, channel_multiplier=0,
                           allow_small_or_imprecise_dtypes=True).then_inc(const_ready, 1)

            def layer_norm_rstd(at, use):
                for t in range(G):
                    pool.wait_ge(S["ln_aggr"], at("ln_aggr", use, t))
                    nc.gpsimd.tensor_tensor(veps[:, t:t + 1], mv[:, t, 1:2], eps[:, :], ALU.add)\
                        .then_inc(S["ln_eps"], 1)
                    pool.wait_ge(S["ln_eps"], at("ln_eps", use, t))
                    nc.gpsimd.tensor_tensor(rstd[:, t:t + 1], veps[:, t:t + 1], minus_half[:, :], ALU.pow)\
                        .then_inc(S["ln_rstd"], 1)

            def key_blocks(at, use, k_of, blk, heads, name, name_use):
                for t in range(G):
                    pool.wait_ge(S[name], at(name, name_use, t) if name in USES else at(name, name_use))
                    dst = big[:, t, 0:heads * P].rearrange("p (b h k) -> p b h k", b=2, h=heads)
                    kk = k_of(t).rearrange("p (b k) -> p b k", b=2).unsqueeze(2).broadcast_to([P, 2, heads, T])
                    mm = blk[:, :].unsqueeze(1).unsqueeze(3).broadcast_to([P, 2, heads, T])
                    nc.gpsimd.tensor_tensor(dst, kk, mm, ALU.mult).then_inc(S["kblk_ready"], 1)

            def add_rows(at, dst, in0, in1, name, use):
                for t in range(G):
                    pool.wait_ge(S[name], at(name, use, t))
                    nc.gpsimd.tensor_tensor(dst[:, t], in0[:, t], in1(t), ALU.add).then_inc(S["pool_x"], 1)

            with pool.Fori(0, R) as r:
                at = counter(PH_A, r)
                layer_norm_rstd(at, 0)
                pool.wait_ge(S["x_free"], at("x_free", 0))
                add_rows(at, x, xin, lambda t: h[:, t], "ln_done", 0)
                layer_norm_rstd(at, 1)
                for t in range(G):
                    pool.wait_ge(S["pool_x"], at("pool_x", 0, t))
                    nc.gpsimd.tensor_tensor(x[:, t], x[:, t], w["a0_bout"][:, :], ALU.add)\
                        .then_inc(S["pool_x"], 1)
                key_blocks(at, 0, lambda t: qk[:, t, 1], blk16, 16, "k_ready", 0)
                layer_norm_rstd(at, 2)
                add_rows(at, x, x, lambda t: w["x0_bo"][:, :], "ln_done", 2)
                key_blocks(at, 1, lambda t: qk[:, t, 1], blk16, 16, "k_ready", 1)
                layer_norm_rstd(at, 3)
                layer_norm_rstd(at, 4)
                key_blocks(at, 2, lambda t: qk[:, t, 1], blk16, 16, "k_ready", 2)
                layer_norm_rstd(at, 5)
                add_rows(at, x, x, lambda t: h[:, t], "x_added", 2)
                layer_norm_rstd(at, 6)

            pool.wait_ge(stat_dve, 7)
            nc.gpsimd.partition_all_reduce(gstats[:, 0:6], stats[:, 0:6], P, bass.bass_isa.ReduceOp.max)\
                .then_inc(stat_all, 1)
            with pool.Fori(0, R) as r:
                at = counter(PH_B, r)
                key_blocks(at, 0, lambda t: qkvq[:, 1, t * P:(t + 1) * P], blk16, 16, "quant_c", 1)
            pool.wait_ge(stat_dve, STAT_Y)
            nc.gpsimd.partition_all_reduce(gstats[:, 6:8], stats[:, 6:8], P, bass.bass_isa.ReduceOp.max)\
                .then_inc(stat_all, 1)
            with pool.Fori(0, R) as r:
                at = counter(PH_C, r)
                layer_norm_rstd(at, 0)
                key_blocks(at, 0, lambda t: qk[:, t, 1], blk8, 8, "k_ready", 0)
                layer_norm_rstd(at, 1)
                layer_norm_rstd(at, 2)
                key_blocks(at, 1, lambda t: qk[:, t, 1], blk16, 16, "rope_done", 0)
                layer_norm_rstd(at, 3)
                add_rows(at, x, x, lambda t: h[:, t], "x_added", 2)

        @block.scalar
        def _(act):
            act.wait_ge(w_attn0, 16 * len(attn0))
            act.wait_ge(const_ready, 1)
            rel = qkv[0:NF, 0, :]
            nc.scalar.activation(rel, rel, ACT.Abs, scale=w["fire_c"][:, :]).then_inc(fire_act, 1)
            nc.scalar.activation(w["fire_L"][:, :], w["fire_L"][:, :], ACT.Abs).then_inc(fire_act, 1)
            act.wait_ge(fire_act, 2)
            nc.scalar.activation(rel, rel, ACT.Ln, bias=1.0).then_inc(fire_act, 1)
            act.wait_ge(fire_dve, 1)
            nc.scalar.activation(qkv[0:NF, 1, 0:T], qkv[0:NF, 1, 0:T], ACT.Abs, scale=w["fire_c"][:, :])\
                .then_inc(fire_act, 1)
            act.wait_ge(fire_act, 4)
            nc.scalar.activation(qkv[0:NF, 1, 0:T], qkv[0:NF, 1, 0:T], ACT.Ln, bias=1.0).then_inc(fire_act, 1)
            act.wait_ge(fire_dve, 4)
            nc.scalar.activation(rel, rel, ACT.Relu, bias=w["fire_b1"][:, :], scale=w["fire_w1"][:, :])\
                .then_inc(fire_act, 1)

            def transposed_rows(at, use, scale=None, shift=None, dst=hT):
                for t in range(G):
                    act.wait_ge(S["hT_ps"], at("hT_ps", use, t))
                    if scale is None:
                        ins = nc.scalar.activation(dst[:, t], hi(t)[:, 0:P], ACT.Copy)
                    else:
                        ins = nc.scalar.activation(dst[:, t], hi(t)[:, 0:P], ACT.Identity, scale=scale[:, :],
                                                   bias=0.0 if shift is None else shift[:, :])
                    ins.then_inc(S["hT_ready"], 1)

            def transposed_ctx(at, use):
                for t in range(G):
                    act.wait_ge(S["ctxT_ps"], at("ctxT_ps", use, t))
                    nc.scalar.activation(ctxT[:, t], lo(t)[:, 0:P], ACT.Copy).then_inc(S["ctxT_ready"], 1)

            def attention(at, use, heads, proj_use, qk_use=None, bq=None, bk=None, scale=1.0, oT_use=None,
                          quantised=False):
                half = heads * 32
                if qk_use is not None:
                    for t in range(G):
                        act.wait_ge(S["proj_ps"], at("proj_ps", proj_use, t))
                        for i, b_, name in ((0, bq, "q_ready"), (1, bk, "k_ready")):
                            if b_ is None:
                                ins = nc.scalar.activation(qk[:, t, i], lo(t)[:, i * P:(i + 1) * P], ACT.Copy)
                            else:
                                ins = nc.scalar.activation(qk[:, t, i], lo(t)[:, i * P:(i + 1) * P],
                                                           ACT.Identity, bias=b_)
                            ins.then_inc(S[name], 1)
                for t in range(G):
                    act.wait_ge(S["shifted"], at("shifted", use, t))
                    nc.scalar.activation(P_(t)[:, 0:2 * half], P_(t)[:, 0:2 * half], ACT.Exp, scale=scale)\
                        .then_inc(S["probs"], 1)
                if quantised:
                    for t in range(G):
                        act.wait_ge(S["normed"], at("normed", use, t))
                        nc.scalar.activation(P_(t), P_(t), ACT.Copy, bias=MAGIC).then_inc(S["rounded"], 1)
                for t in range(G):
                    act.wait_ge(S["pT_ps"], at("pT_ps", use, t))
                    off = -MAGIC if quantised else 0.0
                    nc.scalar.activation(PT(t)[:, 0:half], lo(t)[:, 0:half], ACT.Copy, bias=off)
                    nc.scalar.activation(PT(t)[:, half:2 * half], hi(t)[:, 0:half], ACT.Copy, bias=off)\
                        .then_inc(S["pT_ready"], 1)
                if oT_use is not None:
                    for t in range(G):
                        act.wait_ge(S["oT_ps"], at("oT_ps", oT_use, t))
                        nc.scalar.activation(oT[:, t], hi(t)[:, 0:P], ACT.Copy).then_inc(S["oT_ready"], 1)

            s8 = 8.0 ** -0.5
            with act.Fori(0, R) as r:
                at = counter(PH_A, r)
                transposed_rows(at, 0, w["a0_g"], w["a0_b"])
                attention(at, 0, 16, 0, 0, w["a0_bq"][:, :], w["a0_bk"][:, :], s8, 0)
                transposed_ctx(at, 0)
                transposed_rows(at, 1)
                attention(at, 1, 16, 1, 1, w["x0_bq"][:, :], w["x0_bk"][:, :], s8, 1)
                transposed_rows(at, 2, w["f0_g1"])
                attention(at, 2, 16, 2, 2, None, None, s8, 2)
                transposed_rows(at, 3, w["f0_g2"])
                act.wait_ge(S["route"], at("route", 1))
                nc.scalar.activation(le[:, :, :], lg[:, :, :], ACT.Exp).then_inc(S["route_exp"], 1)
                for c in range(2 * E0):
                    act.wait_ge(S["up_ps"], at("up_ps", c))
                    if c >= 4:
                        act.wait_ge(S["down_ps"], at("down_ps", ((c - 4) // 2) * G + G - 1))
                    nc.scalar.activation(hid[:, c % 4], bank[c % 4][:, :], ACT.Gelu).then_inc(S["act_ready"], 1)
                transposed_rows(at, 4)
                for t in range(G):
                    act.wait_ge(S["proj_ps"], at("proj_ps", 3, t))
                    nc.scalar.activation(qkv[:, 2, bass.ds(r * GT + t * P, P)], hi(t)[:, 0:P], ACT.Copy)\
                        .then_inc(S["v1_ready"], 1)
            with act.Fori(0, R) as r:
                at = counter(PH_B, r)
                attention(at, 0, 16, 0, quantised=True)
            act.wait_ge(w_layer1, 16 * len(layer1))
            with act.Fori(0, R) as r:
                at = counter(PH_C, r)
                transposed_rows(at, 0)
                transposed_ctx(at, 0)
                transposed_rows(at, 1)
                attention(at, 0, 8, 0, 0, None, None, 0.25, None)
                transposed_rows(at, 2, w["f1_g1"], w["f1_b1"], dst=oT)
                attention(at, 1, 16, 1, None, None, None, s8, 0)
                transposed_rows(at, 3, w["f1_g2"], w["f1_b2"])
                for c in range(E1 * F1 // P):
                    act.wait_ge(S["up_ps"], at("up_ps", 2 * c))
                    if c >= 2:
                        act.wait_ge(S["hid_ready"], at("hid_ready", c - 2))
                    nc.scalar.activation(hid[:, 8 + c % 2], bank[2 * (c % 2)][:, :], ACT.Silu)\
                        .then_inc(S["act_ready"], 1)

        @block.tensor
        def _(pe):
            pe.wait_ge(w_attn0, 16 * len(attn0))
            pe.wait_ge(const_ready, 1)
            pe.wait_ge(fire_act, 6)
            fh = qkv[0:NF, 0, :].rearrange("p (i j) -> p i j", j=T)
            for j in range(T):
                for half in (0, 64):
                    last = nc.tensor.matmul(bank[j // 32][half:half + 64, (j % 32) * 16:(j % 32) * 16 + 16],
                                            fh[:, :, j], w["fire_w2"][:, :], start=True, stop=True)
            last.then_inc(fire_pe, 1)
            pe.wait_ge(fire_dve, 6)

            def transpose_rows(at, use, src, name, name_use):
                for t in range(G):
                    pe.wait_ge(S[name], at(name, name_use, t) if name in USES else at(name, name_use))
                    nc.tensor.transpose(hi(t)[:, 0:P], src[:, t], ident[:, :]).then_inc(S["hT_ps"], 1)

            def transpose_ctx(at, use):
                pe.wait_ge(S["ctx_loaded"], at("ctx_loaded", 15))
                for t in range(G):
                    pe.wait_ge(S["x_added"], at("x_added", 0, t))
                    nc.tensor.transpose(lo(t)[:, 0:P], ctxin[:, t], ident[:, :]).then_inc(S["ctxT_ps"], 1)

            def project(at, t, wq, wk, wv, src, kvsrc, heads):
                D = C // heads
                nc.tensor.matmul(lo(t)[:, 0:P], wq, src, start=True, stop=True)
                nc.tensor.matmul(lo(t)[:, P:2 * P], wk, kvsrc, start=True, stop=True)
                return values(t, hi(t)[:, 2 * P:3 * P], wv, kvsrc, heads)

            def values(t, dst, wv, kvsrc, heads):
                D = C // heads
                wv2 = wv.rearrange("p (j two d) -> p two j d", two=2, d=D)
                for b in range(2):
                    for odd in range(2):
                        last = nc.tensor.matmul(dst[64 * odd:64 * odd + 64, 64 * b:64 * b + 64],
                                                kvsrc[:, 64 * b:64 * b + 64], wv2[:, odd], start=True, stop=True)
                return last

            def scores(at, use, heads, causal_, q_of, waits):
                half = heads * 32
                for t in range(G):
                    for name, n in waits:
                        pe.wait_ge(S[name], at(name, n, t))
                    pe.wait_ge(S["kblk_ready"], at("kblk_ready", use, t))
                    pe.wait_ge(S["v_ready"], at("v_ready", use, t))
                    kb = big[:, t, 0:heads * P].rearrange("p (b n) -> p b n", b=2)
                    if causal_:
                        for n in range(2):
                            nc.tensor.matmul(bank[2 * t + n][:, 0:half], ident_bf[:, :],
                                             causal_bf[:, :].unsqueeze(1).broadcast_to([P, heads // 2, T]),
                                             start=True, stop=False, skip_group_check=True)
                    for n in range(2):
                        for b in range(2):
                            last = nc.tensor.matmul(bank[2 * t + n][64 * b:64 * b + 64, 0:half],
                                                    q_of(t)[:, 64 * b:64 * b + 64],
                                                    kb[:, b, n * half:(n + 1) * half],
                                                    start=not causal_, stop=True, skip_group_check=causal_)
                    last.then_inc(S["scores_ps"], 1)

            def weigh(at, use, heads, name):
                D = C // heads
                pairs = heads // 2
                for t in range(G):
                    pe.wait_ge(S[name], at(name, use, t))
                    for j in range(pairs):
                        n, c = divmod(j, pairs // 2)
                        last = nc.tensor.transpose(bank[2 * t + n][:, c * P:(c + 1) * P],
                                                   P_(t)[:, j * P:(j + 1) * P], ident[:, :])
                    last.then_inc(S["pT_ps"], 1)
                for t in range(G):
                    pe.wait_ge(S["pT_ready"], at("pT_ready", use, t))
                    W = 2 * (D + 1)
                    vb = vblocks(t, heads)
                    for j in range(pairs):
                        for b in range(2):
                            last = nc.tensor.matmul(lo(t)[64 * b:64 * b + 64, j * W:(j + 1) * W],
                                                    PT(t)[:, j * P + 64 * b:j * P + 64 * b + 64], vb[:, b, j],
                                                    start=True, stop=True)
                    last.then_inc(S["o_ps"], 1)

            def output(at, use, o_use, wo):
                for t in range(G):
                    pe.wait_ge(S["o_ready"], at("o_ready", o_use, t))
                    nc.tensor.transpose(hi(t)[:, 0:P], o[:, t], ident[:, :]).then_inc(S["oT_ps"], 1)
                for t in range(G):
                    pe.wait_ge(S["oT_ready"], at("oT_ready", use, t))
                    nc.tensor.matmul(hi(t)[:, P:2 * P], oT[:, t], wo, start=True, stop=True)\
                        .then_inc(S["out_ps"], 1)

            def up(at, c, wcol, bk):
                nc.tensor.matmul(bank[bk][:, :], wcol, hT[:, :, :], start=True, stop=True)\
                    .then_inc(S["up_ps"], 1)

            def router(at, hT_use, wr, E):
                pe.wait_ge(S["hT_ready"], at("hT_ready", hT_use, G - 1))
                for t in range(G):
                    last = nc.tensor.matmul(bank[6][:, t * E:(t + 1) * E], hT[:, t], wr, start=True, stop=True)
                last.then_inc(S["router_ps"], 1)

            def down(at, e, chunks, w2, hid_of):
                for t in range(G):
                    dst = bank[4 + e % 2][:, t * C:(t + 1) * C]
                    for i, c in enumerate(chunks):
                        last = nc.tensor.matmul(dst, hid_of(c)[:, t * P:(t + 1) * P], w2[:, c],
                                                start=(i == 0), stop=(i == len(chunks) - 1))
                    last.then_inc(S["down_ps"], 1)

            with pe.Fori(0, R) as r:
                at = counter(PH_A, r)
                for n, aw in enumerate(att_a):
                    if n == 1:
                        transpose_ctx(at, 0)
                    transpose_rows(at, n, h2, "ln_done", (1, 2, 4)[n])
                    for t in range(G):
                        pe.wait_ge(S["hT_ready"], at("hT_ready", n, t))
                        if n == 1:
                            pe.wait_ge(S["ctxT_ready"], at("ctxT_ready", 0, t))
                        project(at, t, aw["q"], aw["k"], aw["v"], hT[:, t],
                                ctxT[:, t] if n == 1 else hT[:, t], 16).then_inc(S["proj_ps"], 1)
                    scores(at, n, 16, aw["causal"], lambda t: qk[:, t, 0], [("q_ready", n), ("k_ready", n)])
                    weigh(at, n, 16, "probs")
                    output(at, n, n, aw["o"])
                pe.wait_ge(w_moe0, 16 * len(moe0))
                transpose_rows(at, 3, h2, "ln_done", 5)
                router(at, 3, w["f0_wr"][:, :], E0)
                for e in range(E0 + 1):
                    if e < E0:
                        for c in (2 * e, 2 * e + 1):
                            if c >= 4:
                                pe.wait_ge(S["act_ready"], at("act_ready", c - 4))
                            up(at, c, w["f0_w1"][:, c * P:(c + 1) * P], c % 4)
                    if e > 0:
                        pe.wait_ge(S["act_ready"], at("act_ready", 2 * e - 1))
                        if e > 2:
                            pe.wait_ge(S["y_added"], at("y_added", (e - 3) * G + G - 1))
                        down(at, e - 1, (2 * e - 2, 2 * e - 1), w["f0_w2"], lambda c: hid[:, c % 4])
                pe.wait_ge(w_layer1, 16 * len(layer1))
                transpose_rows(at, 4, h2, "ln_done", 6)
                for t in range(G):
                    pe.wait_ge(S["hT_ready"], at("hT_ready", 4, t))
                    for i, n in enumerate(("a1_wq", "a1_wk", "a1_wqs", "a1_wks")):
                        nc.tensor.matmul(lo(t)[:, i * P:(i + 1) * P], w[n][:, :], hT[:, t], start=True, stop=True)
                    nc.tensor.matmul(hi(t)[:, 0:P], w["a1_wv"][:, :], hT[:, t], start=True, stop=True)\
                        .then_inc(S["proj_ps"], 1)
                pe.wait_ge(S["rope_sin"], at("rope_sin", 0, G - 1))
                pe.wait_ge(S["v1_ready"], at("v1_ready", 0, G - 1))

            with pe.Fori(0, R) as r:
                at = counter(PH_B, r)
                pe.wait_ge(S["quant_c"], at("quant_c", 2))
                for t in range(G):
                    values(t, lo(t)[:, 2 * P:3 * P], ident[:, :], qkvq[:, 2, t * P:(t + 1) * P], 16)\
                        .then_inc(S["proj_ps"], 1)
                scores(at, 0, 16, False, lambda t: qkvq[:, 0, t * P:(t + 1) * P], [])
                weigh(at, 0, 16, "rounded")
                pe.wait_ge(S["o_ready"], at("o_ready", 0, G - 1))

            with pe.Fori(0, R) as r:
                at = counter(PH_C, r)
                transpose_rows(at, 0, h2, "quant_c", 0)
                for t in range(G):
                    pe.wait_ge(S["hT_ready"], at("hT_ready", 0, t))
                    nc.tensor.matmul(hi(t)[:, P:2 * P], hT[:, t], w["a1_wo"][:, :], start=True, stop=True)\
                        .then_inc(S["out_ps"], 1)
                transpose_ctx(at, 0)
                transpose_rows(at, 1, h2, "ln_done", 0)
                for t in range(G):
                    pe.wait_ge(S["hT_ready"], at("hT_ready", 1, t))
                    pe.wait_ge(S["ctxT_ready"], at("ctxT_ready", 0, t))
                    project(at, t, w["x1_wq"][:, :], w["x1_wk"][:, :], w["x1_wv"][:, :], hT[:, t], ctxT[:, t], 8)\
                        .then_inc(S["proj_ps"], 1)
                scores(at, 0, 8, False, lambda t: qk[:, t, 0], [("q_ready", 0), ("k_ready", 0)])
                weigh(at, 0, 8, "probs")
                transpose_rows(at, 2, h2, "ln_done", 2)
                for t in range(G):
                    pe.wait_ge(S["conv_done"], at("conv_done", 0, t))
                    for i, n in enumerate(("f1_wq", "f1_wk", "f1_wqs", "f1_wks")):
                        nc.tensor.matmul(lo(t)[:, i * P:(i + 1) * P], w[n][:, :], hT[:, t], start=True, stop=True)
                    values(t, hi(t)[:, 0:P], w["f1_wv"][:, :], hT[:, t], 16).then_inc(S["proj_ps"], 1)
                scores(at, 1, 16, True, lambda t: qk[:, t, 0], [("rope_done", 0)])
                weigh(at, 1, 16, "probs")
                output(at, 0, 1, w["f1_wo"][:, :])
                transpose_rows(at, 3, h2, "ln_done", 3)
                router(at, 3, w["f1_wr"][:, :], E1)
                NC = F1 // P
                for e in range(E1 + 1):
                    if e < E1:
                        for c in range(NC * e, NC * e + NC):
                            if c >= 2:
                                pe.wait_ge(S["hid_ready"], at("hid_ready", c - 2))
                            i = c % NC
                            up(at, 2 * c, w["f1_wv13"][:, e, i * P:(i + 1) * P], 2 * (c % 2))
                            up(at, 2 * c + 1, w["f1_wv13"][:, e, F1 + i * P:F1 + (i + 1) * P], 2 * (c % 2) + 1)
                    if e > 0:
                        pe.wait_ge(S["hid_ready"], at("hid_ready", NC * e - 1))
                        if e > 2:
                            pe.wait_ge(S["y_added"], at("y_added", (e - 3) * G + G - 1))
                        down(at, e - 1, range(NC * e - NC, NC * e), w["f1_w2"], lambda c: hid[:, c % 8])

        @block.vector
        def _(v):
            v.wait_ge(w_attn0, 16 * len(attn0))
            v.wait_ge(const_ready, 1)
            v.wait_ge(fire_act, 2)
            posn = qkv[0:NF, 1, 0:T]
            nc.vector.tensor_scalar(posn, posn, w["fire_L"][:, :], None, ALU.max).then_inc(fire_dve, 1)
            v.wait_ge(fire_act, 5)
            nc.vector.tensor_scalar(posn, posn, 1e-6, None, ALU.add).then_inc(fire_dve, 1)
            v.wait_ge(fire_dve, 2)
            nc.vector.reciprocal(posn, posn).then_inc(fire_dve, 1)
            v.wait_ge(fire_dve, 3)
            fr = qkv[0:NF, 0, :].rearrange("p (i j) -> p i j", j=T)
            nc.vector.tensor_tensor(fr, fr, posn.unsqueeze(2).broadcast_to([NF, T, T]), ALU.mult)\
                .then_inc(fire_dve, 1)
            v.wait_ge(fire_pe, 1)
            for n in range(2):
                last = nc.vector.tensor_tensor(bias[:, :, 32 * n:32 * n + 32],
                                               bank[n][:, :].rearrange("p (j h) -> p h j", h=16),
                                               w["fire_b2"][:, :].unsqueeze(2).broadcast_to([P, 16, 32]), ALU.add)
            last.then_inc(fire_dve, 1)
            v.wait_ge(fire_dve, 5)
            nc.vector.tensor_tensor(bias[:, :, :], bias[:, :, :],
                                    causal[:, :].unsqueeze(1).broadcast_to([P, 16, T]), ALU.add)\
                .then_inc(fire_dve, 1)
            v.wait_ge(fire_dve, 6)

            def layer_norm(at, use, src, ready, dst):
                for t in range(G):
                    name, n = ready(t)
                    v.wait_ge(S[name], n)
                    nc.vector.bn_stats(st6[:, t], src[:, t]).then_inc(S["ln_stats"], 1)
                v.wait_ge(S["ln_stats"], at("ln_stats", use, G - 1))
                nc.vector.memset(unused[:, :], 0.0)
                for t in range(G):
                    nc.vector.bn_aggr(mv[:, t], st6[:, t]).then_inc(S["ln_aggr"], 1)
                for t in range(G):
                    v.wait_ge(S["ln_rstd"], at("ln_rstd", use, t))
                    nc.vector.tensor_scalar(dst[:, t], src[:, t], mv[:, t, 0:1], rstd[:, t:t + 1],
                                            ALU.subtract, ALU.mult).then_inc(S["ln_done"], 1)

            def value_blocks(at, use, proj_use, heads, src_of, bv=None):
                D = C // heads
                for t in range(G):
                    v.wait_ge(S["proj_ps"], at("proj_ps", proj_use, t))
                    for odd in range(2):
                        rows = slice(64 * odd, 64 * odd + 64)
                        dst = vblocks(t, heads)[rows, :, :, odd * (D + 1):odd * (D + 1) + D]
                        src = src_of(t)[rows, :].rearrange("p (b j d) -> p b j d", b=2, d=D)
                        if bv is None:
                            last = nc.vector.tensor_copy(dst, src)
                        else:
                            bb = bv[rows, :].rearrange("p (j two d) -> p two j d", two=2, d=D)[:, odd]
                            last = nc.vector.tensor_tensor(
                                dst, src, bb.unsqueeze(1).broadcast_to([64, 2, heads // 2, D]), ALU.add)
                    last.then_inc(S["v_ready"], 1)

            def softmax_shift(at, use, heads, biased=False):
                hh = heads // 2
                if biased:
                    for t in range(G):
                        v.wait_ge(S["scores_ps"], at("scores_ps", use, t))
                        for n in range(2):
                            last = nc.vector.scalar_tensor_tensor(
                                P_(t)[:, n * 512:(n + 1) * 512], bank[2 * t + n][:, :], sS[:, :],
                                bias[:, 8 * n:8 * n + 8, :].rearrange("p h k -> p (h k)"), ALU.mult, ALU.add)
                        last.then_inc(S["biased"], 1)
                for t in range(G):
                    if biased:
                        v.wait_ge(S["biased"], at("biased", use, t))
                        last = nc.vector.tensor_reduce(rmax[:, t], P_(t).rearrange("p (h k) -> p h k", k=T),
                                                       AX.X, ALU.max)
                    else:
                        v.wait_ge(S["scores_ps"], at("scores_ps", use, t))
                        for n in range(2):
                            last = nc.vector.tensor_reduce(
                                rmax[:, t, n * hh:(n + 1) * hh],
                                bank[2 * t + n][:, 0:hh * T].rearrange("p (h k) -> p h k", k=T), AX.X, ALU.max)
                    last.then_inc(S["rowmax"], 1)
                for t in range(G):
                    v.wait_ge(S["rowmax"], at("rowmax", use, t))
                    for n in range(2):
                        dst = P_(t)[:, n * hh * T:(n + 1) * hh * T].rearrange("p (h k) -> p h k", k=T)
                        src = dst if biased else bank[2 * t + n][:, 0:hh * T].rearrange("p (h k) -> p h k", k=T)
                        last = nc.vector.tensor_tensor(
                            dst, src, rmax[:, t, n * hh:(n + 1) * hh].unsqueeze(2).broadcast_to([P, hh, T]),
                            ALU.subtract)
                    last.then_inc(S["shifted"], 1)

            def head_outputs(at, use, inv_use, heads):
                D = C // heads

                def ov(t):
                    return lo(t)[:, 0:heads * (D + 1)].rearrange("p (h d) -> p h d", d=D + 1)

                for t in range(G):
                    v.wait_ge(S["o_ps"], at("o_ps", use, t))
                    nc.vector.reciprocal(rinv[:, t, 0:heads].unsqueeze(2), ov(t)[:, :, D:D + 1])\
                        .then_inc(S["o_inv"], 1)
                for t in range(G):
                    v.wait_ge(S["o_inv"], at("o_inv", inv_use, t))
                    nc.vector.tensor_tensor(o[:, t].rearrange("p (h d) -> p h d", d=D), ov(t)[:, :, 0:D],
                                            rinv[:, t, 0:heads].unsqueeze(2).broadcast_to([P, heads, D]), ALU.mult)\
                        .then_inc(S["o_ready"], 1)

            def add_output(at, out_use, dst, pool_use=None):
                for t in range(G):
                    v.wait_ge(S["out_ps"], at("out_ps", out_use, t))
                    if pool_use is not None:
                        v.wait_ge(S["pool_x"], at("pool_x", pool_use, t))
                    nc.vector.tensor_tensor(dst[:, t], hi(t)[:, P:2 * P], dst[:, t], ALU.add)\
                        .then_inc(S["x_added"], 1)

            def rope(at, proj_use, dst_of):
                def n64(ap):
                    return ap.rearrange("p (n k) -> p n k", k=T)

                cos = w["cosT"][:, :].unsqueeze(1).broadcast_to([P, 4, T])
                sin = w["sinT"][:, :].unsqueeze(1).broadcast_to([P, 4, T])
                for t in range(G):
                    v.wait_ge(S["proj_ps"], at("proj_ps", proj_use, t))
                    nc.vector.tensor_tensor(n64(P_(t)[:, 0:256]), n64(lo(t)[:, 0:256]), cos, ALU.mult)\
                        .then_inc(S["rope_cos"], 1)
                    nc.vector.tensor_tensor(n64(P_(t)[:, 256:512]), n64(lo(t)[:, 256:512]), sin, ALU.mult)\
                        .then_inc(S["rope_sin"], 1)
                for t in range(G):
                    v.wait_ge(S["rope_sin"], at("rope_sin", 0, t))
                    nc.vector.tensor_tensor(dst_of(t), P_(t)[:, 0:256].rearrange("p (n k) -> p n k", n=2),
                                            P_(t)[:, 256:512].rearrange("p (n k) -> p n k", n=2), ALU.add)\
                        .then_inc(S["rope_done"], 1)

            def routing(at, E, experts_per_token):
                n = [0]

                def link(ins):
                    ins.then_inc(S["route"], 1)
                    v.wait_ge(S["route"], at("route", n[0]))
                    n[0] += 1

                L, Z, K1 = lg[:, :, 0:E], l2[:, :, 0:E], key[:, :, 0:E]
                W, S1, S2 = rw[:, :, 0:E], sel1[:, :, 0:E], sel2[:, :, 0:E]
                tb = top[:, :, :].broadcast_to([P, G, E])
                f8 = first8[:, 0:E].unsqueeze(1).broadcast_to([P, G, E])
                ps = bank[6][:, 0:G * E].rearrange("p (g e) -> p g e", e=E)

                def first_max(src, sel):
                    link(nc.vector.tensor_tensor(K1, src, tb, ALU.is_ge))
                    link(nc.vector.tensor_tensor(K1, K1, f8, ALU.mult))
                    link(nc.vector.tensor_reduce(top[:, :, :], K1, AX.X, ALU.max))
                    link(nc.vector.tensor_tensor(sel, K1, tb, ALU.is_ge))

                v.wait_ge(S["router_ps"], at("router_ps", 0))
                link(nc.vector.tensor_reduce(top[:, :, :], ps, AX.X, ALU.max))
                link(nc.vector.tensor_tensor(L, ps, tb, ALU.subtract))
                link(nc.vector.memset(top[:, :, :], 0.0))
                if experts_per_token == 1:
                    first_max(L, W)
                    return
                first_max(L, S1)
                link(nc.vector.scalar_tensor_tensor(Z, S1, -3e38, L, ALU.mult, ALU.add))
                link(nc.vector.tensor_reduce(top[:, :, :], Z, AX.X, ALU.max))
                first_max(Z, S2)
                v.wait_ge(S["route_exp"], at("route_exp", 0))
                link(nc.vector.tensor_tensor(S1, S1, S2, ALU.add))
                link(nc.vector.tensor_tensor(W, S1, le[:, :, 0:E], ALU.mult))
                link(nc.vector.tensor_reduce(top[:, :, :], W, AX.X, ALU.add))
                link(nc.vector.reciprocal(top[:, :, :], top[:, :, :]))
                link(nc.vector.tensor_tensor(W, W, tb, ALU.mult))

            def add_experts(at, e, pool_use):
                v.wait_ge(S["down_ps"], at("down_ps", e * G + G - 1))
                for t in range(G):
                    if e == 0:
                        v.wait_ge(S["pool_x"], at("pool_x", pool_use, t))
                    else:
                        v.wait_ge(S["y_added"], at("y_added", (e - 1) * G + t))
                    nc.vector.scalar_tensor_tensor(x[:, t], bank[4 + e % 2][:, t * C:(t + 1) * C],
                                                   rw[:, t, e:e + 1], x[:, t], ALU.mult, ALU.add)\
                        .then_inc(S["y_added"], 1)

            def quantise(at, i, src, dst, col):
                nc.vector.tensor_scalar(dst, src, qinv[:, col:col + 1], MAGIC, ALU.mult, ALU.add)\
                    .then_inc(S["quant_a"], 1)
                v.wait_ge(S["quant_a"], at("quant_a", i))
                nc.vector.tensor_scalar(dst, dst, qmagic[:, col:col + 1], 0.0, ALU.subtract, ALU.max)\
                    .then_inc(S["quant_b"], 1)
                v.wait_ge(S["quant_b"], at("quant_b", i))
                nc.vector.tensor_scalar(dst, dst, QMAX, qzero[:, col:col + 1], ALU.min, ALU.subtract)\
                    .then_inc(S["quant_c"], 1)

            with v.Fori(0, R) as r:
                at = counter(PH_A, r)
                layer_norm(at, 0, xin, lambda t: ("x_loaded", at("x_loaded", 15)), h)
                layer_norm(at, 1, h, lambda t: ("ln_done", at("ln_done", 0, t)), h2)
                value_blocks(at, 0, 0, 16, lambda t: hi(t)[:, 2 * P:3 * P], w["a0_bv"])
                softmax_shift(at, 0, 16)
                head_outputs(at, 0, 0, 16)
                add_output(at, 0, x, 1)
                layer_norm(at, 2, x, lambda t: ("x_added", at("x_added", 0, t)), h2)
                value_blocks(at, 1, 1, 16, lambda t: hi(t)[:, 2 * P:3 * P], w["x0_bv"])
                softmax_shift(at, 1, 16)
                head_outputs(at, 1, 1, 16)
                add_output(at, 1, x, 2)
                layer_norm(at, 3, x, lambda t: ("x_added", at("x_added", 1, t)), h)
                layer_norm(at, 4, h, lambda t: ("ln_done", at("ln_done", 3, t)), h2)
                value_blocks(at, 2, 2, 16, lambda t: hi(t)[:, 2 * P:3 * P])
                softmax_shift(at, 2, 16)
                head_outputs(at, 2, 2, 16)
                add_output(at, 2, h)
                layer_norm(at, 5, h, lambda t: ("x_added", at("x_added", 2, t)), h2)
                routing(at, E0, 2)
                for e in range(E0):
                    add_experts(at, e, 3)
                layer_norm(at, 6, x, lambda t: ("y_added", at("y_added", (E0 - 1) * G + t)), h2)
                rope(at, 3, lambda t: qkv[:, 0:2, bass.ds(r * GT + t * P, P)])

            n = [0]

            def link(ins):
                n[0] += 1
                ins.then_inc(stat_dve, 1)
                v.wait_ge(stat_dve, n[0])

            def ranges(src, col, count, most, least):
                for i in range(count):
                    link(nc.vector.tensor_reduce(stats[:, most + i:most + i + 1], src(i), AX.X, ALU.max))
                    link(nc.vector.tensor_reduce(stats[:, least + i:least + i + 1], src(i), AX.X, ALU.min))
                link(nc.vector.tensor_scalar(stats[:, least:least + count], stats[:, least:least + count],
                                             -1.0, None, ALU.mult))

            def steps(col, count, most, least):
                c = slice(col, col + count)
                link(nc.vector.tensor_tensor(qstep[:, c], gstats[:, most:most + count],
                                             gstats[:, least:least + count], ALU.add))
                link(nc.vector.tensor_scalar(qstep[:, c], qstep[:, c], 1.0 / QMAX, 1e-12, ALU.mult, ALU.add))
                link(nc.vector.reciprocal(qinv[:, c], qstep[:, c]))
                link(nc.vector.tensor_tensor(qzero[:, c], gstats[:, least:least + count], qinv[:, c], ALU.mult))
                link(nc.vector.tensor_scalar(qzero[:, c], qzero[:, c], MAGIC, None, ALU.add))
                link(nc.vector.tensor_scalar(qzero[:, c], qzero[:, c], MAGIC, None, ALU.subtract))
                link(nc.vector.tensor_scalar(qmagic[:, c], qzero[:, c], -1.0, MAGIC, ALU.mult, ALU.add))

            v.wait_ge(S["rope_done"], total("rope_done", PH_A))
            v.wait_ge(S["v1_ready"], total("v1_ready", PH_A))
            ranges(lambda i: qkv[:, i, :], 0, 3, 0, 3)
            v.wait_ge(stat_all, 1)
            steps(0, 3, 0, 3)
            link(nc.vector.scalar_tensor_tensor(sS[:, :], qstep[:, 0:1], 8.0 ** -0.5, qstep[:, 1:2],
                                                ALU.mult, ALU.mult))
            assert n[0] == STAT_Y - 3
            with v.Fori(0, R) as r:
                at = counter(PH_B, r)
                for i in range(3):
                    quantise(at, i, qkv[:, i, bass.ds(r * GT, GT)], qkvq[:, i, :], i)
                value_blocks(at, 0, 0, 16, lambda t: lo(t)[:, 2 * P:3 * P])
                softmax_shift(at, 0, 16, biased=True)
                for t in range(G):
                    v.wait_ge(S["probs"], at("probs", 0, t))
                    nc.vector.tensor_reduce(rsum[:, t], P_(t).rearrange("p (h k) -> p h k", k=T), AX.X, ALU.add)\
                        .then_inc(S["rowsum"], 1)
                for t in range(G):
                    v.wait_ge(S["rowsum"], at("rowsum", 0, t))
                    nc.vector.reciprocal(rinv[:, t], rsum[:, t]).then_inc(S["rowinv"], 1)
                for t in range(G):
                    v.wait_ge(S["rowinv"], at("rowinv", 0, t))
                    pv = P_(t).rearrange("p (h k) -> p h k", k=T)
                    nc.vector.scalar_tensor_tensor(pv, pv, QMAX, rinv[:, t].unsqueeze(2).broadcast_to([P, 16, T]),
                                                   ALU.mult, ALU.mult).then_inc(S["normed"], 1)
                for t in range(G):
                    v.wait_ge(S["o_ps"], at("o_ps", 0, t))
                    nc.vector.tensor_scalar(
                        qkv[:, 0, bass.ds(r * GT + t * P, P)].rearrange("p (h d) -> p h d", d=8),
                        lo(t)[:, 0:144].rearrange("p (h d) -> p h d", d=9)[:, :, 0:8],
                        qstep[:, 2:3], 1.0 / QMAX, ALU.mult, ALU.mult).then_inc(S["o_ready"], 1)

            v.wait_ge(S["o_ready"], total("o_ready", PH_B))
            ranges(lambda i: qkv[:, 0, :], 3, 1, 6, 7)
            assert n[0] == STAT_Y
            v.wait_ge(stat_all, 2)
            steps(3, 1, 6, 7)
            v.wait_ge(w_layer1, 16 * len(layer1))
            with v.Fori(0, R) as r:
                at = counter(PH_C, r)
                quantise(at, 0, qkv[:, 0, bass.ds(r * GT, GT)], h2[:, :, :].rearrange("p g c -> p (g c)"), 3)
                v.wait_ge(S["x_loaded"], at("x_loaded", 15))
                v.wait_ge(S["x_free"], at("x_free", 0))
                for t in range(G):
                    v.wait_ge(S["out_ps"], at("out_ps", 0, t))
                    nc.vector.scalar_tensor_tensor(x[:, t], hi(t)[:, P:2 * P], qstep[:, 3:4], xin[:, t],
                                                   ALU.mult, ALU.add).then_inc(S["x_added"], 1)
                layer_norm(at, 0, x, lambda t: ("x_added", at("x_added", 0, t)), h2)
                value_blocks(at, 0, 0, 8, lambda t: hi(t)[:, 2 * P:3 * P])
                softmax_shift(at, 0, 8)
                head_outputs(at, 0, 0, 8)
                for t in range(G):
                    v.wait_ge(S["o_ready"], at("o_ready", 0, t))
                    nc.vector.tensor_tensor(x[:, t], x[:, t], o[:, t], ALU.add).then_inc(S["x_added"], 1)
                layer_norm(at, 1, x, lambda t: ("x_added", at("x_added", 1, t)), h)
                layer_norm(at, 2, h, lambda t: ("ln_done", at("ln_done", 1, t)), h2)
                for t in range(G):
                    v.wait_ge(S["hT_ready"], at("hT_ready", 2, t))
                    nc.vector.tensor_scalar(hT[:, t], oT[:, t], w["f1_conv"][:, 2:3], None, ALU.mult)\
                        .then_inc(S["conv_mid"], 1)
                for back, name, done in ((1, "conv_mid", "conv_mid2"), (2, "conv_mid2", "conv_done")):
                    for t in range(G):
                        v.wait_ge(S[name], at(name, 0, t))
                        rows = hT[:, t].rearrange("p (b k) -> p b k", b=2)[:, :, back:T]
                        before = oT[:, t].rearrange("p (b k) -> p b k", b=2)[:, :, 0:T - back]
                        nc.vector.scalar_tensor_tensor(rows, before, w["f1_conv"][:, 2 - back:3 - back], rows,
                                                       ALU.mult, ALU.add).then_inc(S[done], 1)
                rope(at, 1, lambda t: qk[:, t])
                value_blocks(at, 1, 1, 16, lambda t: hi(t)[:, 0:P])
                softmax_shift(at, 1, 16)
                head_outputs(at, 1, 1, 16)
                add_output(at, 1, h)
                layer_norm(at, 3, h, lambda t: ("x_added", at("x_added", 2, t)), h2)
                routing(at, E1, 1)
                NC = F1 // P
                for e in range(E1 + 1):
                    if e < E1:
                        if e >= 2:
                            v.wait_ge(S["down_ps"], at("down_ps", (e - 2) * G + G - 1))
                        for c in range(NC * e, NC * e + NC):
                            v.wait_ge(S["up_ps"], at("up_ps", 2 * c + 1))
                            v.wait_ge(S["act_ready"], at("act_ready", c))
                            nc.vector.tensor_tensor(hid[:, c % 8], bank[2 * (c % 2) + 1][:, :], hid[:, 8 + c % 2],
                                                    ALU.mult).then_inc(S["hid_ready"], 1)
                    if e > 0:
                        add_experts(at, e - 1, 0)


def kernel(**inputs):
    import numpy as np
    import concourse.bacc as bacc
    from concourse import mybir as mb
    from concourse.bass_utils import run_bass_kernel_spmd

    def g(name):
        return np.asarray(inputs[name])

    def col(v):
        return v.reshape(-1, 1)

    def rows(v, n=128):
        return np.tile(v.reshape(1, -1), (n, 1))

    def chunks(m):
        return m.reshape(-1, 128, 128).transpose(1, 0, 2)

    def swapped(m):
        return m.reshape(128, 16, 2, 4)[:, :, ::-1, :].reshape(128, 128)

    def spread(m):
        return np.repeat(m.reshape(128, 4, 1, 8), 4, axis=2).reshape(128, 128)

    freq = (1.0 / 10000.0 ** (np.arange(0, 8, 2, dtype=np.float32) / 8)).astype(np.float32)
    angle = (np.arange(64, dtype=np.float32)[None, :] * freq[:, None]).astype(np.float32)
    cos = np.tile(np.cos(angle), (32, 1)).astype(np.float32)
    sin = np.tile(np.concatenate([-np.sin(angle), np.sin(angle)]), (16, 1)).astype(np.float32)

    wqkv, bqkv, fqkv = g("L0_attn_w_qkv"), g("L0_attn_b_qkv"), g("L1_ffn_attn_w")
    wk1 = spread(g("L1_attn_Wk"))
    arrays = {
        "x": g("x").reshape(4096, 128), "ctx": g("ctx_1024").reshape(4096, 128),
        "fire_w1": col(g("L1_attn_fire_w1")), "fire_b1": col(g("L1_attn_fire_b1")), "fire_w2": g("L1_attn_fire_w2"),
        "fire_b2": rows(g("L1_attn_fire_b2")), "fire_c": rows(g("L1_attn_fire_c"), 32),
        "fire_L": rows(g("L1_attn_fire_L"), 32),
        "a0_g": col(g("L0_attn_ln_gamma")), "a0_b": col(g("L0_attn_ln_beta")), "a0_wqkv": wqkv,
        "a0_bq": col(bqkv[0:128]), "a0_bk": col(bqkv[128:256]), "a0_bv": rows(bqkv[256:384]),
        "a0_wout": g("L0_attn_w_out"), "a0_bout": rows(g("L0_attn_b_out")),
        "x0_wq": g("L0_xattn_Wq"), "x0_wk": g("L0_xattn_Wk"), "x0_wv": g("L0_xattn_Wv"), "x0_wo": g("L0_xattn_Wo"),
        "x0_bq": col(g("L0_xattn_bq")), "x0_bk": col(g("L0_xattn_bk")), "x0_bv": rows(g("L0_xattn_bv")),
        "x0_bo": rows(g("L0_xattn_bo")),
        "f0_g1": col(g("L0_ffn_ln1_w")), "f0_g2": col(g("L0_ffn_ln2_w")), "f0_wqkv": g("L0_ffn_c_attn_w"),
        "f0_wo": g("L0_ffn_c_proj_w"), "f0_wr": g("L0_ffn_router_w"),
        "f0_w1": g("L0_ffn_w1"), "f0_w2": chunks(g("L0_ffn_w2")),
        "cosT": cos, "sinT": sin,
        "a1_wq": g("L1_attn_Wq"), "a1_wqs": swapped(g("L1_attn_Wq")), "a1_wk": wk1, "a1_wks": swapped(wk1),
        "a1_wv": spread(g("L1_attn_Wv")), "a1_wo": g("L1_attn_Wproj"),
        "x1_wq": g("L1_xattn_Wq").T, "x1_wk": g("L1_xattn_Wk").T, "x1_wv": g("L1_xattn_Wv").T,
        "f1_g1": col(g("L1_ffn_ln1_w")), "f1_b1": col(g("L1_ffn_ln1_b")),
        "f1_g2": col(g("L1_ffn_ln2_w")), "f1_b2": col(g("L1_ffn_ln2_b")),
        "f1_conv": g("L1_ffn_conv_w").reshape(128, 3),
        "f1_wq": fqkv[:, 0:128], "f1_wqs": swapped(fqkv[:, 0:128]),
        "f1_wk": fqkv[:, 128:256], "f1_wks": swapped(fqkv[:, 128:256]), "f1_wv": fqkv[:, 256:384],
        "f1_wo": g("L1_ffn_proj_w"), "f1_wr": g("L1_ffn_router_w"),
        "f1_wv13": g("L1_ffn_expert_wv").transpose(1, 0, 2), "f1_w2": chunks(g("L1_ffn_expert_proj")),
    }
    arrays = {"in_" + n: np.ascontiguousarray(v) for n, v in arrays.items()}
    nc = bacc.Bacc("TRN2", target_bir_lowering=False, num_devices=1)
    aps = {n[3:]: nc.dram_tensor(n, v.shape, mb.dt.from_np(v.dtype), kind="ExternalInput").ap()
           for n, v in arrays.items()}
    aps["xmid"] = nc.dram_tensor("xmid", (4096, 128), mb.dt.float32, kind="Internal").ap()
    out = nc.dram_tensor("out", (4096, 128), mb.dt.float32, kind="ExternalOutput").ap()
    decoder_kernel(nc, aps, out)
    r = run_bass_kernel_spmd(nc, [arrays], core_ids=[0])
    return r.results[0]["out"].reshape(64, 64, 128)
```

```python
from contextlib import ExitStack

import concourse.bass as bass
from concourse import mybir

F32 = mybir.dt.float32
BF16 = mybir.dt.bfloat16
I32 = mybir.dt.int32
U32 = mybir.dt.uint32
ALU = mybir.AluOpType
ACT = mybir.ActivationFunctionType
AX = mybir.AxisListType

P = 128
C = 128
T = 64
B = 64
N = B * T
NT = N // P
G = 4
R = NT // G
E0, F0, K0 = 8, 256, 2
E1, F1, K1 = 4, 512, 1
CAP = N + P
NF = 32
EPS = 1e-5
MAGIC = 12582912.0
QMAX = 255.0
NEG = -1e30

NS0 = -(-(N * K0 // P + E0 - 1) // G) * G
NS1 = -(-(N * K1 // P + E1 - 1) // G) * G

PH_A, PH_M0, PH_Q, PH_B, PH_C, PH_M1, PH_O = range(7)
GROUPS = (R, NS0 // G, R, R, R, NS1 // G, R)


def seq(uses, *events):
    return [(u, e) for u in range(uses) for e in (events or (None,))]


EVENTS = {
    "ln": {PH_A: seq(6, "stats", "mean", "done"), PH_Q: seq(1, "stats", "mean", "done"),
           PH_C: seq(4, "stats", "mean", "done")},
    "veps": {PH_A: seq(6), PH_Q: seq(1), PH_C: seq(4)},
    "rstd": {PH_A: seq(6), PH_Q: seq(1), PH_C: seq(4)},
    "rows_ps": {PH_A: seq(4), PH_Q: seq(1), PH_C: seq(4)},
    "rows_T": {PH_A: seq(4), PH_Q: seq(2), PH_C: seq(4)},
    "ctx_ps": {PH_A: seq(1), PH_C: seq(1)},
    "ctx_T": {PH_A: seq(1), PH_C: seq(1)},
    "att_ps": {PH_A: seq(3, "proj", "scores", "pT", "o"), PH_Q: seq(1, "proj"),
               PH_B: seq(1, "proj", "scores", "pT", "o"), PH_C: seq(2, "proj", "scores", "pT", "o")},
    "qk": {PH_A: seq(3), PH_C: seq(1)},
    "v": {PH_A: seq(3, "v", "spread"), PH_B: seq(1, "v"), PH_C: seq(2, "v", "spread")},
    "kblk": {PH_A: seq(3), PH_B: seq(1), PH_C: seq(2)},
    "shift": {PH_A: seq(3, "max", "shifted"), PH_B: seq(1, "max"), PH_C: seq(2, "max", "shifted")},
    "probs": {PH_A: seq(3), PH_B: seq(1), PH_C: seq(2)},
    "pT": {PH_A: seq(3), PH_B: seq(1), PH_C: seq(2)},
    "o": {PH_A: seq(3, "inv", "done"), PH_B: seq(1, "done"), PH_C: seq(2, "inv", "done")},
    "out_ps": {PH_A: seq(3, "oT", "out"), PH_C: [(0, "out"), (1, "oT"), (1, "out")]},
    "oT": {PH_A: seq(3), PH_C: seq(1)},
    "x_added": {PH_A: seq(3), PH_Q: seq(2), PH_C: seq(3), PH_O: seq(1)},
    "pool_x": {PH_A: seq(4), PH_Q: seq(1), PH_B: seq(1), PH_C: seq(1), PH_O: seq(1)},
    "rope": {PH_Q: seq(1, "cos", "sin", "done"), PH_C: seq(1, "cos", "sin", "done")},
    "conv": {PH_C: seq(3)},
    "quant": {PH_B: [(i, e) for e in "abc" for i in range(3)], PH_C: seq(1, "a", "b", "c")},
    "soft": {PH_B: seq(1, "biased", "sum", "inv", "normed")},
    "rounded": {PH_B: seq(1)},
    "logit_ps": {PH_A: seq(1), PH_C: seq(1)},
    "logits": {PH_A: seq(1), PH_Q: seq(1), PH_C: seq(1)},
    "slot_ps": {PH_M0: seq(1, "rows", "up", "hid", "y"), PH_M1: seq(1, "rows", "up", "hid", "y")},
    "slot_act": {PH_M0: seq(1, "rows", "act", "hid"), PH_M1: seq(1, "rows", "act", "hid")},
    "slot_y": {PH_M0: seq(1, "y"), PH_M1: seq(1, "hid", "y")},
    "loaded": {PH_A: seq(2), PH_Q: seq(1), PH_C: seq(2), PH_O: seq(1)},
    "stored": {PH_A: seq(1), PH_Q: seq(1), PH_C: seq(1), PH_O: seq(1)},
    "gathered": {PH_Q: seq(K0), PH_O: seq(K1)},
    "slot_in": {PH_M0: seq(1), PH_M1: seq(1)},
    "slot_out": {PH_M0: seq(1), PH_M1: seq(1)},
}
DMA = ("loaded", "stored", "gathered", "slot_in", "slot_out")
ROUTE = {PH_A: 25, PH_C: 13}
CHOSEN = {PH_A: 11, PH_C: 5}
RANKED = {PH_A: 12, PH_C: 6}
TABLE = {PH_M0: 28, PH_M1: 28 + 9 + 24}
TABLE_POS = {PH_Q: 28 + 9, PH_O: 28 + 9 + 24 + 9}
STAT_Y = 18


def phase_of_moe(phase):
    return PH_M0 if phase == PH_A else PH_M1


def counter(phase, r):
    def at(name, use=0, event=None):
        by = EVENTS[name]
        before = sum(GROUPS[p] * len(by[p]) for p in by if p < phase)
        value = r * len(by[phase]) + (before + by[phase].index((use, event)) + 1)
        return value * 16 if name in DMA else value
    return at


def total(name, phase):
    n = sum(GROUPS[p] * len(e) for p, e in EVENTS[name].items() if p <= phase)
    return n * 16 if name in DMA else n


def route_at(phase, r, step):
    return r * ROUTE[phase] + ((R * ROUTE[PH_A] if phase == PH_C else 0) + step + 1)


VECTOR_HEADS = {(PH_A, 0): 4, (PH_A, 1): 4, (PH_A, 2): 4, (PH_C, 0): 1, (PH_C, 1): 2}

TIMES = {
    PH_A: [
        ("load", 0, dict(sp=0.00)), ("stats", 0, dict(dve=11.37, act=12.18, pool=14.26)),
        ("norm", 0, dict(dve=14.84)), ("stats", 1, dict(dve=14.99, act=16.30, pool=16.38)),
        ("norm", 1, dict(dve=17.11, pool=21.33)), ("rows", 0, dict(pe=22.39, act=22.87)),
        ("project", 0, dict(pe=24.20, act=26.56, dve=24.78)), ("spread", 0, dict(pool=28.07, dve=27.14)),
        ("scores", 0, dict(pe=28.96)), ("shift", 0, dict(dve=35.80)), ("softmax", 0, dict(act=36.62)),
        ("turn", 0, dict(pe=38.29, act=41.81)), ("weigh", 0, dict(pe=42.27, dve=44.04)),
        ("turn_o", 0, dict(pe=44.64, act=46.28)), ("output", 0, dict(pe=46.54, dve=47.17)),
        ("stats", 2, dict(dve=48.27, act=49.12, pool=52.23)), ("norm", 2, dict(dve=52.55, pool=53.95)),
        ("rows", 1, dict(pe=55.78, act=55.97)), ("project", 1, dict(pe=56.14, act=61.38, dve=56.98)),
        ("spread", 1, dict(pool=62.53, dve=64.01)), ("scores", 1, dict(pe=64.09)), ("shift", 1, dict(dve=67.92)),
        ("softmax", 1, dict(act=69.97)), ("turn", 1, dict(pe=70.65, act=71.35)),
        ("weigh", 1, dict(pe=72.52, dve=73.94)), ("turn_o", 1, dict(pe=75.12, act=77.23)),
        ("output", 1, dict(pe=79.05, dve=79.69)), ("stats", 3, dict(dve=79.80, act=81.49, pool=83.15)),
        ("norm", 3, dict(dve=83.81)), ("stats", 4, dict(dve=84.87, act=85.99, pool=89.98)),
        ("norm", 4, dict(dve=90.12)), ("rows", 2, dict(pe=90.59, act=90.79)),
        ("project", 2, dict(pe=91.05, act=91.12, dve=92.88)), ("spread", 2, dict(pool=96.77, dve=93.85)),
        ("scores", 2, dict(pe=96.96)), ("shift", 2, dict(dve=99.54)), ("softmax", 2, dict(act=101.25)),
        ("turn", 2, dict(pe=105.38, act=108.51)), ("weigh", 2, dict(pe=110.26, dve=111.87)),
        ("turn_o", 2, dict(pe=112.90, act=113.20)), ("output", 2, dict(pe=113.49, dve=114.34)),
        ("stats", 5, dict(dve=118.29, act=118.50, pool=120.99)), ("norm", 5, dict(dve=122.33)),
        ("router_rows", 0, dict(pe=123.11, act=124.10)), ("router", 0, dict(pe=124.89, dve=125.18)),
        ("store", 0, dict(sp=125.88)), ("collect", 0, dict(act=125.28)), ("choose", 0, dict(dve=125.68)),
        ("ranks", 0, dict(pe=129.27, act=130.66)), ("ranked", 0, dict(dve=132.38, pe=136.98)),
        ("places", 0, dict(dve=139.20)), ("scatter", 0, dict(pool=146.97)), ("scatter", 1, dict(pool=155.18)),
        ("scatter", 2, dict(pool=157.48)), ("scatter", 3, dict(pool=157.98))],
    PH_M0: [
        ("load", 0, dict(sp=0.00)), ("rows", 0, dict(pe=6.48, act=6.85)), ("up", 0, dict(pe=8.66, act=9.24)),
        ("hid", 0, dict(pe=11.22, act=13.51)), ("down", 0, dict(pe=13.62, dve=15.11)), ("store", 0, dict(sp=15.81))],
    PH_Q: [
        ("load", 0, dict(sp=0.16, pool=0.00)), ("combine", 0, dict(dve=8.02)),
        ("stats", 0, dict(dve=9.89, act=10.33, pool=10.81)), ("norm", 0, dict(dve=11.76)),
        ("rows", 0, dict(pe=14.38, act=14.61)), ("project", 0, dict(pe=14.68, act=17.20)),
        ("rope", 0, dict(dve=20.79)), ("store", 0, dict(sp=21.49))],
    PH_B: [
        ("quantise", 0, dict(dve=0.00)), ("values", 0, dict(pe=0.47, dve=1.70)), ("spread", 0, dict(pool=5.51)),
        ("scores", 0, dict(pe=11.01)), ("shift", 0, dict(dve=16.96, pool=20.13)), ("softmax", 0, dict(act=23.70)),
        ("normalise", 0, dict(dve=35.55, act=36.88)), ("turn", 0, dict(pe=42.53, act=47.40)),
        ("weigh", 0, dict(pe=48.47, dve=51.38))],
    PH_C: [
        ("load", 0, dict(sp=0.00)), ("quantise", 0, dict(dve=21.94)), ("y_rows", 0, dict(pe=24.75, act=27.69)),
        ("y_out", 0, dict(pe=28.76, dve=28.93)), ("stats", 0, dict(dve=29.98, act=32.23, pool=33.00)),
        ("norm", 0, dict(dve=37.44)), ("rows", 0, dict(pe=38.62, act=39.68)),
        ("project", 0, dict(pe=40.63, act=43.62, dve=41.55)), ("spread", 0, dict(pool=44.58, dve=46.23)),
        ("scores", 0, dict(pe=48.06)), ("shift", 0, dict(dve=48.56)), ("softmax", 0, dict(act=53.33)),
        ("turn", 0, dict(pe=53.46, act=54.02)), ("weigh", 0, dict(pe=56.31, dve=57.13)),
        ("stats", 1, dict(dve=59.04, act=60.71, pool=62.65)), ("norm", 1, dict(dve=62.86)),
        ("stats", 2, dict(dve=63.61, act=63.75, pool=67.10)), ("norm", 2, dict(dve=67.27)),
        ("conv_rows", 0, dict(pe=70.22, act=71.85)), ("convolve", 0, dict(dve=72.55)),
        ("project", 1, dict(pe=74.23, dve=77.25)), ("rope", 0, dict(dve=77.71)),
        ("spread", 1, dict(pool=83.09, dve=79.56)), ("scores", 1, dict(pe=84.44)), ("shift", 1, dict(dve=91.84)),
        ("softmax", 1, dict(act=94.80)), ("turn", 1, dict(pe=97.35, act=102.07)),
        ("weigh", 1, dict(pe=102.45, dve=104.03)), ("turn_o", 1, dict(pe=105.25, act=106.99)),
        ("output", 1, dict(pe=108.48, dve=109.10)), ("stats", 3, dict(dve=110.84, act=112.99, pool=114.12)),
        ("norm", 3, dict(dve=115.00)), ("router_rows", 0, dict(pe=115.34, act=115.99)),
        ("router", 0, dict(pe=117.42, dve=118.13)), ("store", 0, dict(sp=118.83)), ("collect", 0, dict(act=124.11)),
        ("choose", 0, dict(dve=124.21)), ("ranks", 0, dict(pe=126.67)), ("ranked", 0, dict(dve=136.42, pe=137.58)),
        ("places", 0, dict(dve=148.26)), ("scatter", 0, dict(pool=150.74)), ("scatter", 1, dict(pool=176.59)),
        ("scatter", 2, dict(pool=177.89)), ("scatter", 3, dict(pool=180.11))],
    PH_M1: [
        ("load", 0, dict(sp=0.00)), ("rows", 0, dict(pe=7.31, act=7.62)),
        ("up", 0, dict(pe=8.64, act=11.09, dve=11.58)), ("hid", 0, dict(pe=12.18, act=15.32)),
        ("down", 0, dict(pe=16.24, dve=17.93)), ("store", 0, dict(sp=18.63))],
    PH_O: [
        ("load", 0, dict(sp=0.00, pool=0.00)), ("combine", 0, dict(dve=5.86)), ("store", 0, dict(sp=6.56))],
}
ROUTING = ("collect", "choose", "ranks", "ranked", "places", "scatter")
BEAT = {PH_A: 28.534, PH_M0: 2.260, PH_Q: 3.594, PH_B: 13.051, PH_C: 25.219, PH_M1: 2.687, PH_O: 2.200}


def timetable(phase, engine):
    turn, found = G * BEAT[phase], []
    for n, (name, use, when) in enumerate(TIMES[phase]):
        for lane in (G - 1,) if name in ROUTING else range(G):
            if engine in when:
                late, time = divmod(when[engine] + lane * BEAT[phase], turn)
                found.append((time, n, name, use, lane, int(late)))
    return sorted(found)


def run(engine, which, phase, stage):
    groups, stages = GROUPS[phase], timetable(phase, which)
    most = max((late for *_, late in stages), default=0)

    def turn(n):
        for _, _, name, use, lane, late in stages:
            if 0 <= n - late < groups:
                stage(name, use, lane, n - late)

    for n in range(most):
        turn(n)
    if stages:
        with engine.Fori(most, groups) as r:
            group = [r - late if late else r for late in range(most + 1)]
            for _, _, name, use, lane, late in stages:
                stage(name, use, lane, group[late])
    for n in range(groups, groups + most):
        turn(n)


def decoder_kernel(nc, a, out):
    ctx = ExitStack()
    with ctx:
        def sb(name, shape, dt=F32):
            return ctx.enter_context(nc.sbuf_tensor(name, shape, dt))

        def sem(name):
            return ctx.enter_context(nc.semaphore(name))

        S = {name: [sem(f"{name}{t}") for t in range(G)] for name in EVENTS}
        w_attn0 = sem("w_attn0")
        w_moe0 = sem("w_moe0")
        w_layer1 = sem("w_layer1")
        const_ready = sem("const_ready")
        const_step = sem("const_step")
        fire_pe = sem("fire_pe")
        fire_act = sem("fire_act")
        fire_dve = sem("fire_dve")
        stat_dve = sem("stat_dve")
        stat_all = sem("stat_all")
        route = sem("route")
        collected = sem("collected")
        route_exp = sem("route_exp")
        rank_ps = sem("rank_ps")
        scattered = sem("scattered")
        count_ps = sem("count_ps")
        table = sem("table")
        zero_rows = sem("zero_rows")

        w = {n: sb("w_" + n, list(a[n].shape)) for n in a if n not in ("x", "ctx") and n[0] != "_"}
        moe0 = [n for n in w if n in ("f0_w1", "f0_w2")]
        layer1 = [n for n in w if n[:2] in ("a1", "x1", "f1") or n in ("cosT", "sinT")]
        attn0 = [n for n in w if n not in moe0 + layer1]

        ident = sb("ident", [P, P])
        ident_bf = sb("ident_bf", [P, P], BF16)
        ones_bf = sb("ones_bf", [P, P], BF16)
        before_bf = sb("before_bf", [P, P], BF16)
        causal_bf = sb("causal_bf", [P, T], BF16)
        causal = sb("causal", [P, T])
        blk16 = sb("blk16", [P, 16])
        blk8 = sb("blk8", [P, 8])
        minus_half = sb("minus_half", [P, 1])
        eps = sb("eps", [P, 1])
        unused = sb("unused", [P, G])
        unused_pool = sb("unused_pool", [P, 3 * G])
        first8 = sb("first8", [P, E0])
        ecap = sb("ecap", [P, E0 + 1])
        eid = sb("eid", [P, E0 + 1])
        zeros = sb("zeros", [P, C])
        xin = sb("xin", [P, G, C])
        ctxin = sb("ctxin", [P, G, C])
        x = sb("xres", [P, G, C])
        h = sb("h", [P, G, C])
        h2 = sb("h2", [P, G, C])
        hx = sb("hx", [P, G, C])
        rows_out = sb("rows_out", [P, G, C])
        hT = sb("hT", [P, G, P])
        ctxT = sb("ctxT", [P, G, P])
        qk = sb("qk", [P, G, 2, P])
        big = sb("big", [P, G, 2048])
        vb16 = sb("vb16", [P, G, 2, 8, 18])
        vb8 = sb("vb8", [P, G, 2, 4, 34])
        o = sb("o", [P, G, C])
        oT = sb("oT", [P, G, P])
        st6 = sb("st6", [P, G, 6])
        mv = sb("mv", [P, G, 2])
        veps = sb("veps", [P, G])
        rstd = sb("rstd", [P, G])
        rmax = sb("rmax", [P, G, 16])
        rsum = sb("rsum", [P, G, 16])
        rinv = sb("rinv", [P, G, 16])
        lg = sb("lg", [P, G, E0])
        lr = sb("lr", [P, G, E0])
        key = sb("key", [P, G, E0])
        sel = [sb("sel1", [P, G, E0]), sb("sel2", [P, G, E0])]
        chosen = sb("chosen", [P, G, E0], BF16)
        taken = sb("taken", [P, E0])
        taken_bf = sb("taken_bf", [P, E0], BF16)
        top = sb("top", [P, G, K0])
        first = sb("first", [P, G, 1])
        e2 = sb("e2", [P, G])
        w12 = sb("w12", [P, G, K0])
        row = sb("row", [P, G, E0])
        row12 = sb("row12", [P, G, K0])
        row_idx = sb("row_idx", [P, G, K0], U32)
        w_t = sb("w_t", [P, G, K0])
        w_all = sb("w_all", [P, NT, K0])
        row_all = sb("row_all", [P, NT, K0])
        pos_idx = sb("pos_idx", [P, NT, K0], U32)
        cnt = sb("cnt", [P, E0])
        cnt_i = sb("cnt_i", [P, E0], I32)
        nblk = sb("nblk", [P, E0])
        cblk = sb("cblk", [P, E0 + 1])
        delta = sb("delta", [P, E0 + 1])
        ddelta = sb("ddelta", [P, E0])
        slot_f = sb("slot_f", [P, NS0, 3])
        slot_i = sb("slot_i", [P, NS0, 2], I32)
        qkv = sb("qkv", [P, 3, N])
        qkvq = sb("qkvq", [P, G, 3, P])
        bias = sb("bias", [P, 16, T])
        stats = sb("stats", [P, 8])
        gstats = sb("gstats", [P, 8])
        qstep = sb("qstep", [P, 4])
        qinv = sb("qinv", [P, 4])
        qzero = sb("qzero", [P, 4])
        qmagic = sb("qmagic", [P, 4])
        sS = sb("sS", [P, 1])

        bank = [ctx.enter_context(nc.psum_tensor(f"bank{i}", [P, 512], F32)) for i in range(2 * G)]

        def lo(t):
            return bank[2 * t]

        def hi(t):
            return bank[2 * t + 1]

        block = ctx.enter_context(nc.Block())

        def P_(t):
            return big[:, t, 0:1024]

        def PT(t):
            return big[:, t, 1024:2048]

        def tile_of(dram, r, t):
            return dram.rearrange("(r g p) c -> r g p c", g=G, p=P)[r, t]

        def rows_at(dram, row_, n=P):
            return dram[bass.ds(row_, n), :]

        moe = {
            PH_M0: dict(w1=w["f0_w1"][:, :], w2=w["f0_w2"][:, :, :].rearrange("p c n -> p (c n)"), E=E0, F=F0,
                        up=F0, rows=a["_rows0"], out=a["_out0"], ns=NS0, scale=w["f0_g2"], shift=None),
            PH_M1: dict(w1=w["f1_wv13"][:, :, :].rearrange("p e n -> p (e n)"),
                        w2=w["f1_w2"][:, :, :].rearrange("p c n -> p (c n)"), E=E1, F=F1,
                        up=2 * F1, rows=a["_rows1"], out=a["_out1"], ns=NS1, scale=w["f1_g2"], shift=w["f1_b2"]),
        }
        routed = {PH_A: (moe[PH_M0], E0, K0), PH_C: (moe[PH_M1], E1, K1)}

        att = {
            (PH_A, 0): dict(q=w["a0_wqkv"][:, 0:128], k=w["a0_wqkv"][:, 128:256], v=w["a0_wqkv"][:, 256:384],
                            bq=w["a0_bq"], bk=w["a0_bk"], bv=w["a0_bv"], o=w["a0_wout"], kv=hT,
                            norm=(w["a0_g"], w["a0_b"]), heads=16, causal=False, ln=1),
            (PH_A, 1): dict(q=w["x0_wq"][:, :], k=w["x0_wk"][:, :], v=w["x0_wv"][:, :],
                            bq=w["x0_bq"], bk=w["x0_bk"], bv=w["x0_bv"], o=w["x0_wo"], kv=ctxT,
                            norm=(None, None), heads=16, causal=False, ln=2),
            (PH_A, 2): dict(q=w["f0_wqkv"][:, 0:128], k=w["f0_wqkv"][:, 128:256], v=w["f0_wqkv"][:, 256:384],
                            bq=None, bk=None, bv=None, o=w["f0_wo"], kv=hT,
                            norm=(w["f0_g1"], None), heads=16, causal=True, ln=4),
            (PH_B, 0): dict(heads=16, causal=False),
            (PH_C, 0): dict(q=w["x1_wq"][:, :], k=w["x1_wk"][:, :], v=w["x1_wv"][:, :],
                            bq=None, bk=None, bv=None, kv=ctxT, norm=(None, None), heads=8, causal=False, ln=0),
            (PH_C, 1): dict(o=w["f1_wo"], bv=None, norm=(w["f1_g1"], w["f1_b1"]), heads=16, causal=True, ln=2),
        }

        def vblocks(t, heads):
            return (vb16 if heads == 16 else vb8)[:, t]

        def spread_of(t, k, heads, h0, h1):
            n = h1 - h0
            dst = big[:, t, 0:heads * P].rearrange("p (b h k) -> p b h k", b=2, h=heads)[:, :, h0:h1]
            kk = k.rearrange("p (b k) -> p b k", b=2).unsqueeze(2).broadcast_to([P, 2, n, T])
            blk = (blk16 if heads == 16 else blk8)[:, h0:h1].unsqueeze(1).unsqueeze(3).broadcast_to([P, 2, n, T])
            return dst, kk, blk

        def phase_over(engine, phase):
            last = {PH_A: "stored", PH_M0: "slot_out", PH_Q: "stored", PH_B: "o", PH_C: "stored",
                    PH_M1: "slot_out", PH_O: "stored"}[phase]
            for t in range(G):
                engine.wait_ge(S[last][t], total(last, phase))
                if phase == PH_Q:
                    engine.wait_ge(S["rope"][t], total("rope", PH_Q))
                    engine.wait_ge(S["rows_T"][t], total("rows_T", PH_Q))

        @block.sync
        def _(sp):
            for names, done in ((attn0, w_attn0), (moe0, w_moe0), (layer1, w_layer1)):
                for n in names:
                    sp.dma_start(w[n][:], a[n]).then_inc(done, 16)

            def tiles(phase, src, dst):
                at_last = {PH_A: ("pool_x", 3, None), PH_Q: ("x_added", K0 - 1, None), PH_C: ("pool_x", 0, None),
                           PH_O: ("x_added", 0, None)}[phase]

                def stage(name, use, t, r):
                    at = counter(phase, r)
                    if name == "load":
                        if not (isinstance(r, int) and r == 0):
                            used = counter(phase, r - 1)
                            if phase in (PH_A, PH_C):
                                sp.wait_ge(S["ctx_ps"][t], used("ctx_ps"))
                            if phase == PH_A:
                                sp.wait_ge(S["pool_x"][t], used("pool_x", 0))
                            else:
                                sp.wait_ge(S["x_added"][t], used("x_added", 0))
                        sp.dma_start(xin[:, t], tile_of(src, r, t)).then_inc(S["loaded"][t], 16)
                        if phase in (PH_A, PH_C):
                            sp.dma_start(ctxin[:, t], tile_of(a["ctx"], r, t)).then_inc(S["loaded"][t], 16)
                    if name == "store":
                        sp.wait_ge(S[at_last[0]][t], at(*at_last))
                        sp.dma_start(tile_of(dst, r, t), x[:, t]).then_inc(S["stored"][t], 16)

                run(sp, "sp", phase, stage)

            def slots(phase, zeros_before):
                m = moe[phase]
                sp.wait_ge(table, TABLE[phase])
                sp.dma_start(rows_at(m["rows"], m["E"] * CAP), zeros[:, :]).then_inc(zero_rows, 16)
                for e in range(m["E"]):
                    n = sp.value_load(cnt_i[0:1, e:e + 1], min_val=0, max_val=N)
                    sp.dma_start(rows_at(m["rows"], n + e * CAP), zeros[:, :]).then_inc(zero_rows, 16)
                sp.wait_ge(zero_rows, zeros_before + 16 * (m["E"] + 1))
                sp.wait_ge(scattered, 16 * NT * (K0 if phase == PH_M0 else K0 + K1))

                def stage(name, use, t, r):
                    at = counter(phase, r)
                    if name == "load":
                        first = sp.value_load(slot_i[0:1, bass.ds(r * G + t, 1), 0], min_val=0, max_val=m["E"] * CAP)
                        if not (isinstance(r, int) and r == 0):
                            sp.wait_ge(S["slot_ps"][t], counter(phase, r - 1)("slot_ps", 0, "rows"))
                        sp.dma_start(h[:, t], rows_at(m["rows"], first)).then_inc(S["slot_in"][t], 16)
                    if name == "store":
                        sp.wait_ge(S["slot_y"][t], at("slot_y", 0, "y"))
                        sp.dma_start(rows_at(m["out"], r * (G * P) + t * P), o[:, t]).then_inc(S["slot_out"][t], 16)

                run(sp, "sp", phase, stage)

            tiles(PH_A, a["x"], a["_mid"])
            slots(PH_M0, 0)
            tiles(PH_Q, a["_mid"], a["_mid2"])
            phase_over(sp, PH_B)
            tiles(PH_C, a["_mid2"], a["_mid"])
            slots(PH_M1, 16 * (E0 + 1))
            tiles(PH_O, a["_mid"], out)
            phase_over(sp, PH_O)

        @block.gpsimd
        def _(pool):
            step = [0]

            def link(ins):
                step[0] += 1
                ins.then_inc(const_step, 1)
                pool.wait_ge(const_step, step[0])

            def keep(dst, compare, fill, base, pattern, per_partition):
                link(nc.gpsimd.affine_select(out=dst, in_=dst, compare_op=compare, fill=fill, base=base,
                                             pattern=pattern, channel_multiplier=per_partition))

            link(nc.gpsimd.memset(ident[:, :], 0.0))
            keep(ident[:, :], ALU.not_equal, 1.0, 0, [[-1, P]], 1)
            link(nc.gpsimd.tensor_copy(ident_bf[:, :], ident[:, :]))
            link(nc.gpsimd.memset(ones_bf[:, :], 1.0))
            link(nc.gpsimd.memset(before_bf[:, :], 1.0))
            keep(before_bf[:, :], ALU.is_ge, 0.0, -1, [[1, P]], -1)
            link(nc.gpsimd.memset(causal[:, :], 0.0))
            for half in (0, 64):
                keep(causal[half:half + 64, :], ALU.is_ge, NEG, 0, [[-1, T]], 1)
            link(nc.gpsimd.tensor_copy(causal_bf[:, :], causal[:, :]))
            for blk, heads in ((blk16, 16), (blk8, 8)):
                D = C // heads
                link(nc.gpsimd.memset(blk[:, :], 1.0))
                keep(blk[:, :], ALU.is_ge, 0.0, 0, [[-D, heads]], 1)
                keep(blk[:, :], ALU.is_ge, 0.0, D - 1, [[D, heads]], -1)
            link(nc.gpsimd.memset(minus_half[:, :], -0.5))
            link(nc.gpsimd.memset(eps[:, :], EPS))
            link(nc.gpsimd.memset(zeros[:, :], 0.0))
            link(nc.gpsimd.memset(taken[:, :], 0.0))
            link(nc.gpsimd.memset(taken_bf[:, :], 0.0))
            for dst, step_, base, n in ((first8, -1, E0, E0), (ecap, CAP, 0, E0 + 1), (eid, 1, 0, E0 + 1)):
                link(nc.gpsimd.iota(dst[:, :], pattern=[[step_, n]], base=base, channel_multiplier=0,
                                    allow_small_or_imprecise_dtypes=True))
            link(nc.gpsimd.iota(slot_f[:, :, 2], pattern=[[1, NS0]], base=0, channel_multiplier=0,
                                allow_small_or_imprecise_dtypes=True))
            link(nc.gpsimd.memset(vb16[:, :, :, :, :], 0.0))
            link(nc.gpsimd.memset(vb8[:, :, :, :, :], 0.0))
            for half in (0, 1):
                for vb, D in ((vb16, 8), (vb8, 16)):
                    col = half * (D + 1) + D
                    for t in range(G):
                        link(nc.gpsimd.memset(vb[64 * half:64 * half + 64, t, :, :, col:col + 1], 1.0))
            link(nc.gpsimd.iota(qkv[0:NF, 0, :].rearrange("p (i j) -> p i j", j=T), pattern=[[1, T], [-1, T]],
                                base=0, channel_multiplier=0, allow_small_or_imprecise_dtypes=True))
            nc.gpsimd.iota(qkv[0:NF, 1, 0:T], pattern=[[1, T]], base=0, channel_multiplier=0,
                           allow_small_or_imprecise_dtypes=True).then_inc(const_ready, 1)

            def norm_rstd(at, use, t):
                pool.wait_ge(S["veps"][t], at("veps", use))
                nc.gpsimd.tensor_tensor(rstd[:, t:t + 1], veps[:, t:t + 1], minus_half[:, :], ALU.pow)\
                    .then_inc(S["rstd"][t], 1)

            def spread(phase, at, use, t):
                heads = att[phase, use]["heads"]
                k = qkvq[:, t, 1] if phase == PH_B else qk[:, t, 1]
                if phase == PH_B:
                    pool.wait_ge(S["quant"][t], at("quant", 1, "c"))
                elif (phase, use) == (PH_C, 1):
                    pool.wait_ge(S["rope"][t], at("rope", 0, "done"))
                else:
                    pool.wait_ge(S["qk"][t], at("qk", use))
                mine = heads if phase == PH_B else heads - VECTOR_HEADS[phase, use]
                nc.gpsimd.tensor_tensor(*spread_of(t, k, heads, 0, mine), ALU.mult).then_inc(S["kblk"][t], 1)

            def hold(t):
                nc.gpsimd.tensor_tensor(unused_pool[:, t:t + 1], eps[:, :], eps[:, :], ALU.add)

            def add(t, dst, in0, in1):
                nc.gpsimd.tensor_tensor(dst[:, t], in0, in1, ALU.add).then_inc(S["pool_x"][t], 1)

            def attentions(phase):
                m, E, K = routed[phase]

                def stage(name, use, t, r):
                    at = counter(phase, r)
                    if name == "stats":
                        norm_rstd(at, use, t)
                        if use == (5 if phase == PH_A else 3):
                            pool.wait_ge(S["x_added"][t], at("x_added", 2))
                            add(t, x, x[:, t], h[:, t])
                    if name == "norm" and phase == PH_A and use == 1:
                        if not (isinstance(r, int) and r == 0):
                            pool.wait_ge(S["stored"][t], counter(phase, r - 1)("stored"))
                        pool.wait_ge(S["ln"][t], at("ln", 0, "done"))
                        add(t, x, xin[:, t], h[:, t])
                        pool.wait_ge(S["pool_x"][t], at("pool_x", 0))
                        add(t, x, x[:, t], w["a0_bout"][:, :])
                    if name == "norm" and phase == PH_A and use == 2:
                        pool.wait_ge(S["ln"][t], at("ln", 2, "done"))
                        add(t, x, x[:, t], w["x0_bo"][:, :])
                    if name == "spread":
                        spread(phase, at, use, t)
                    if name == "scatter":
                        pool.wait_ge(route, route_at(phase, r, ROUTE[phase] - 1))
                        pool.wait_ge(collected, r + (R + 1 if phase == PH_C else 1))
                        hold(use)
                        for s_ in range(K):
                            pool.indirect_dma_start(
                                m["rows"], bass.IndirectOffsetOnAxis(ap=row_idx[:, use, s_:s_ + 1], axis=0),
                                rows_out[:, use], None).then_inc(scattered, 16)

                run(pool, "pool", phase, stage)

            def gather(phase, m, K, idx0):
                def stage(name, use, t, r):
                    if name == "load":
                        if not (isinstance(r, int) and r == 0):
                            pool.wait_ge(S["x_added"][t], counter(phase, r - 1)("x_added", K - 1))
                            hold(G + t)
                        nc.gpsimd.tensor_copy(row_idx[:, t, 0:K], pos_idx[:, bass.ds(r * G + t, 1), 0:K]
                                              .rearrange("p a k -> p (a k)")).then_inc(S["pool_x"][t], 1)
                        pool.wait_ge(S["pool_x"][t], counter(phase, r)("pool_x"))
                        hold(2 * G + t)
                        for s_ in range(K):
                            pool.indirect_dma_start(
                                big[:, t, s_ * C:(s_ + 1) * C], None, m["out"],
                                bass.IndirectOffsetOnAxis(ap=row_idx[:, t, s_:s_ + 1], axis=0))\
                                .then_inc(S["gathered"][t], 16)
                    if name == "stats":
                        norm_rstd(counter(phase, r), 0, t)

                pool.wait_ge(table, TABLE_POS[phase])
                phase_over(pool, PH_M0 if phase == PH_Q else PH_M1)
                run(pool, "pool", phase, stage)

            attentions(PH_A)
            gather(PH_Q, moe[PH_M0], K0, 0)
            pool.wait_ge(stat_dve, 7)
            nc.gpsimd.partition_all_reduce(gstats[:, 0:6], stats[:, 0:6], P, bass.bass_isa.ReduceOp.max)\
                .then_inc(stat_all, 1)

            def stage_b(name, use, t, r):
                at = counter(PH_B, r)
                if name == "spread":
                    spread(PH_B, at, use, t)
                if name == "shift":
                    pool.wait_ge(S["shift"][t], at("shift", 0, "max"))
                    pv = P_(t).rearrange("p (h k) -> p h k", k=T)
                    nc.gpsimd.tensor_tensor(pv, pv, rmax[:, t].unsqueeze(2).broadcast_to([P, 16, T]), ALU.subtract)\
                        .then_inc(S["pool_x"][t], 1)

            run(pool, "pool", PH_B, stage_b)
            pool.wait_ge(stat_dve, STAT_Y)
            nc.gpsimd.partition_all_reduce(gstats[:, 6:8], stats[:, 6:8], P, bass.bass_isa.ReduceOp.max)\
                .then_inc(stat_all, 1)
            attentions(PH_C)
            gather(PH_O, moe[PH_M1], K1, 0)

        @block.scalar
        def _(act):
            act.wait_ge(w_attn0, 16 * len(attn0))
            act.wait_ge(const_ready, 1)
            rel = qkv[0:NF, 0, :]
            nc.scalar.activation(rel, rel, ACT.Abs, scale=w["fire_c"][:, :]).then_inc(fire_act, 1)
            nc.scalar.activation(w["fire_L"][:, :], w["fire_L"][:, :], ACT.Abs).then_inc(fire_act, 1)
            act.wait_ge(fire_act, 2)
            nc.scalar.activation(rel, rel, ACT.Ln, bias=1.0).then_inc(fire_act, 1)
            act.wait_ge(fire_dve, 1)
            nc.scalar.activation(qkv[0:NF, 1, 0:T], qkv[0:NF, 1, 0:T], ACT.Abs, scale=w["fire_c"][:, :])\
                .then_inc(fire_act, 1)
            act.wait_ge(fire_act, 4)
            nc.scalar.activation(qkv[0:NF, 1, 0:T], qkv[0:NF, 1, 0:T], ACT.Ln, bias=1.0).then_inc(fire_act, 1)
            act.wait_ge(fire_dve, 4)
            nc.scalar.activation(rel, rel, ACT.Relu, bias=w["fire_b1"][:, :], scale=w["fire_w1"][:, :])\
                .then_inc(fire_act, 1)

            def evict_rows(at, use, t, scale, shift, dst=hT):
                act.wait_ge(S["rows_ps"][t], at("rows_ps", use))
                if scale is None:
                    ins = nc.scalar.activation(dst[:, t], hi(t)[:, 0:P], ACT.Copy)
                else:
                    ins = nc.scalar.activation(dst[:, t], hi(t)[:, 0:P], ACT.Identity, scale=scale[:, :],
                                               bias=0.0 if shift is None else shift[:, :])
                ins.then_inc(S["rows_T"][t], 1)

            def norm_eps(at, use, t):
                act.wait_ge(S["ln"][t], at("ln", use, "mean"))
                nc.scalar.activation(veps[:, t:t + 1], mv[:, t, 1:2], ACT.Identity, bias=eps[:, :])\
                    .then_inc(S["veps"][t], 1)

            def collect(phase, r):
                for lane in range(G):
                    act.wait_ge(S["ln"][lane], counter(phase, r)("ln", 5 if phase == PH_A else 3, "done"))
                if phase == PH_C:
                    act.wait_ge(scattered, r * (16 * G * K1) + 16 * NT * K0)
                elif not (isinstance(r, int) and r == 0):
                    act.wait_ge(scattered, r * (16 * G * K0))
                nc.scalar.activation(rows_out[:, :, :], hx[:, :, :], ACT.Copy).then_inc(collected, 1)

            def attention_stage(phase, name, use, t, at, rows_use):
                aw = att[phase, use]
                heads = aw["heads"]
                half = heads * 32
                quantised = phase == PH_B
                roped = (phase, use) == (PH_C, 1)
                if name == "rows":
                    if aw["kv"] is ctxT:
                        act.wait_ge(S["ctx_ps"][t], at("ctx_ps"))
                        nc.scalar.activation(ctxT[:, t], lo(t)[:, 0:P], ACT.Copy).then_inc(S["ctx_T"][t], 1)
                    evict_rows(at, rows_use, t, *aw["norm"])
                if name == "project" and not roped:
                    act.wait_ge(S["att_ps"][t], at("att_ps", use, "proj"))
                    for i, b_ in ((0, aw["bq"]), (1, aw["bk"])):
                        if b_ is None:
                            ins = nc.scalar.activation(qk[:, t, i], lo(t)[:, i * P:(i + 1) * P], ACT.Copy)
                        else:
                            ins = nc.scalar.activation(qk[:, t, i], lo(t)[:, i * P:(i + 1) * P],
                                                       ACT.Identity, bias=b_[:, :])
                    ins.then_inc(S["qk"][t], 1)
                if name == "softmax":
                    if quantised:
                        act.wait_ge(S["pool_x"][t], at("pool_x"))
                    else:
                        act.wait_ge(S["shift"][t], at("shift", use, "shifted"))
                    nc.scalar.activation(P_(t)[:, 0:2 * half], P_(t)[:, 0:2 * half], ACT.Exp,
                                         scale=1.0 if quantised else float(C // heads) ** -0.5)\
                        .then_inc(S["probs"][t], 1)
                if name == "normalise":
                    act.wait_ge(S["soft"][t], at("soft", 0, "normed"))
                    nc.scalar.activation(P_(t), P_(t), ACT.Copy, bias=MAGIC).then_inc(S["rounded"][t], 1)
                if name == "turn":
                    act.wait_ge(S["att_ps"][t], at("att_ps", use, "pT"))
                    off = -MAGIC if quantised else 0.0
                    nc.scalar.activation(PT(t)[:, 0:half], lo(t)[:, 0:half], ACT.Copy, bias=off)
                    nc.scalar.activation(PT(t)[:, half:2 * half], hi(t)[:, 0:half], ACT.Copy, bias=off)\
                        .then_inc(S["pT"][t], 1)
                if name == "turn_o":
                    act.wait_ge(S["out_ps"][t], at("out_ps", use, "oT"))
                    nc.scalar.activation(oT[:, t], hi(t)[:, 0:P], ACT.Copy).then_inc(S["oT"][t], 1)

            def stage_a(name, use, t, r):
                at = counter(PH_A, r)
                if (PH_A, use) in att:
                    attention_stage(PH_A, name, use, t, at, use)
                if name == "stats":
                    norm_eps(at, use, t)
                if name == "router_rows":
                    evict_rows(at, 3, t, w["f0_g2"], None)
                if name == "collect":
                    collect(PH_A, r)
                if name == "ranks":
                    act.wait_ge(route, route_at(PH_A, r, 6))
                    nc.scalar.activation(e2[:, :], top[:, :, 1], ACT.Exp).then_inc(route_exp, 1)

            def slots(phase):
                m = moe[phase]

                def stage(name, use, t, r):
                    at = counter(phase, r)
                    if name == "rows":
                        act.wait_ge(S["slot_ps"][t], at("slot_ps", 0, "rows"))
                        nc.scalar.activation(hT[:, t], hi(t)[:, 0:P], ACT.Identity, scale=m["scale"][:, :],
                                             bias=0.0 if m["shift"] is None else m["shift"][:, :])\
                            .then_inc(S["slot_act"][t], 1)
                    if name == "up":
                        act.wait_ge(S["slot_ps"][t], at("slot_ps", 0, "up"))
                        nc.scalar.activation(big[:, t, 0:m["F"]], lo(t)[:, 0:m["F"]],
                                             ACT.Gelu if phase == PH_M0 else ACT.Silu).then_inc(S["slot_act"][t], 1)
                    if name == "hid":
                        act.wait_ge(S["slot_ps"][t], at("slot_ps", 0, "hid"))
                        nc.scalar.activation(big[:, t, 1024:1024 + m["F"]], lo(t)[:, 0:m["F"]], ACT.Copy)\
                            .then_inc(S["slot_act"][t], 1)

                run(act, "act", phase, stage)

            def stage_q(name, use, t, r):
                at = counter(PH_Q, r)
                if name == "stats":
                    norm_eps(at, 0, t)
                if name == "rows":
                    evict_rows(at, 0, t, None, None)
                if name == "project":
                    act.wait_ge(S["att_ps"][t], at("att_ps", 0, "proj"))
                    nc.scalar.activation(qkv[:, 2, bass.ds(r * (G * P) + t * P, P)], hi(t)[:, 0:P], ACT.Copy)\
                        .then_inc(S["rows_T"][t], 1)

            def stage_b(name, use, t, r):
                attention_stage(PH_B, name, use, t, counter(PH_B, r), None)

            def stage_c(name, use, t, r):
                at = counter(PH_C, r)
                if name == "y_rows":
                    evict_rows(at, 0, t, None, None)
                if (PH_C, use) in att:
                    attention_stage(PH_C, name, use, t, at, 1)
                if name == "stats":
                    norm_eps(at, use, t)
                if name == "conv_rows":
                    evict_rows(at, 2, t, *att[PH_C, 1]["norm"], dst=oT)
                if name == "router_rows":
                    evict_rows(at, 3, t, w["f1_g2"], w["f1_b2"])
                if name == "collect":
                    collect(PH_C, r)

            run(act, "act", PH_A, stage_a)
            slots(PH_M0)
            run(act, "act", PH_Q, stage_q)
            run(act, "act", PH_B, stage_b)
            act.wait_ge(w_layer1, 16 * len(layer1))
            run(act, "act", PH_C, stage_c)
            slots(PH_M1)

        @block.tensor
        def _(pe):
            pe.wait_ge(w_attn0, 16 * len(attn0))
            pe.wait_ge(const_ready, 1)
            pe.wait_ge(fire_act, 6)
            fh = qkv[0:NF, 0, :].rearrange("p (i j) -> p i j", j=T)
            for j in range(T):
                for half in (0, 64):
                    last = nc.tensor.matmul(bank[j // 32][half:half + 64, (j % 32) * 16:(j % 32) * 16 + 16],
                                            fh[:, :, j], w["fire_w2"][:, :], start=True, stop=True)
            last.then_inc(fire_pe, 1)
            pe.wait_ge(fire_dve, 6)

            def transpose_rows(at, use, t, src):
                nc.tensor.transpose(hi(t)[:, 0:P], src[:, t], ident[:, :]).then_inc(S["rows_ps"][t], 1)

            def values(t, dst, wv, kvsrc, heads):
                wv2 = wv.rearrange("p (j two d) -> p two j d", two=2, d=C // heads)
                for b in range(2):
                    for odd in range(2):
                        last = nc.tensor.matmul(dst[64 * odd:64 * odd + 64, 64 * b:64 * b + 64],
                                                kvsrc[:, 64 * b:64 * b + 64], wv2[:, odd], start=True, stop=True)
                return last

            def attention_stage(phase, name, use, t, at, rows_use):
                aw = att[phase, use]
                heads = aw["heads"]
                half = heads * 32
                pairs = heads // 2
                roped = (phase, use) == (PH_C, 1)
                if name == "rows":
                    if aw["kv"] is ctxT:
                        pe.wait_ge(S["x_added"][t], at("x_added", 0))
                        pe.wait_ge(S["loaded"][t], at("loaded", 1))
                        nc.tensor.transpose(lo(t)[:, 0:P], ctxin[:, t], ident[:, :]).then_inc(S["ctx_ps"][t], 1)
                    pe.wait_ge(S["ln"][t], at("ln", aw["ln"], "done"))
                    transpose_rows(at, rows_use, t, h2)
                if name == "project" and not roped:
                    if aw["kv"] is ctxT:
                        pe.wait_ge(S["ctx_T"][t], at("ctx_T"))
                    pe.wait_ge(S["rows_T"][t], at("rows_T", rows_use))
                    kv = aw["kv"][:, t]
                    nc.tensor.matmul(lo(t)[:, 0:P], aw["q"], hT[:, t], start=True, stop=True)
                    nc.tensor.matmul(lo(t)[:, P:2 * P], aw["k"], kv, start=True, stop=True)
                    values(t, hi(t)[:, 2 * P:3 * P], aw["v"], kv, heads).then_inc(S["att_ps"][t], 1)
                if name == "scores":
                    q = qkvq[:, t, 0] if phase == PH_B else qk[:, t, 0]
                    pe.wait_ge(S["kblk"][t], at("kblk", use))
                    pe.wait_ge(S["v"][t], at("v", use, "v" if phase == PH_B else "spread"))
                    kb = big[:, t, 0:heads * P].rearrange("p (b n) -> p b n", b=2)
                    if aw["causal"]:
                        for n in range(2):
                            nc.tensor.matmul(bank[2 * t + n][:, 0:half], ident_bf[:, :],
                                             causal_bf[:, :].unsqueeze(1).broadcast_to([P, heads // 2, T]),
                                             start=True, stop=False, skip_group_check=True)
                    for n in range(2):
                        for b in range(2):
                            last = nc.tensor.matmul(bank[2 * t + n][64 * b:64 * b + 64, 0:half],
                                                    q[:, 64 * b:64 * b + 64], kb[:, b, n * half:(n + 1) * half],
                                                    start=not aw["causal"], stop=True,
                                                    skip_group_check=aw["causal"])
                    last.then_inc(S["att_ps"][t], 1)
                if name == "turn":
                    if phase == PH_B:
                        pe.wait_ge(S["rounded"][t], at("rounded"))
                    else:
                        pe.wait_ge(S["probs"][t], at("probs", use))
                    for j in range(pairs):
                        n, c = divmod(j, pairs // 2)
                        last = nc.tensor.transpose(bank[2 * t + n][:, c * P:(c + 1) * P],
                                                   P_(t)[:, j * P:(j + 1) * P], ident[:, :])
                    last.then_inc(S["att_ps"][t], 1)
                if name == "weigh":
                    pe.wait_ge(S["pT"][t], at("pT", use))
                    W = 2 * (C // heads + 1)
                    vb = vblocks(t, heads)
                    for j in range(pairs):
                        for b in range(2):
                            last = nc.tensor.matmul(lo(t)[64 * b:64 * b + 64, j * W:(j + 1) * W],
                                                    PT(t)[:, j * P + 64 * b:j * P + 64 * b + 64], vb[:, b, j],
                                                    start=True, stop=True)
                    last.then_inc(S["att_ps"][t], 1)
                if name == "turn_o":
                    pe.wait_ge(S["o"][t], at("o", use, "done"))
                    nc.tensor.transpose(hi(t)[:, 0:P], o[:, t], ident[:, :]).then_inc(S["out_ps"][t], 1)
                if name == "output":
                    pe.wait_ge(S["oT"][t], at("oT", use if phase == PH_A else 0))
                    nc.tensor.matmul(hi(t)[:, P:2 * P], oT[:, t], aw["o"][:, :], start=True, stop=True)\
                        .then_inc(S["out_ps"][t], 1)

            def router(phase, name, at, t, wr, ln_use):
                if name == "router_rows":
                    pe.wait_ge(S["ln"][t], at("ln", ln_use, "done"))
                    transpose_rows(at, 3, t, hx)
                if name == "router":
                    pe.wait_ge(S["rows_T"][t], at("rows_T", 3))
                    nc.tensor.matmul(lo(t)[:, 0:routed[phase][1]], hT[:, t], wr, start=True, stop=True)\
                        .then_inc(S["logit_ps"][t], 1)

            def ranks(phase, r):
                E = routed[phase][1]
                pe.wait_ge(route, route_at(phase, r, CHOSEN[phase]))
                for lane in range(G):
                    dst = lo(G - 1)[:, lane * E:(lane + 1) * E]
                    nc.tensor.matmul(dst, before_bf[:, :], chosen[:, lane, 0:E], start=True, stop=False)
                    for b in range(lane):
                        nc.tensor.matmul(dst, ones_bf[:, :], chosen[:, b, 0:E], start=False, stop=False)
                    last = nc.tensor.matmul(dst, ones_bf[:, :], taken_bf[:, 0:E], start=False, stop=True)
                last.then_inc(rank_ps, 1)

            def stage_a(name, use, t, r):
                at = counter(PH_A, r)
                if (PH_A, use) in att:
                    attention_stage(PH_A, name, use, t, at, use)
                router(PH_A, name, at, t, w["f0_wr"][:, :], 5)
                if name == "ranks":
                    ranks(PH_A, r)
                if name == "ranked":
                    pe.wait_ge(route, route_at(PH_A, r, RANKED[PH_A]))

            def counts(phase):
                pe.wait_ge(route, route_at(phase, R - 1, ROUTE[phase] - 1))
                nc.tensor.matmul(lo(0)[:, 0:routed[phase][1]], ones_bf[:, :], taken_bf[:, 0:routed[phase][1]],
                                 start=True, stop=True).then_inc(count_ps, 1)

            def slots(phase):
                m = moe[phase]
                F, up = m["F"], m["up"]
                expert = {}
                pe.wait_ge(table, TABLE[phase])

                def stage(name, use, t, r):
                    at = counter(phase, r)
                    if name == "rows":
                        pe.wait_ge(S["slot_in"][t], at("slot_in"))
                        if not (isinstance(r, int) and r == 0):
                            pe.wait_ge(S["slot_y"][t], counter(phase, r - 1)("slot_y", 0, "y"))
                        nc.tensor.transpose(hi(t)[:, 0:P], h[:, t], ident[:, :]).then_inc(S["slot_ps"][t], 1)
                    if name == "up":
                        e = pe.value_load(slot_i[0:1, bass.ds(r * G + t, 1), 1], min_val=0, max_val=m["E"] - 1)
                        expert[t] = r, e
                        pe.wait_ge(S["slot_act"][t], at("slot_act", 0, "rows"))
                        for i in range(up // min(up, 512)):
                            n = min(up, 512)
                            last = nc.tensor.matmul(bank[2 * t + i][:, 0:n], hT[:, t],
                                                    m["w1"][:, bass.ds(e * up + i * n, n)], start=True, stop=True)
                        last.then_inc(S["slot_ps"][t], 1)
                    if name == "hid":
                        if phase == PH_M1:
                            pe.wait_ge(S["slot_y"][t], at("slot_y", 0, "hid"))
                        else:
                            pe.wait_ge(S["slot_act"][t], at("slot_act", 0, "act"))
                        for i in range(F // P):
                            last = nc.tensor.transpose(lo(t)[:, i * P:(i + 1) * P], big[:, t, i * P:(i + 1) * P],
                                                       ident[:, :])
                        last.then_inc(S["slot_ps"][t], 1)
                    if name == "down":
                        of, e = expert[t]
                        if of is not r:
                            e = pe.value_load(slot_i[0:1, bass.ds(r * G + t, 1), 1], min_val=0, max_val=m["E"] - 1)
                        pe.wait_ge(S["slot_act"][t], at("slot_act", 0, "hid"))
                        for i in range(F // P):
                            last = nc.tensor.matmul(hi(t)[:, 0:C], big[:, t, 1024 + i * P:1024 + (i + 1) * P],
                                                    m["w2"][:, bass.ds(e * F + i * P, P)],
                                                    start=(i == 0), stop=(i == F // P - 1))
                        last.then_inc(S["slot_ps"][t], 1)

                run(pe, "pe", phase, stage)

            def stage_q(name, use, t, r):
                at = counter(PH_Q, r)
                if name == "rows":
                    pe.wait_ge(S["ln"][t], at("ln", 0, "done"))
                    if not (isinstance(r, int) and r == 0):
                        pe.wait_ge(S["rows_T"][t], counter(PH_Q, r - 1)("rows_T", 1))
                    transpose_rows(at, 0, t, h2)
                if name == "project":
                    if not (isinstance(r, int) and r == 0):
                        pe.wait_ge(S["rope"][t], counter(PH_Q, r - 1)("rope", 0, "done"))
                    pe.wait_ge(S["rows_T"][t], at("rows_T", 0))
                    for i, n in enumerate(("a1_wq", "a1_wk", "a1_wqs", "a1_wks")):
                        nc.tensor.matmul(lo(t)[:, i * P:(i + 1) * P], w[n][:, :], hT[:, t], start=True, stop=True)
                    nc.tensor.matmul(hi(t)[:, 0:P], w["a1_wv"][:, :], hT[:, t], start=True, stop=True)\
                        .then_inc(S["att_ps"][t], 1)

            def stage_b(name, use, t, r):
                at = counter(PH_B, r)
                if name == "values":
                    pe.wait_ge(S["quant"][t], at("quant", 2, "c"))
                    values(t, hi(t)[:, 2 * P:3 * P], ident[:, :], qkvq[:, t, 2], 16).then_inc(S["att_ps"][t], 1)
                else:
                    attention_stage(PH_B, name, use, t, at, None)

            def stage_c(name, use, t, r):
                at = counter(PH_C, r)
                if name == "y_rows":
                    pe.wait_ge(S["quant"][t], at("quant", 0, "c"))
                    transpose_rows(at, 0, t, h2)
                if name == "y_out":
                    pe.wait_ge(S["rows_T"][t], at("rows_T", 0))
                    nc.tensor.matmul(hi(t)[:, P:2 * P], hT[:, t], w["a1_wo"][:, :], start=True, stop=True)\
                        .then_inc(S["out_ps"][t], 1)
                if (PH_C, use) in att:
                    attention_stage(PH_C, name, use, t, at, 1)
                if name == "conv_rows":
                    pe.wait_ge(S["ln"][t], at("ln", 2, "done"))
                    transpose_rows(at, 2, t, h2)
                if name == "project" and use == 1:
                    pe.wait_ge(S["conv"][t], at("conv", 2))
                    for i, n in enumerate(("f1_wq", "f1_wk", "f1_wqs", "f1_wks")):
                        nc.tensor.matmul(lo(t)[:, i * P:(i + 1) * P], w[n][:, :], hT[:, t], start=True, stop=True)
                    values(t, hi(t)[:, 2 * P:3 * P], w["f1_wv"][:, :], hT[:, t], 16).then_inc(S["att_ps"][t], 1)
                router(PH_C, name, at, t, w["f1_wr"][:, :], 3)
                if name == "ranks":
                    ranks(PH_C, r)
                if name == "ranked":
                    pe.wait_ge(route, route_at(PH_C, r, RANKED[PH_C]))

            run(pe, "pe", PH_A, stage_a)
            counts(PH_A)
            pe.wait_ge(w_moe0, 16 * len(moe0))
            slots(PH_M0)
            pe.wait_ge(w_layer1, 16 * len(layer1))
            phase_over(pe, PH_M0)
            run(pe, "pe", PH_Q, stage_q)
            phase_over(pe, PH_Q)
            run(pe, "pe", PH_B, stage_b)
            phase_over(pe, PH_B)
            run(pe, "pe", PH_C, stage_c)
            counts(PH_C)
            slots(PH_M1)

        @block.vector
        def _(v):
            v.wait_ge(w_attn0, 16 * len(attn0))
            v.wait_ge(const_ready, 1)
            v.wait_ge(fire_act, 2)
            posn = qkv[0:NF, 1, 0:T]
            nc.vector.tensor_scalar(posn, posn, w["fire_L"][:, :], None, ALU.max).then_inc(fire_dve, 1)
            v.wait_ge(fire_act, 5)
            nc.vector.tensor_scalar(posn, posn, 1e-6, None, ALU.add).then_inc(fire_dve, 1)
            v.wait_ge(fire_dve, 2)
            nc.vector.reciprocal(posn, posn).then_inc(fire_dve, 1)
            v.wait_ge(fire_dve, 3)
            fr = qkv[0:NF, 0, :].rearrange("p (i j) -> p i j", j=T)
            nc.vector.tensor_tensor(fr, fr, posn.unsqueeze(2).broadcast_to([NF, T, T]), ALU.mult)\
                .then_inc(fire_dve, 1)
            v.wait_ge(fire_pe, 1)
            for n in range(2):
                last = nc.vector.tensor_tensor(bias[:, :, 32 * n:32 * n + 32],
                                               bank[n][:, :].rearrange("p (j h) -> p h j", h=16),
                                               w["fire_b2"][:, :].unsqueeze(2).broadcast_to([P, 16, 32]), ALU.add)
            last.then_inc(fire_dve, 1)
            v.wait_ge(fire_dve, 5)
            nc.vector.tensor_tensor(bias[:, :, :], bias[:, :, :],
                                    causal[:, :].unsqueeze(1).broadcast_to([P, 16, T]), ALU.add)\
                .then_inc(fire_dve, 1)
            v.wait_ge(fire_dve, 6)

            layer_norms = {
                (PH_A, 0): (xin, h, ("loaded", 1, None)), (PH_A, 1): (h, h2, ("ln", 0, "done")),
                (PH_A, 2): (x, h2, ("x_added", 0, None)), (PH_A, 3): (x, h, ("x_added", 1, None)),
                (PH_A, 4): (h, h2, ("ln", 3, "done")), (PH_A, 5): (h, hx, ("x_added", 2, None)),
                (PH_Q, 0): (x, h2, ("x_added", K0 - 1, None)),
                (PH_C, 0): (x, h2, ("x_added", 0, None)), (PH_C, 1): (x, h, ("x_added", 1, None)),
                (PH_C, 2): (h, h2, ("ln", 1, "done")), (PH_C, 3): (h, hx, ("x_added", 2, None)),
            }

            def layer_norm(phase, name, use, t, r):
                at = counter(phase, r)
                src, dst, rows_there = layer_norms[phase, use]
                if name == "stats":
                    v.wait_ge(S[rows_there[0]][t], at(*rows_there))
                    nc.vector.bn_stats(st6[:, t], src[:, t]).then_inc(S["ln"][t], 1)
                    v.wait_ge(S["ln"][t], at("ln", use, "stats"))
                    nc.vector.memset(unused[:, t:t + 1], 0.0)
                    nc.vector.bn_aggr(mv[:, t], st6[:, t]).then_inc(S["ln"][t], 1)
                else:
                    if dst is hx and not (isinstance(r, int) and r == 0):
                        v.wait_ge(collected, r + R if phase == PH_C else r)
                    v.wait_ge(S["rstd"][t], at("rstd", use))
                    nc.vector.tensor_scalar(dst[:, t], src[:, t], mv[:, t, 0:1], rstd[:, t:t + 1],
                                            ALU.subtract, ALU.mult).then_inc(S["ln"][t], 1)

            def attention_stage(phase, name, use, t, at):
                aw = att[phase, use]
                heads = aw["heads"]
                D = C // heads
                hh = heads // 2
                if name in ("project", "values"):
                    v.wait_ge(S["att_ps"][t], at("att_ps", use, "proj"))
                    bv = aw.get("bv")
                    for odd in range(2):
                        rows = slice(64 * odd, 64 * odd + 64)
                        dst = vblocks(t, heads)[rows, :, :, odd * (D + 1):odd * (D + 1) + D]
                        src = hi(t)[rows, 2 * P:3 * P].rearrange("p (b j d) -> p b j d", b=2, d=D)
                        if bv is None:
                            last = nc.vector.tensor_copy(dst, src)
                        else:
                            bb = bv[rows, :].rearrange("p (j two d) -> p two j d", two=2, d=D)[:, odd]
                            last = nc.vector.tensor_tensor(
                                dst, src, bb.unsqueeze(1).broadcast_to([64, 2, heads // 2, D]), ALU.add)
                    last.then_inc(S["v"][t], 1)
                if name == "spread" and phase != PH_B:
                    if (phase, use) == (PH_C, 1):
                        v.wait_ge(S["rope"][t], at("rope", 0, "done"))
                    else:
                        v.wait_ge(S["qk"][t], at("qk", use))
                    nc.vector.tensor_tensor(*spread_of(t, qk[:, t, 1], heads, heads - VECTOR_HEADS[phase, use], heads),
                                            ALU.mult).then_inc(S["v"][t], 1)
                if name == "shift":
                    v.wait_ge(S["att_ps"][t], at("att_ps", use, "scores"))
                    if phase == PH_B:
                        for n in range(2):
                            last = nc.vector.scalar_tensor_tensor(
                                P_(t)[:, n * 512:(n + 1) * 512], bank[2 * t + n][:, :], sS[:, :],
                                bias[:, 8 * n:8 * n + 8, :].rearrange("p h k -> p (h k)"), ALU.mult, ALU.add)
                        last.then_inc(S["soft"][t], 1)
                        v.wait_ge(S["soft"][t], at("soft", 0, "biased"))
                        last = nc.vector.tensor_reduce(rmax[:, t], P_(t).rearrange("p (h k) -> p h k", k=T),
                                                       AX.X, ALU.max)
                    else:
                        for n in range(2):
                            last = nc.vector.tensor_reduce(
                                rmax[:, t, n * hh:(n + 1) * hh],
                                bank[2 * t + n][:, 0:hh * T].rearrange("p (h k) -> p h k", k=T), AX.X, ALU.max)
                    last.then_inc(S["shift"][t], 1)
                    if phase != PH_B:
                        v.wait_ge(S["shift"][t], at("shift", use, "max"))
                        for n in range(2):
                            last = nc.vector.tensor_tensor(
                                P_(t)[:, n * hh * T:(n + 1) * hh * T].rearrange("p (h k) -> p h k", k=T),
                                bank[2 * t + n][:, 0:hh * T].rearrange("p (h k) -> p h k", k=T),
                                rmax[:, t, n * hh:(n + 1) * hh].unsqueeze(2).broadcast_to([P, hh, T]), ALU.subtract)
                        last.then_inc(S["shift"][t], 1)
                if name == "weigh" and phase != PH_B:
                    v.wait_ge(S["att_ps"][t], at("att_ps", use, "o"))
                    ov = lo(t)[:, 0:heads * (D + 1)].rearrange("p (h d) -> p h d", d=D + 1)
                    nc.vector.reciprocal(rinv[:, t, 0:heads].unsqueeze(2), ov[:, :, D:D + 1]).then_inc(S["o"][t], 1)
                    v.wait_ge(S["o"][t], at("o", use, "inv"))
                    nc.vector.tensor_tensor(o[:, t].rearrange("p (h d) -> p h d", d=D), ov[:, :, 0:D],
                                            rinv[:, t, 0:heads].unsqueeze(2).broadcast_to([P, heads, D]), ALU.mult)\
                        .then_inc(S["o"][t], 1)

            def add_output(at, use, t, dst):
                v.wait_ge(S["out_ps"][t], at("out_ps", use, "out"))
                nc.vector.tensor_tensor(dst[:, t], hi(t)[:, P:2 * P], dst[:, t], ALU.add)\
                    .then_inc(S["x_added"][t], 1)

            def rope(at, t, dst):
                def n64(ap):
                    return ap.rearrange("p (n k) -> p n k", k=T)

                cos = w["cosT"][:, :].unsqueeze(1).broadcast_to([P, 4, T])
                sin = w["sinT"][:, :].unsqueeze(1).broadcast_to([P, 4, T])
                nc.vector.tensor_tensor(n64(P_(t)[:, 512:768]), n64(lo(t)[:, 0:256]), cos, ALU.mult)\
                    .then_inc(S["rope"][t], 1)
                nc.vector.tensor_tensor(n64(P_(t)[:, 768:1024]), n64(lo(t)[:, 256:512]), sin, ALU.mult)\
                    .then_inc(S["rope"][t], 1)
                v.wait_ge(S["rope"][t], at("rope", 0, "sin"))
                nc.vector.tensor_tensor(dst, P_(t)[:, 512:768].rearrange("p (n k) -> p n k", n=2),
                                        P_(t)[:, 768:1024].rearrange("p (n k) -> p n k", n=2), ALU.add)\
                    .then_inc(S["rope"][t], 1)

            def keep_logits(phase, at, t):
                E = routed[phase][1]
                v.wait_ge(S["logit_ps"][t], at("logit_ps"))
                nc.vector.tensor_copy(lg[:, t, 0:E], lo(t)[:, 0:E]).then_inc(S["logits"][t], 1)

            def routing(phase, r, name):
                _, E, K = routed[phase]
                n = [{"choose": 0, "ranked": RANKED[phase], "places": RANKED[phase] + 1}[name]]

                def link(ins):
                    ins.then_inc(route, 1)
                    v.wait_ge(route, route_at(phase, r, n[0]))
                    n[0] += 1

                L, K_ = lr[:, :, 0:E], key[:, :, 0:E]
                sl = [s_[:, :, 0:E] for s_ in sel]
                ch = chosen[:, :, 0:E]
                if name == "choose":
                    f8 = first8[:, 0:E].unsqueeze(1).broadcast_to([P, G, E])
                    for lane in range(G):
                        v.wait_ge(S["logits"][lane], counter(phase, r)("logits"))
                    src = lg[:, :, 0:E]
                    for s_ in range(K):
                        most = top[:, :, s_:s_ + 1]
                        link(nc.vector.tensor_reduce(most, src, AX.X, ALU.max))
                        link(nc.vector.tensor_tensor(L, src, most.broadcast_to([P, G, E]), ALU.subtract))
                        link(nc.vector.scalar_tensor_tensor(K_, L, 0.0, f8, ALU.is_ge, ALU.mult))
                        link(nc.vector.tensor_reduce(first[:, :, :], K_, AX.X, ALU.max))
                        link(nc.vector.tensor_tensor(sl[s_], K_, first[:, :, :].broadcast_to([P, G, E]), ALU.is_ge))
                        if s_ + 1 < K:
                            link(nc.vector.scalar_tensor_tensor(L, sl[s_], -3e38, L, ALU.mult, ALU.add))
                            src = L
                    if K == 2:
                        link(nc.vector.tensor_tensor(ch, sl[0], sl[1], ALU.add))
                    else:
                        link(nc.vector.tensor_copy(ch, sl[0]))
                    assert n[0] == CHOSEN[phase] + 1 == RANKED[phase]
                    return
                if name == "ranked":
                    v.wait_ge(rank_ps, r + (1 if phase == PH_A else R + 1))
                    link(nc.vector.tensor_tensor(row[:, :, 0:E],
                                                 lo(G - 1)[:, 0:G * E].rearrange("p (g e) -> p g e", e=E),
                                                 ecap[:, 0:E].unsqueeze(1).broadcast_to([P, G, E]), ALU.add))
                    return
                v.wait_ge(collected, r + (R + 1 if phase == PH_C else 1))
                if K == 2:
                    v.wait_ge(route_exp, r + 1)
                    link(nc.vector.tensor_scalar(e2[:, :], e2[:, :], 1.0, None, ALU.add))
                    link(nc.vector.reciprocal(w12[:, :, 0], e2[:, :]))
                    link(nc.vector.tensor_scalar(w12[:, :, 1], w12[:, :, 0], -1.0, 1.0, ALU.mult, ALU.add))
                    link(nc.vector.tensor_copy(w_all[:, bass.ds(r * G, G), :], w12[:, :, :]))
                for s_ in range(K):
                    link(nc.vector.tensor_tensor(K_, sl[s_], row[:, :, 0:E], ALU.mult))
                    link(nc.vector.tensor_reduce(row12[:, :, s_:s_ + 1], K_, AX.X, ALU.add))
                link(nc.vector.tensor_copy(row_all[:, bass.ds(r * G, G), 0:K], row12[:, :, 0:K]))
                link(nc.vector.tensor_reduce(key[:, 0, 0:E].unsqueeze(2), ch.rearrange("p g e -> p e g"), AX.X, ALU.add))
                link(nc.vector.tensor_tensor(taken[:, 0:E], taken[:, 0:E], key[:, 0, 0:E], ALU.add))
                nc.vector.tensor_copy(taken_bf[:, 0:E], taken[:, 0:E])
                link(nc.vector.tensor_copy(row_idx[:, :, 0:K], row12[:, :, 0:K]))
                assert n[0] == ROUTE[phase], (phase, n[0])

            def slot_table(phase, first):
                m, E, K = routed[phase]
                ns = m["ns"]
                n = [first]

                def link(ins):
                    n[0] += 1
                    ins.then_inc(table, 1)
                    v.wait_ge(table, n[0])

                v.wait_ge(count_ps, 1 if phase == PH_A else 2)
                link(nc.vector.tensor_copy(cnt[:, 0:E], lo(0)[:, 0:E]))
                link(nc.vector.tensor_copy(cnt_i[:, 0:E], cnt[:, 0:E]))
                nb = nblk[:, 0:E]
                link(nc.vector.tensor_scalar(nb, cnt[:, 0:E], 1.0 / P, (P - 1 - (P - 1) / 2) / P, ALU.mult, ALU.add))
                link(nc.vector.tensor_scalar(nb, nb, MAGIC, None, ALU.add))
                link(nc.vector.tensor_scalar(nb, nb, MAGIC, None, ALU.subtract))
                link(nc.vector.memset(cblk[:, 0:1], 0.0))
                for e in range(E):
                    link(nc.vector.tensor_tensor(cblk[:, e + 1:e + 2], cblk[:, e:e + 1], nblk[:, e:e + 1], ALU.add))
                link(nc.vector.scalar_tensor_tensor(delta[:, 0:E], cblk[:, 0:E], -float(P), ecap[:, 0:E],
                                                    ALU.mult, ALU.add))
                link(nc.vector.memset(delta[:, E:E + 1], float(E * CAP)))
                sz = ns * (E + 1)
                reached = big[:, 0, 0:sz].rearrange("p (j e) -> p j e", e=E + 1)
                owner = big[:, 1, 0:sz].rearrange("p (j e) -> p j e", e=E + 1)
                term = big[:, 2, 0:sz].rearrange("p (j e) -> p j e", e=E + 1)
                num = slot_f[:, 0:ns, 2]

                def per_e(ap):
                    return ap[:, 0:E + 1].unsqueeze(1).broadcast_to([P, ns, E + 1])

                link(nc.vector.tensor_tensor(reached, num.unsqueeze(2).broadcast_to([P, ns, E + 1]), per_e(cblk),
                                             ALU.is_ge))
                link(nc.vector.tensor_tensor(owner[:, :, 0:E], reached[:, :, 0:E], reached[:, :, 1:E + 1],
                                             ALU.subtract))
                link(nc.vector.tensor_copy(owner[:, :, E:E + 1], reached[:, :, E:E + 1]))
                link(nc.vector.tensor_tensor(term, owner, per_e(delta), ALU.mult))
                link(nc.vector.tensor_reduce(slot_f[:, 0:ns, 0:1], term, AX.X, ALU.add))
                link(nc.vector.tensor_scalar(term[:, :, 0], owner[:, :, E], -float(P), float(P), ALU.mult, ALU.add))
                link(nc.vector.tensor_tensor(term[:, :, 0], term[:, :, 0], num, ALU.mult))
                link(nc.vector.tensor_tensor(slot_f[:, 0:ns, 0], slot_f[:, 0:ns, 0], term[:, :, 0], ALU.add))
                link(nc.vector.tensor_tensor(term, owner, per_e(eid), ALU.mult))
                link(nc.vector.tensor_reduce(slot_f[:, 0:ns, 1:2], term, AX.X, ALU.add))
                link(nc.vector.tensor_scalar(slot_f[:, 0:ns, 1], slot_f[:, 0:ns, 1], float(E - 1), None, ALU.min))
                link(nc.vector.tensor_copy(slot_i[:, 0:ns, :], slot_f[:, 0:ns, 0:2]))
                assert n[0] == TABLE[phase_of_moe(phase)], n[0]
                link(nc.vector.tensor_copy(ddelta[:, 0:1], delta[:, 0:1]))
                link(nc.vector.tensor_tensor(ddelta[:, 1:E], delta[:, 1:E], delta[:, 0:E - 1], ALU.subtract))
                rows = row_all[:, :, 0:K]
                room = qkvq[:, :, :, :].rearrange("p g i k -> p (g i k)")
                at_least = room[:, 0:NT * K * E].rearrange("p (n k e) -> p n k e", k=K, e=E)
                less = room[:, NT * K * E:NT * K * (E + 1)].rearrange("p (n k) -> p n k", k=K)
                link(nc.vector.tensor_tensor(at_least, rows.unsqueeze(3).broadcast_to([P, NT, K, E]),
                                             ecap[:, 0:E].unsqueeze(1).unsqueeze(1).broadcast_to([P, NT, K, E]),
                                             ALU.is_ge))
                link(nc.vector.tensor_tensor(at_least, at_least,
                                             ddelta[:, 0:E].unsqueeze(1).unsqueeze(1).broadcast_to([P, NT, K, E]),
                                             ALU.mult))
                link(nc.vector.tensor_reduce(less.unsqueeze(3), at_least, AX.X, ALU.add))
                link(nc.vector.tensor_tensor(less, rows, less, ALU.subtract))
                link(nc.vector.tensor_copy(pos_idx[:, :, 0:K], less))
                link(nc.vector.memset(taken[:, :], 0.0))
                link(nc.vector.memset(taken_bf[:, :], 0.0))
                assert n[0] == TABLE_POS[PH_Q if phase == PH_A else PH_O], n[0]

            def slots(phase):
                m = moe[phase]

                def stage(name, use, t, r):
                    at = counter(phase, r)
                    if name == "up" and phase == PH_M1:
                        v.wait_ge(S["slot_act"][t], at("slot_act", 0, "act"))
                        nc.vector.tensor_tensor(big[:, t, 0:F1], hi(t)[:, :], big[:, t, 0:F1], ALU.mult)\
                            .then_inc(S["slot_y"][t], 1)
                    if name == "down":
                        if not (isinstance(r, int) and r == 0):
                            v.wait_ge(S["slot_out"][t], counter(phase, r - 1)("slot_out"))
                        v.wait_ge(S["slot_ps"][t], at("slot_ps", 0, "y"))
                        nc.vector.tensor_copy(o[:, t], hi(t)[:, 0:C]).then_inc(S["slot_y"][t], 1)

                run(v, "dve", phase, stage)

            def quantise(at, event, i, t, src, dst, col):
                if event == "a":
                    ins = nc.vector.tensor_scalar(dst, src, qinv[:, col:col + 1], MAGIC, ALU.mult, ALU.add)
                elif event == "b":
                    v.wait_ge(S["quant"][t], at("quant", i, "a"))
                    ins = nc.vector.tensor_scalar(dst, dst, qmagic[:, col:col + 1], 0.0, ALU.subtract, ALU.max)
                else:
                    v.wait_ge(S["quant"][t], at("quant", i, "b"))
                    ins = nc.vector.tensor_scalar(dst, dst, QMAX, qzero[:, col:col + 1], ALU.min, ALU.subtract)
                ins.then_inc(S["quant"][t], 1)

            def stage_a(name, use, t, r):
                at = counter(PH_A, r)
                if name in ("stats", "norm"):
                    layer_norm(PH_A, name, use, t, r)
                if (PH_A, use) in att:
                    attention_stage(PH_A, name, use, t, at)
                if name == "output":
                    if use < 2:
                        v.wait_ge(S["pool_x"][t], at("pool_x", use + 1))
                    add_output(at, use, t, x if use < 2 else h)
                if name == "router":
                    keep_logits(PH_A, at, t)
                if name in ("choose", "ranked", "places"):
                    routing(PH_A, r, name)

            run(v, "dve", PH_A, stage_a)
            slot_table(PH_A, 0)
            slots(PH_M0)
            v.wait_ge(w_layer1, 16 * len(layer1))
            phase_over(v, PH_M0)

            def stage_q(name, use, t, r):
                at = counter(PH_Q, r)
                if name == "combine":
                    if not (isinstance(r, int) and r == 0):
                        v.wait_ge(S["stored"][t], counter(PH_Q, r - 1)("stored"))
                    v.wait_ge(S["loaded"][t], at("loaded", 0))
                    v.wait_ge(S["gathered"][t], at("gathered", K0 - 1))
                    wt = w_t[:, t]
                    nc.vector.tensor_copy(wt, w_all[:, bass.ds(r * G + t, 1), :].rearrange("p a k -> p (a k)"))\
                        .then_inc(S["logits"][t], 1)
                    v.wait_ge(S["logits"][t], at("logits"))
                    for s_ in range(K0):
                        if s_ == 1:
                            v.wait_ge(S["x_added"][t], at("x_added", 0))
                        nc.vector.scalar_tensor_tensor(x[:, t], big[:, t, s_ * C:(s_ + 1) * C], wt[:, s_:s_ + 1],
                                                       xin[:, t] if s_ == 0 else x[:, t], ALU.mult, ALU.add)\
                            .then_inc(S["x_added"][t], 1)
                if name in ("stats", "norm"):
                    layer_norm(PH_Q, name, 0, t, r)
                if name == "rope":
                    v.wait_ge(S["att_ps"][t], at("att_ps", 0, "proj"))
                    rope(at, t, qkv[:, 0:2, bass.ds(r * (G * P) + t * P, P)])

            run(v, "dve", PH_Q, stage_q)

            n = [0]

            def link(ins):
                n[0] += 1
                ins.then_inc(stat_dve, 1)
                v.wait_ge(stat_dve, n[0])

            def ranges(src, count, most, least):
                for i in range(count):
                    link(nc.vector.tensor_reduce(stats[:, most + i:most + i + 1], src(i), AX.X, ALU.max))
                    link(nc.vector.tensor_reduce(stats[:, least + i:least + i + 1], src(i), AX.X, ALU.min))
                link(nc.vector.tensor_scalar(stats[:, least:least + count], stats[:, least:least + count],
                                             -1.0, None, ALU.mult))

            def quantisers(col, count, most, least):
                c = slice(col, col + count)
                link(nc.vector.tensor_tensor(qstep[:, c], gstats[:, most:most + count],
                                             gstats[:, least:least + count], ALU.add))
                link(nc.vector.tensor_scalar(qstep[:, c], qstep[:, c], 1.0 / QMAX, 1e-12, ALU.mult, ALU.add))
                link(nc.vector.reciprocal(qinv[:, c], qstep[:, c]))
                link(nc.vector.tensor_tensor(qzero[:, c], gstats[:, least:least + count], qinv[:, c], ALU.mult))
                link(nc.vector.tensor_scalar(qzero[:, c], qzero[:, c], MAGIC, None, ALU.add))
                link(nc.vector.tensor_scalar(qzero[:, c], qzero[:, c], MAGIC, None, ALU.subtract))
                link(nc.vector.tensor_scalar(qmagic[:, c], qzero[:, c], -1.0, MAGIC, ALU.mult, ALU.add))

            phase_over(v, PH_Q)
            ranges(lambda i: qkv[:, i, :], 3, 0, 3)
            v.wait_ge(stat_all, 1)
            quantisers(0, 3, 0, 3)
            link(nc.vector.scalar_tensor_tensor(sS[:, :], qstep[:, 0:1], 8.0 ** -0.5, qstep[:, 1:2],
                                                ALU.mult, ALU.mult))
            assert n[0] == STAT_Y - 3

            def stage_b(name, use, t, r):
                at = counter(PH_B, r)
                if name == "quantise":
                    for event in "abc":
                        for i in range(3):
                            quantise(at, event, i, t, qkv[:, i, bass.ds(r * (G * P) + t * P, P)], qkvq[:, t, i], i)
                attention_stage(PH_B, name, use, t, at)
                if name == "normalise":
                    v.wait_ge(S["probs"][t], at("probs"))
                    pv = P_(t).rearrange("p (h k) -> p h k", k=T)
                    nc.vector.tensor_reduce(rsum[:, t], pv, AX.X, ALU.add).then_inc(S["soft"][t], 1)
                    v.wait_ge(S["soft"][t], at("soft", 0, "sum"))
                    nc.vector.reciprocal(rinv[:, t], rsum[:, t]).then_inc(S["soft"][t], 1)
                    v.wait_ge(S["soft"][t], at("soft", 0, "inv"))
                    nc.vector.scalar_tensor_tensor(pv, pv, QMAX, rinv[:, t].unsqueeze(2).broadcast_to([P, 16, T]),
                                                   ALU.mult, ALU.mult).then_inc(S["soft"][t], 1)
                if name == "weigh":
                    v.wait_ge(S["att_ps"][t], at("att_ps", 0, "o"))
                    nc.vector.tensor_scalar(
                        qkv[:, 0, bass.ds(r * (G * P) + t * P, P)].rearrange("p (h d) -> p h d", d=8),
                        lo(t)[:, 0:144].rearrange("p (h d) -> p h d", d=9)[:, :, 0:8],
                        qstep[:, 2:3], 1.0 / QMAX, ALU.mult, ALU.mult).then_inc(S["o"][t], 1)

            run(v, "dve", PH_B, stage_b)

            phase_over(v, PH_B)
            ranges(lambda i: qkv[:, 0, :], 1, 6, 7)
            assert n[0] == STAT_Y
            v.wait_ge(stat_all, 2)
            quantisers(3, 1, 6, 7)

            def stage_c(name, use, t, r):
                at = counter(PH_C, r)
                if name == "quantise":
                    for event in "abc":
                        quantise(at, event, 0, t, qkv[:, 0, bass.ds(r * (G * P) + t * P, P)], h2[:, t], 3)
                if name == "y_out":
                    v.wait_ge(S["loaded"][t], at("loaded", 1))
                    if not (isinstance(r, int) and r == 0):
                        v.wait_ge(S["stored"][t], counter(PH_C, r - 1)("stored"))
                    v.wait_ge(S["out_ps"][t], at("out_ps", 0, "out"))
                    nc.vector.scalar_tensor_tensor(x[:, t], hi(t)[:, P:2 * P], qstep[:, 3:4], xin[:, t],
                                                   ALU.mult, ALU.add).then_inc(S["x_added"][t], 1)
                if name in ("stats", "norm"):
                    layer_norm(PH_C, name, use, t, r)
                if (PH_C, use) in att:
                    attention_stage(PH_C, name, use, t, at)
                if name == "weigh" and use == 0:
                    v.wait_ge(S["o"][t], at("o", 0, "done"))
                    nc.vector.tensor_tensor(x[:, t], x[:, t], o[:, t], ALU.add).then_inc(S["x_added"][t], 1)
                if name == "convolve":
                    v.wait_ge(S["rows_T"][t], at("rows_T", 2))
                    nc.vector.tensor_scalar(hT[:, t], oT[:, t], w["f1_conv"][:, 2:3], None, ALU.mult)\
                        .then_inc(S["conv"][t], 1)
                    for back in (1, 2):
                        v.wait_ge(S["conv"][t], at("conv", back - 1))
                        rows = hT[:, t].rearrange("p (b k) -> p b k", b=2)[:, :, back:T]
                        before = oT[:, t].rearrange("p (b k) -> p b k", b=2)[:, :, 0:T - back]
                        nc.vector.scalar_tensor_tensor(rows, before, w["f1_conv"][:, 2 - back:3 - back], rows,
                                                       ALU.mult, ALU.add).then_inc(S["conv"][t], 1)
                if name == "rope":
                    rope(at, t, qk[:, t])
                if name == "output":
                    add_output(at, 1, t, h)
                if name == "router":
                    keep_logits(PH_C, at, t)
                if name in ("choose", "ranked", "places"):
                    routing(PH_C, r, name)

            run(v, "dve", PH_C, stage_c)
            slot_table(PH_C, TABLE_POS[PH_Q])
            slots(PH_M1)
            phase_over(v, PH_M1)

            def stage_o(name, use, t, r):
                at = counter(PH_O, r)
                if name == "combine":
                    if not (isinstance(r, int) and r == 0):
                        v.wait_ge(S["stored"][t], counter(PH_O, r - 1)("stored"))
                    v.wait_ge(S["loaded"][t], at("loaded", 0))
                    v.wait_ge(S["gathered"][t], at("gathered", 0))
                    nc.vector.tensor_tensor(x[:, t], xin[:, t], big[:, t, 0:C], ALU.add)\
                        .then_inc(S["x_added"][t], 1)

            run(v, "dve", PH_O, stage_o)


def kernel(**inputs):
    import numpy as np
    import concourse.bacc as bacc
    from concourse import mybir as mb
    from concourse.bass_utils import run_bass_kernel_spmd

    def g(name):
        return np.asarray(inputs[name])

    def col(v):
        return v.reshape(-1, 1)

    def rows(v, n=128):
        return np.tile(v.reshape(1, -1), (n, 1))

    def chunks(m):
        return m.reshape(-1, 128, 128).transpose(1, 0, 2)

    def swapped(m):
        return m.reshape(128, 16, 2, 4)[:, :, ::-1, :].reshape(128, 128)

    def spread(m):
        return np.repeat(m.reshape(128, 4, 1, 8), 4, axis=2).reshape(128, 128)

    freq = (1.0 / 10000.0 ** (np.arange(0, 8, 2, dtype=np.float32) / 8)).astype(np.float32)
    angle = (np.arange(64, dtype=np.float32)[None, :] * freq[:, None]).astype(np.float32)
    cos = np.tile(np.cos(angle), (32, 1)).astype(np.float32)
    sin = np.tile(np.concatenate([-np.sin(angle), np.sin(angle)]), (16, 1)).astype(np.float32)

    wqkv, bqkv, fqkv = g("L0_attn_w_qkv"), g("L0_attn_b_qkv"), g("L1_ffn_attn_w")
    wk1 = spread(g("L1_attn_Wk"))
    arrays = {
        "x": g("x").reshape(4096, 128), "ctx": g("ctx_1024").reshape(4096, 128),
        "fire_w1": col(g("L1_attn_fire_w1")), "fire_b1": col(g("L1_attn_fire_b1")), "fire_w2": g("L1_attn_fire_w2"),
        "fire_b2": rows(g("L1_attn_fire_b2")), "fire_c": rows(g("L1_attn_fire_c"), 32),
        "fire_L": rows(g("L1_attn_fire_L"), 32),
        "a0_g": col(g("L0_attn_ln_gamma")), "a0_b": col(g("L0_attn_ln_beta")), "a0_wqkv": wqkv,
        "a0_bq": col(bqkv[0:128]), "a0_bk": col(bqkv[128:256]), "a0_bv": rows(bqkv[256:384]),
        "a0_wout": g("L0_attn_w_out"), "a0_bout": rows(g("L0_attn_b_out")),
        "x0_wq": g("L0_xattn_Wq"), "x0_wk": g("L0_xattn_Wk"), "x0_wv": g("L0_xattn_Wv"), "x0_wo": g("L0_xattn_Wo"),
        "x0_bq": col(g("L0_xattn_bq")), "x0_bk": col(g("L0_xattn_bk")), "x0_bv": rows(g("L0_xattn_bv")),
        "x0_bo": rows(g("L0_xattn_bo")),
        "f0_g1": col(g("L0_ffn_ln1_w")), "f0_g2": col(g("L0_ffn_ln2_w")), "f0_wqkv": g("L0_ffn_c_attn_w"),
        "f0_wo": g("L0_ffn_c_proj_w"), "f0_wr": g("L0_ffn_router_w"),
        "f0_w1": g("L0_ffn_w1"), "f0_w2": chunks(g("L0_ffn_w2")),
        "cosT": cos, "sinT": sin,
        "a1_wq": g("L1_attn_Wq"), "a1_wqs": swapped(g("L1_attn_Wq")), "a1_wk": wk1, "a1_wks": swapped(wk1),
        "a1_wv": spread(g("L1_attn_Wv")), "a1_wo": g("L1_attn_Wproj"),
        "x1_wq": g("L1_xattn_Wq").T, "x1_wk": g("L1_xattn_Wk").T, "x1_wv": g("L1_xattn_Wv").T,
        "f1_g1": col(g("L1_ffn_ln1_w")), "f1_b1": col(g("L1_ffn_ln1_b")),
        "f1_g2": col(g("L1_ffn_ln2_w")), "f1_b2": col(g("L1_ffn_ln2_b")),
        "f1_conv": g("L1_ffn_conv_w").reshape(128, 3),
        "f1_wq": fqkv[:, 0:128], "f1_wqs": swapped(fqkv[:, 0:128]),
        "f1_wk": fqkv[:, 128:256], "f1_wks": swapped(fqkv[:, 128:256]), "f1_wv": fqkv[:, 256:384],
        "f1_wo": g("L1_ffn_proj_w"), "f1_wr": g("L1_ffn_router_w"),
        "f1_wv13": g("L1_ffn_expert_wv").transpose(1, 0, 2), "f1_w2": chunks(g("L1_ffn_expert_proj")),
    }
    arrays = {"in_" + n: np.ascontiguousarray(v) for n, v in arrays.items()}
    nc = bacc.Bacc("TRN2", target_bir_lowering=False, num_devices=1)
    aps = {n[3:]: nc.dram_tensor(n, v.shape, mb.dt.from_np(v.dtype), kind="ExternalInput").ap()
           for n, v in arrays.items()}
    for n, rows_ in (("_mid", N), ("_mid2", N), ("_rows0", E0 * CAP + P), ("_rows1", E1 * CAP + P),
                     ("_out0", NS0 * P), ("_out1", NS1 * P)):
        aps[n] = nc.dram_tensor("scratch" + n, (rows_, 128), mb.dt.float32, kind="Internal").ap()
    out = nc.dram_tensor("out", (4096, 128), mb.dt.float32, kind="ExternalOutput").ap()
    decoder_kernel(nc, aps, out)
    r = run_bass_kernel_spmd(nc, [arrays], core_ids=[0])
    return r.results[0]["out"].reshape(64, 64, 128)
```

```python
from contextlib import ExitStack

import concourse.bass as bass
from concourse import mybir

F32 = mybir.dt.float32
BF16 = mybir.dt.bfloat16
I32 = mybir.dt.int32
U32 = mybir.dt.uint32
ALU = mybir.AluOpType
ACT = mybir.ActivationFunctionType
AX = mybir.AxisListType

P = 128
C = 128
T = 64
B = 64
N = B * T
NT = N // P
G = 4
R = NT // G
E0, F0, K0 = 8, 256, 2
E1, F1, K1 = 4, 512, 1
CAP = N + P
NF = 32
EPS = 1e-5
MAGIC = 12582912.0
QMAX = 255.0
NEG = -1e30

NS0 = -(-(N * K0 // P + E0 - 1) // G) * G
NS1 = -(-(N * K1 // P + E1 - 1) // G) * G

PH_A, PH_M0, PH_Q, PH_B, PH_C, PH_M1, PH_O = range(7)
GROUPS = (R, NS0 // G, R, R, R, NS1 // G, R)


def seq(uses, *events):
    return [(u, e) for u in range(uses) for e in (events or (None,))]


EVENTS = {
    "ln": {PH_A: seq(6, "stats", "mean", "done"), PH_Q: seq(1, "stats", "mean", "done"),
           PH_C: seq(4, "stats", "mean", "done")},
    "veps": {PH_A: seq(6), PH_Q: seq(1), PH_C: seq(4)},
    "rstd": {PH_A: seq(6), PH_Q: seq(1), PH_C: seq(4)},
    "rows_ps": {PH_A: seq(4), PH_Q: seq(1), PH_C: seq(4)},
    "rows_T": {PH_A: seq(4), PH_Q: seq(2), PH_C: seq(4)},
    "ctx_ps": {PH_A: seq(1), PH_C: seq(1)},
    "ctx_T": {PH_A: seq(1), PH_C: seq(1)},
    "att_ps": {PH_A: seq(3, "proj", "scores0", "scores1", "pT0", "pT1", "o"), PH_Q: seq(1, "proj"),
               PH_B: seq(1, "proj", "scores0", "scores1", "pT0", "pT1", "o"),
               PH_C: seq(2, "proj", "scores0", "scores1", "pT0", "pT1", "o")},
    "qk": {PH_A: seq(3), PH_C: seq(1)},
    "v": {PH_A: seq(3, "v", "spread"), PH_B: seq(1, "v"), PH_C: seq(2, "v", "spread")},
    "kblk": {PH_A: seq(3), PH_B: seq(1), PH_C: seq(2)},
    "shift": {PH_A: seq(3, "max0", "shifted0", "max1", "shifted1"), PH_B: seq(1, "max0", "max1"),
              PH_C: seq(2, "max0", "shifted0", "max1", "shifted1")},
    "probs": {PH_A: seq(3, "0", "1"), PH_B: seq(1, "0", "1"), PH_C: seq(2, "0", "1")},
    "pT": {PH_A: seq(3, "0", "1"), PH_B: seq(1, "0", "1"), PH_C: seq(2, "0", "1")},
    "o": {PH_A: seq(3, "inv", "done"), PH_B: seq(1, "done"), PH_C: seq(2, "inv", "done")},
    "out_ps": {PH_A: seq(3, "oT", "out"), PH_C: [(0, "out"), (1, "oT"), (1, "out")]},
    "oT": {PH_A: seq(3), PH_C: seq(1)},
    "x_added": {PH_A: seq(3), PH_Q: seq(2), PH_C: seq(3), PH_O: seq(1)},
    "pool_x": {PH_A: seq(4), PH_Q: seq(1), PH_B: seq(1, "0", "1"), PH_C: seq(1), PH_O: seq(1)},
    "rope": {PH_Q: seq(1, "cos", "sin", "done"), PH_C: seq(1, "cos", "sin", "done")},
    "conv": {PH_C: seq(3)},
    "quant": {PH_B: [(i, e) for e in "abc" for i in range(3)], PH_C: seq(1, "a", "b", "c")},
    "soft": {PH_B: seq(1, "biased0", "biased1", "sum0", "inv0", "normed0", "sum1", "inv1", "normed1")},
    "rounded": {PH_B: seq(1, "0", "1")},
    "logit_ps": {PH_A: seq(1), PH_C: seq(1)},
    "logits": {PH_A: seq(1), PH_Q: seq(1), PH_C: seq(1)},
    "slot_ps": {PH_M0: seq(1, "rows", "up", "hid", "y"), PH_M1: seq(1, "rows", "up", "hid", "y")},
    "slot_act": {PH_M0: seq(1, "rows", "act", "hid"), PH_M1: seq(1, "rows", "act", "hid")},
    "slot_y": {PH_M0: seq(1, "weights", "y"), PH_M1: seq(1, "weights", "hid", "y")},
    "loaded": {PH_A: seq(2), PH_Q: seq(1), PH_C: seq(2), PH_O: seq(1)},
    "stored": {PH_A: seq(1), PH_Q: seq(1), PH_C: seq(1), PH_O: seq(1)},
    "gathered": {PH_Q: seq(K0), PH_O: seq(K1)},
    "slot_in": {PH_M0: seq(1), PH_M1: seq(1)},
    "slot_out": {PH_M0: seq(1), PH_M1: seq(1)},
}
DMA = ("loaded", "stored", "gathered", "slot_in", "slot_out")
ROUTE = {PH_A: 25, PH_C: 13}
CHOSEN = {PH_A: 11, PH_C: 5}
RANKED = {PH_A: 12, PH_C: 6}
TABLE = {PH_M0: 28, PH_M1: 28 + 9 + 24}
TABLE_POS = {PH_Q: 28 + 9, PH_O: 28 + 9 + 24 + 9}
STAT_Y = 19


def phase_of_moe(phase):
    return PH_M0 if phase == PH_A else PH_M1


def counter(phase, r):
    def at(name, use=0, event=None):
        by = EVENTS[name]
        before = sum(GROUPS[p] * len(by[p]) for p in by if p < phase)
        value = r * len(by[phase]) + (before + by[phase].index((use, event)) + 1)
        return value * 16 if name in DMA else value
    return at


def total(name, phase):
    n = sum(GROUPS[p] * len(e) for p, e in EVENTS[name].items() if p <= phase)
    return n * 16 if name in DMA else n


def route_at(phase, r, step):
    return r * ROUTE[phase] + ((R * ROUTE[PH_A] if phase == PH_C else 0) + step + 1)


VECTOR_HEADS = {(PH_A, 0): 4, (PH_A, 1): 4, (PH_A, 2): 4, (PH_C, 0): 2, (PH_C, 1): 4}

TIMES = {
    PH_A: [
        ("load", 0, dict(sp=0.00)), ("stats", 0, dict(dve=7.49, act=7.89, pool=8.93)), ("norm", 0, dict(dve=9.31)),
        ("stats", 1, dict(dve=9.65, act=10.24, pool=13.53)), ("norm", 1, dict(dve=13.59, pool=14.97)),
        ("rows", 0, dict(pe=15.65, act=16.12)), ("project", 0, dict(pe=16.43, act=16.97, dve=16.71)),
        ("spread", 0, dict(pool=19.40, dve=19.01)), ("scores0", 0, dict(pe=21.66)), ("scores1", 0, dict(pe=22.28)),
        ("shift0", 0, dict(dve=22.51)), ("shift1", 0, dict(dve=23.23)), ("softmax0", 0, dict(act=22.74)),
        ("softmax1", 0, dict(act=24.56)), ("turn0", 0, dict(pe=23.65, act=24.87)),
        ("turn1", 0, dict(pe=25.82, act=26.07)), ("weigh", 0, dict(pe=27.72, dve=30.12)),
        ("turn_o", 0, dict(pe=32.52, act=32.93)), ("output", 0, dict(pe=33.83, dve=36.86)),
        ("stats", 2, dict(dve=37.32, act=37.51, pool=38.54)), ("norm", 2, dict(dve=39.17, pool=39.62)),
        ("rows", 1, dict(pe=40.34, act=40.40)), ("project", 1, dict(pe=41.85, act=43.16, dve=43.01)),
        ("spread", 1, dict(pool=45.00, dve=43.94)), ("scores0", 1, dict(pe=46.49)), ("scores1", 1, dict(pe=49.93)),
        ("shift0", 1, dict(dve=47.60)), ("shift1", 1, dict(dve=51.14)), ("softmax0", 1, dict(act=51.64)),
        ("softmax1", 1, dict(act=53.88)), ("turn0", 1, dict(pe=53.36, act=54.65)),
        ("turn1", 1, dict(pe=54.44, act=54.92)), ("weigh", 1, dict(pe=56.12, dve=57.04)),
        ("turn_o", 1, dict(pe=57.61, act=59.33)), ("output", 1, dict(pe=61.80, dve=61.90)),
        ("stats", 3, dict(dve=62.30, act=63.07, pool=63.35)), ("norm", 3, dict(dve=63.53)),
        ("stats", 4, dict(dve=63.78, act=64.98, pool=65.93)), ("norm", 4, dict(dve=67.63)),
        ("rows", 2, dict(pe=68.48, act=68.87)), ("project", 2, dict(pe=68.99, act=70.22, dve=69.87)),
        ("spread", 2, dict(pool=75.11, dve=72.82)), ("scores0", 2, dict(pe=76.19)), ("scores1", 2, dict(pe=77.95)),
        ("shift0", 2, dict(dve=78.09)), ("shift1", 2, dict(dve=79.47)), ("softmax0", 2, dict(act=78.46)),
        ("softmax1", 2, dict(act=81.94)), ("turn0", 2, dict(pe=80.60, act=82.41)),
        ("turn1", 2, dict(pe=82.58, act=83.04)), ("weigh", 2, dict(pe=85.43, dve=85.80)),
        ("turn_o", 2, dict(pe=87.01, act=87.14)), ("output", 2, dict(pe=88.95, dve=89.68)),
        ("stats", 5, dict(dve=90.57, act=91.84, pool=92.45)), ("norm", 5, dict(dve=92.72)),
        ("router_rows", 0, dict(pe=93.77, act=95.68)), ("router", 0, dict(pe=97.62, dve=97.72)),
        ("collect", 0, dict(act=100.92)), ("choose", 0, dict(dve=102.23)), ("ranks", 0, dict(pe=103.63, act=104.26)),
        ("ranked", 0, dict(dve=106.60, pe=107.14)), ("places", 0, dict(dve=107.86)),
        ("scatter", 0, dict(pool=115.91)), ("scatter", 1, dict(pool=122.17)), ("scatter", 2, dict(pool=125.09)),
        ("scatter", 3, dict(pool=146.39)), ("store", 0, dict(sp=98.42))],
    PH_M0: [
        ("load", 0, dict(sp=0.00)), ("rows", 0, dict(pe=3.39, act=3.81)), ("weights", 0, dict(dve=2.84)),
        ("up", 0, dict(pe=4.83, act=5.91)), ("hid", 0, dict(pe=6.73, act=6.94)),
        ("down", 0, dict(pe=8.29, dve=9.64)), ("store", 0, dict(sp=10.34))],
    PH_Q: [
        ("load", 0, dict(sp=0.16, pool=0.00)), ("combine", 0, dict(dve=8.02)),
        ("stats", 0, dict(dve=9.89, act=10.33, pool=10.81)), ("norm", 0, dict(dve=11.76)),
        ("rows", 0, dict(pe=14.38, act=14.61)), ("project", 0, dict(pe=14.68, act=17.20)),
        ("rope", 0, dict(dve=20.79)), ("store", 0, dict(sp=21.49))],
    PH_B: [
        ("quantise", 0, dict(act=0.00, dve=4.46)), ("centre", 0, dict(act=5.55)),
        ("values", 0, dict(pe=6.41, act=9.96)), ("spread", 0, dict(pool=14.11)), ("scores0", 0, dict(pe=23.78)),
        ("scores1", 0, dict(pe=30.11)), ("shift0", 0, dict(dve=26.34, pool=41.23)),
        ("shift1", 0, dict(dve=43.23, pool=43.31)), ("softmax0", 0, dict(act=45.34)),
        ("normalise0", 0, dict(dve=48.04, act=54.21)), ("softmax1", 0, dict(act=47.99)),
        ("normalise1", 0, dict(dve=55.69, act=58.35)), ("turn0", 0, dict(pe=58.99, act=60.03)),
        ("turn1", 0, dict(pe=61.74, act=64.85)), ("weigh", 0, dict(pe=67.20, dve=71.51))],
    PH_C: [
        ("load", 0, dict(sp=0.00)), ("quantise", 0, dict(dve=20.98)), ("y_rows", 0, dict(pe=24.44, act=25.30)),
        ("y_out", 0, dict(pe=26.20, dve=26.58)), ("stats", 0, dict(dve=31.36, act=32.93, pool=35.86)),
        ("norm", 0, dict(dve=38.08)), ("rows", 0, dict(pe=38.54, act=41.53)),
        ("project", 0, dict(pe=44.09, act=45.16, dve=44.26)), ("spread", 0, dict(pool=46.59, dve=48.92)),
        ("scores0", 0, dict(pe=49.76)), ("scores1", 0, dict(pe=57.03)), ("shift0", 0, dict(dve=55.41)),
        ("shift1", 0, dict(dve=61.31)), ("softmax0", 0, dict(act=58.20)), ("softmax1", 0, dict(act=65.64)),
        ("turn0", 0, dict(pe=64.36, act=68.09)), ("turn1", 0, dict(pe=66.53, act=73.36)),
        ("weigh", 0, dict(pe=73.87, dve=75.98)), ("stats", 1, dict(dve=76.21, act=79.11, pool=80.68)),
        ("norm", 1, dict(dve=83.61)), ("stats", 2, dict(dve=84.81, act=85.62, pool=86.06)),
        ("norm", 2, dict(dve=88.09)), ("conv_rows", 0, dict(pe=88.31, act=90.07)), ("convolve", 0, dict(dve=93.20)),
        ("project", 1, dict(pe=99.35, dve=103.53)), ("rope", 0, dict(dve=107.73)),
        ("spread", 1, dict(pool=115.19, dve=111.88)), ("scores0", 1, dict(pe=115.96)),
        ("scores1", 1, dict(pe=121.14)), ("shift0", 1, dict(dve=122.05)), ("shift1", 1, dict(dve=125.92)),
        ("softmax0", 1, dict(act=126.57)), ("softmax1", 1, dict(act=127.36)),
        ("turn0", 1, dict(pe=129.40, act=131.49)), ("turn1", 1, dict(pe=131.07, act=136.48)),
        ("weigh", 1, dict(pe=142.87, dve=146.15)), ("turn_o", 1, dict(pe=147.60, act=149.40)),
        ("output", 1, dict(pe=151.55, dve=153.72)), ("stats", 3, dict(dve=154.15, act=155.11, pool=155.45)),
        ("norm", 3, dict(dve=157.86)), ("router_rows", 0, dict(pe=158.05, act=159.89)),
        ("router", 0, dict(pe=160.52, dve=162.62)), ("collect", 0, dict(act=163.31)),
        ("choose", 0, dict(dve=165.69)), ("ranks", 0, dict(pe=171.58)), ("ranked", 0, dict(dve=172.36, pe=180.67)),
        ("places", 0, dict(dve=208.17)), ("scatter", 0, dict(pool=222.10)), ("scatter", 1, dict(pool=242.91)),
        ("scatter", 2, dict(pool=273.39)), ("scatter", 3, dict(pool=281.56)), ("store", 0, dict(sp=163.32))],
    PH_M1: [
        ("load", 0, dict(sp=0.00)), ("rows", 0, dict(pe=6.95, act=8.19)), ("weights", 0, dict(dve=6.15)),
        ("up", 0, dict(pe=8.93, act=10.55, dve=10.70)), ("hid", 0, dict(pe=14.19, act=15.86)),
        ("down", 0, dict(pe=19.23, dve=20.49)), ("store", 0, dict(sp=21.19))],
    PH_O: [
        ("load", 0, dict(sp=0.00, pool=0.00)), ("combine", 0, dict(dve=5.86)), ("store", 0, dict(sp=6.56))],
}
ROUTING = ("collect", "choose", "ranks", "ranked", "places", "scatter")
BEAT = {PH_A: 23.148, PH_M0: 2.176, PH_Q: 3.594, PH_B: 18.721, PH_C: 35.780, PH_M1: 3.724, PH_O: 2.200}


def timetable(phase, engine):
    turn, found = G * BEAT[phase], []
    for n, (name, use, when) in enumerate(TIMES[phase]):
        for lane in (G - 1,) if name in ROUTING else range(G):
            if engine in when:
                late, time = divmod(when[engine] + lane * BEAT[phase], turn)
                found.append((time, n, name, use, lane, int(late)))
    return sorted(found)


def run(engine, which, phase, stage):
    groups, stages = GROUPS[phase], timetable(phase, which)
    most = max((late for *_, late in stages), default=0)

    def turn(n):
        for _, _, name, use, lane, late in stages:
            if 0 <= n - late < groups:
                stage(name, use, lane, n - late)

    for n in range(most):
        turn(n)
    if stages:
        with engine.Fori(most, groups) as r:
            group = [r - late if late else r for late in range(most + 1)]
            for _, _, name, use, lane, late in stages:
                stage(name, use, lane, group[late])
    for n in range(groups, groups + most):
        turn(n)


def decoder_kernel(nc, a, out):
    ctx = ExitStack()
    with ctx:
        def sb(name, shape, dt=F32):
            return ctx.enter_context(nc.sbuf_tensor(name, shape, dt))

        def sem(name):
            return ctx.enter_context(nc.semaphore(name))

        S = {name: [sem(f"{name}{t}") for t in range(G)] for name in EVENTS}
        w_attn0 = sem("w_attn0")
        w_moe0 = sem("w_moe0")
        w_layer1 = sem("w_layer1")
        const_ready = sem("const_ready")
        const_step = sem("const_step")
        fire_pe = sem("fire_pe")
        fire_act = sem("fire_act")
        fire_dve = sem("fire_dve")
        fire_pool = sem("fire_pool")
        stat_dve = sem("stat_dve")
        stat_all = sem("stat_all")
        route = sem("route")
        collected = sem("collected")
        route_exp = sem("route_exp")
        rank_ps = sem("rank_ps")
        scattered = sem("scattered")
        count_ps = sem("count_ps")
        table = sem("table")
        zero_rows = sem("zero_rows")

        w = {n: sb("w_" + n, list(a[n].shape)) for n in a if n not in ("x", "ctx") and n[0] != "_"}
        moe0 = [n for n in w if n in ("f0_w1", "f0_w2")]
        layer1 = [n for n in w if n[:2] in ("a1", "x1", "f1") or n in ("cosT", "sinT")]
        attn0 = [n for n in w if n not in moe0 + layer1]

        ident = sb("ident", [P, P])
        ident_bf = sb("ident_bf", [P, P], BF16)
        ones_bf = sb("ones_bf", [P, P], BF16)
        before_bf = sb("before_bf", [P, P], BF16)
        causal_bf = sb("causal_bf", [P, T], BF16)
        causal = sb("causal", [P, T])
        blk16 = sb("blk16", [P, 16])
        blk8 = sb("blk8", [P, 8])
        minus_half = sb("minus_half", [P, 1])
        eps = sb("eps", [P, 1])
        unused = sb("unused", [P, G])
        unused_pool = sb("unused_pool", [P, 3 * G])
        first8 = sb("first8", [P, E0])
        ecap = sb("ecap", [P, E0 + 1])
        eid = sb("eid", [P, E0 + 1])
        zeros = sb("zeros", [P, C])
        xin = sb("xin", [P, G, C])
        ctxin = sb("ctxin", [P, G, C])
        x = sb("xres", [P, G, C])
        h = sb("h", [P, G, C])
        h2 = sb("h2", [P, G, C])
        hx = sb("hx", [P, G, C])
        rows_out = sb("rows_out", [P, G, C])
        hT = sb("hT", [P, G, P])
        ctxT = sb("ctxT", [P, G, P])
        qk = sb("qk", [P, G, 2, P])
        big = sb("big", [P, G, 2048])
        vb16 = sb("vb16", [P, G, 2, 8, 18])
        vb8 = sb("vb8", [P, G, 2, 4, 34])
        o = sb("o", [P, G, C])
        oT = sb("oT", [P, G, P])
        st6 = sb("st6", [P, G, 6])
        mv = sb("mv", [P, G, 2])
        veps = sb("veps", [P, G])
        rstd = sb("rstd", [P, G])
        rmax = sb("rmax", [P, G, 16])
        rsum = sb("rsum", [P, G, 16])
        rinv = sb("rinv", [P, G, 16])
        lg = sb("lg", [P, G, E0])
        lr = sb("lr", [P, G, E0])
        key = sb("key", [P, G, E0])
        sel = [sb("sel1", [P, G, E0]), sb("sel2", [P, G, E0])]
        chosen = sb("chosen", [P, G, E0], BF16)
        taken = sb("taken", [P, E0])
        taken_bf = sb("taken_bf", [P, E0], BF16)
        top = sb("top", [P, G, K0])
        first = sb("first", [P, G, 1])
        e2 = sb("e2", [P, G])
        w12 = sb("w12", [P, G, K0])
        row = sb("row", [P, G, E0])
        row12 = sb("row12", [P, G, K0])
        row_idx = sb("row_idx", [P, G, K0], U32)
        w_t = sb("w_t", [P, G, K0])
        w_all = sb("w_all", [P, NT, K0])
        row_all = sb("row_all", [P, NT, K0])
        pos_idx = sb("pos_idx", [P, NT, K0], U32)
        cnt = sb("cnt", [P, E0])
        cnt_i = sb("cnt_i", [P, E0], I32)
        nblk = sb("nblk", [P, E0])
        cblk = sb("cblk", [P, E0 + 1])
        delta = sb("delta", [P, E0 + 1])
        ddelta = sb("ddelta", [P, E0])
        slot_f = sb("slot_f", [P, NS0, 3])
        slot_i = sb("slot_i", [P, NS0, 2], I32)
        qkv = sb("qkv", [P, 3, N])
        qkvq = sb("qkvq", [P, G, 3, P])
        bias = sb("bias", [P, 16, T])
        stats = sb("stats", [P, 8])
        gstats = sb("gstats", [P, 8])
        qstep = sb("qstep", [P, 4])
        qinv = sb("qinv", [P, 4])
        qzero = sb("qzero", [P, 4])
        qmagic = sb("qmagic", [P, 4])
        qhigh = sb("qhigh", [P, 4])
        magic = sb("magic", [P, 1])
        sS = sb("sS", [P, 1])

        bank = [ctx.enter_context(nc.psum_tensor(f"bank{i}", [P, 512], F32)) for i in range(2 * G)]

        def lo(t):
            return bank[2 * t]

        def hi(t):
            return bank[2 * t + 1]

        expert_w = qkv[:, :, :].rearrange("p i n -> p (i n)").rearrange("p (g n) -> p g n", g=G)
        rel = big[0:NF, 0:2, :].rearrange("p g n -> p (g n)")
        posn = big[0:NF, 2, 0:T]

        block = ctx.enter_context(nc.Block())

        def P_(t):
            return big[:, t, 0:1024]

        def PT(t):
            return big[:, t, 1024:2048]

        def tile_of(dram, r, t):
            return dram.rearrange("(r g p) c -> r g p c", g=G, p=P)[r, t]

        def rows_at(dram, row_, n=P):
            return dram[bass.ds(row_, n), :]

        moe = {
            PH_M0: dict(w1=w["f0_w1"][:, :], w2=w["f0_w2"][:, :, :].rearrange("p c n -> p (c n)"), E=E0, F=F0,
                        up=F0, rows=a["_rows0"], out=a["_out0"], ns=NS0, scale=w["f0_g2"], shift=None),
            PH_M1: dict(w1=w["f1_wv13"][:, :, :].rearrange("p e n -> p (e n)"),
                        w2=w["f1_w2"][:, :, :].rearrange("p c n -> p (c n)"), E=E1, F=F1,
                        up=2 * F1, rows=a["_rows1"], out=a["_out1"], ns=NS1, scale=w["f1_g2"], shift=w["f1_b2"]),
        }
        routed = {PH_A: (moe[PH_M0], E0, K0), PH_C: (moe[PH_M1], E1, K1)}

        att = {
            (PH_A, 0): dict(q=w["a0_wqkv"][:, 0:128], k=w["a0_wqkv"][:, 128:256], v=w["a0_wqkv"][:, 256:384],
                            bq=w["a0_bq"], bk=w["a0_bk"], bv=w["a0_bv"], o=w["a0_wout"], kv=hT,
                            norm=(w["a0_g"], w["a0_b"]), heads=16, causal=False, ln=1),
            (PH_A, 1): dict(q=w["x0_wq"][:, :], k=w["x0_wk"][:, :], v=w["x0_wv"][:, :],
                            bq=w["x0_bq"], bk=w["x0_bk"], bv=w["x0_bv"], o=w["x0_wo"], kv=ctxT,
                            norm=(None, None), heads=16, causal=False, ln=2),
            (PH_A, 2): dict(q=w["f0_wqkv"][:, 0:128], k=w["f0_wqkv"][:, 128:256], v=w["f0_wqkv"][:, 256:384],
                            bq=None, bk=None, bv=None, o=w["f0_wo"], kv=hT,
                            norm=(w["f0_g1"], None), heads=16, causal=True, ln=4),
            (PH_B, 0): dict(heads=16, causal=False),
            (PH_C, 0): dict(q=w["x1_wq"][:, :], k=w["x1_wk"][:, :], v=w["x1_wv"][:, :],
                            bq=None, bk=None, bv=None, kv=ctxT, norm=(None, None), heads=8, causal=False, ln=0),
            (PH_C, 1): dict(o=w["f1_wo"], bv=None, norm=(w["f1_g1"], w["f1_b1"]), heads=16, causal=True, ln=2),
        }

        def vblocks(t, heads):
            return (vb16 if heads == 16 else vb8)[:, t]

        def spread_of(t, k, heads, h0, h1):
            n = h1 - h0
            dst = big[:, t, 0:heads * P].rearrange("p (b h k) -> p b h k", b=2, h=heads)[:, :, h0:h1]
            kk = k.rearrange("p (b k) -> p b k", b=2).unsqueeze(2).broadcast_to([P, 2, n, T])
            blk = (blk16 if heads == 16 else blk8)[:, h0:h1].unsqueeze(1).unsqueeze(3).broadcast_to([P, 2, n, T])
            return dst, kk, blk

        def phase_over(engine, phase):
            last = {PH_A: "stored", PH_M0: "slot_out", PH_Q: "stored", PH_B: "o", PH_C: "stored",
                    PH_M1: "slot_out", PH_O: "stored"}[phase]
            for t in range(G):
                engine.wait_ge(S[last][t], total(last, phase))
                if phase == PH_Q:
                    engine.wait_ge(S["rope"][t], total("rope", PH_Q))
                    engine.wait_ge(S["rows_T"][t], total("rows_T", PH_Q))

        @block.sync
        def _(sp):
            def weights(names, done):
                for n in names:
                    sp.dma_start(w[n][:], a[n]).then_inc(done, 16)

            weights(attn0, w_attn0)

            def tiles(phase, src, dst):
                at_last = {PH_A: ("pool_x", 3, None), PH_Q: ("x_added", K0 - 1, None), PH_C: ("pool_x", 0, None),
                           PH_O: ("x_added", 0, None)}[phase]

                def stage(name, use, t, r):
                    at = counter(phase, r)
                    if name == "load":
                        if not (isinstance(r, int) and r == 0):
                            used = counter(phase, r - 1)
                            if phase in (PH_A, PH_C):
                                sp.wait_ge(S["ctx_ps"][t], used("ctx_ps"))
                            if phase == PH_A:
                                sp.wait_ge(S["pool_x"][t], used("pool_x", 0))
                            else:
                                sp.wait_ge(S["x_added"][t], used("x_added", 0))
                        sp.dma_start(xin[:, t], tile_of(src, r, t)).then_inc(S["loaded"][t], 16)
                        if phase in (PH_A, PH_C):
                            sp.dma_start(ctxin[:, t], tile_of(a["ctx"], r, t)).then_inc(S["loaded"][t], 16)
                        if phase == PH_A and t == G - 1 and isinstance(r, int) and r == 0:
                            weights(moe0, w_moe0)
                            weights(layer1, w_layer1)
                    if name == "store":
                        sp.wait_ge(S[at_last[0]][t], at(*at_last))
                        sp.dma_start(tile_of(dst, r, t), x[:, t]).then_inc(S["stored"][t], 16)

                run(sp, "sp", phase, stage)

            def slots(phase, zeros_before):
                m = moe[phase]
                sp.wait_ge(table, TABLE[phase])
                sp.dma_start(rows_at(m["rows"], m["E"] * CAP), zeros[:, :]).then_inc(zero_rows, 16)
                for e in range(m["E"]):
                    n = sp.value_load(cnt_i[0:1, e:e + 1], min_val=0, max_val=N)
                    sp.dma_start(rows_at(m["rows"], n + e * CAP), zeros[:, :]).then_inc(zero_rows, 16)
                sp.wait_ge(zero_rows, zeros_before + 16 * (m["E"] + 1))
                sp.wait_ge(scattered, 16 * NT * (K0 if phase == PH_M0 else K0 + K1))

                def stage(name, use, t, r):
                    at = counter(phase, r)
                    if name == "load":
                        first = sp.value_load(slot_i[0:1, bass.ds(r * G + t, 1), 0], min_val=0, max_val=m["E"] * CAP)
                        if not (isinstance(r, int) and r == 0):
                            sp.wait_ge(S["slot_ps"][t], counter(phase, r - 1)("slot_ps", 0, "rows"))
                        sp.dma_start(h[:, t], rows_at(m["rows"], first)).then_inc(S["slot_in"][t], 16)
                    if name == "store":
                        sp.wait_ge(S["slot_y"][t], at("slot_y", 0, "y"))
                        sp.dma_start(rows_at(m["out"], r * (G * P) + t * P), o[:, t]).then_inc(S["slot_out"][t], 16)

                run(sp, "sp", phase, stage)

            tiles(PH_A, a["x"], a["_mid"])
            slots(PH_M0, 0)
            tiles(PH_Q, a["_mid"], a["_mid2"])
            phase_over(sp, PH_B)
            tiles(PH_C, a["_mid2"], a["_mid"])
            slots(PH_M1, 16 * (E0 + 1))
            tiles(PH_O, a["_mid"], out)
            phase_over(sp, PH_O)

        @block.gpsimd
        def _(pool):
            step = [0]

            def link(ins):
                step[0] += 1
                ins.then_inc(const_step, 1)
                pool.wait_ge(const_step, step[0])

            def keep(dst, compare, fill, base, pattern, per_partition):
                link(nc.gpsimd.affine_select(out=dst, in_=dst, compare_op=compare, fill=fill, base=base,
                                             pattern=pattern, channel_multiplier=per_partition))

            link(nc.gpsimd.memset(ident[:, :], 0.0))
            keep(ident[:, :], ALU.not_equal, 1.0, 0, [[-1, P]], 1)
            link(nc.gpsimd.tensor_copy(ident_bf[:, :], ident[:, :]))
            link(nc.gpsimd.memset(ones_bf[:, :], 1.0))
            link(nc.gpsimd.memset(before_bf[:, :], 1.0))
            keep(before_bf[:, :], ALU.is_ge, 0.0, -1, [[1, P]], -1)
            link(nc.gpsimd.memset(causal[:, :], 0.0))
            for half in (0, 64):
                keep(causal[half:half + 64, :], ALU.is_ge, NEG, 0, [[-1, T]], 1)
            link(nc.gpsimd.tensor_copy(causal_bf[:, :], causal[:, :]))
            for blk, heads in ((blk16, 16), (blk8, 8)):
                D = C // heads
                link(nc.gpsimd.memset(blk[:, :], 1.0))
                keep(blk[:, :], ALU.is_ge, 0.0, 0, [[-D, heads]], 1)
                keep(blk[:, :], ALU.is_ge, 0.0, D - 1, [[D, heads]], -1)
            link(nc.gpsimd.memset(minus_half[:, :], -0.5))
            link(nc.gpsimd.memset(eps[:, :], EPS))
            link(nc.gpsimd.memset(magic[:, :], MAGIC))
            link(nc.gpsimd.memset(zeros[:, :], 0.0))
            link(nc.gpsimd.memset(taken[:, :], 0.0))
            link(nc.gpsimd.memset(taken_bf[:, :], 0.0))
            for dst, step_, base, n in ((first8, -1, E0, E0), (ecap, CAP, 0, E0 + 1), (eid, 1, 0, E0 + 1)):
                link(nc.gpsimd.iota(dst[:, :], pattern=[[step_, n]], base=base, channel_multiplier=0,
                                    allow_small_or_imprecise_dtypes=True))
            link(nc.gpsimd.iota(slot_f[:, :, 2], pattern=[[1, NS0]], base=0, channel_multiplier=0,
                                allow_small_or_imprecise_dtypes=True))
            link(nc.gpsimd.memset(vb16[:, :, :, :, :], 0.0))
            link(nc.gpsimd.memset(vb8[:, :, :, :, :], 0.0))
            for half in (0, 1):
                for vb, D in ((vb16, 8), (vb8, 16)):
                    col = half * (D + 1) + D
                    for t in range(G):
                        link(nc.gpsimd.memset(vb[64 * half:64 * half + 64, t, :, :, col:col + 1], 1.0))
            nc.gpsimd.memset(unused_pool[:, :], 0.0).then_inc(const_ready, 1)

            def norm_rstd(at, use, t):
                pool.wait_ge(S["veps"][t], at("veps", use))
                nc.gpsimd.tensor_tensor(rstd[:, t:t + 1], veps[:, t:t + 1], minus_half[:, :], ALU.pow)\
                    .then_inc(S["rstd"][t], 1)

            def spread(phase, at, use, t):
                heads = att[phase, use]["heads"]
                k = qkvq[:, t, 1] if phase == PH_B else qk[:, t, 1]
                if phase == PH_B:
                    pool.wait_ge(S["quant"][t], at("quant", 1, "c"))
                elif (phase, use) == (PH_C, 1):
                    pool.wait_ge(S["rope"][t], at("rope", 0, "done"))
                else:
                    pool.wait_ge(S["qk"][t], at("qk", use))
                mine = heads if phase == PH_B else heads - VECTOR_HEADS[phase, use]
                nc.gpsimd.tensor_tensor(*spread_of(t, k, heads, 0, mine), ALU.mult).then_inc(S["kblk"][t], 1)

            def hold(t):
                nc.gpsimd.tensor_tensor(unused_pool[:, t:t + 1], eps[:, :], eps[:, :], ALU.add)

            def add(t, dst, in0, in1):
                nc.gpsimd.tensor_tensor(dst[:, t], in0, in1, ALU.add).then_inc(S["pool_x"][t], 1)

            def attentions(phase):
                m, E, K = routed[phase]

                def stage(name, use, t, r):
                    at = counter(phase, r)
                    if name == "stats":
                        norm_rstd(at, use, t)
                        if use == (5 if phase == PH_A else 3):
                            pool.wait_ge(S["x_added"][t], at("x_added", 2))
                            add(t, x, x[:, t], h[:, t])
                    if name == "norm" and phase == PH_A and use == 1:
                        if not (isinstance(r, int) and r == 0):
                            pool.wait_ge(S["stored"][t], counter(phase, r - 1)("stored"))
                        pool.wait_ge(S["ln"][t], at("ln", 0, "done"))
                        add(t, x, xin[:, t], h[:, t])
                        pool.wait_ge(S["pool_x"][t], at("pool_x", 0))
                        add(t, x, x[:, t], w["a0_bout"][:, :])
                    if name == "norm" and phase == PH_A and use == 2:
                        pool.wait_ge(S["ln"][t], at("ln", 2, "done"))
                        add(t, x, x[:, t], w["x0_bo"][:, :])
                    if name == "spread":
                        spread(phase, at, use, t)
                    if name == "scatter":
                        pool.wait_ge(route, route_at(phase, r, ROUTE[phase] - 1))
                        pool.wait_ge(collected, r + (R + 1 if phase == PH_C else 1))
                        hold(use)
                        for s_ in range(K):
                            pool.indirect_dma_start(
                                m["rows"], bass.IndirectOffsetOnAxis(ap=row_idx[:, use, s_:s_ + 1], axis=0),
                                rows_out[:, use], None).then_inc(scattered, 16)

                run(pool, "pool", phase, stage)

            def gather(phase, m, K):
                def stage(name, use, t, r):
                    if name == "load":
                        if not (isinstance(r, int) and r == 0):
                            pool.wait_ge(S["x_added"][t], counter(phase, r - 1)("x_added", K - 1))
                            hold(G + t)
                        nc.gpsimd.tensor_copy(row_idx[:, t, 0:K], pos_idx[:, bass.ds(r * G + t, 1), 0:K]
                                              .rearrange("p a k -> p (a k)")).then_inc(S["pool_x"][t], 1)
                        pool.wait_ge(S["pool_x"][t], counter(phase, r)("pool_x"))
                        hold(2 * G + t)
                        for s_ in range(K):
                            pool.indirect_dma_start(
                                big[:, t, s_ * C:(s_ + 1) * C], None, m["out"],
                                bass.IndirectOffsetOnAxis(ap=row_idx[:, t, s_:s_ + 1], axis=0))\
                                .then_inc(S["gathered"][t], 16)
                    if name == "stats":
                        norm_rstd(counter(phase, r), 0, t)

                pool.wait_ge(table, TABLE_POS[phase])
                phase_over(pool, PH_M0 if phase == PH_Q else PH_M1)
                run(pool, "pool", phase, stage)

            attentions(PH_A)
            gather(PH_Q, moe[PH_M0], K0)
            phase_over(pool, PH_Q)
            nc.gpsimd.iota(rel[:, :].rearrange("p (i j) -> p i j", j=T), pattern=[[1, T], [-1, T]],
                           base=0, channel_multiplier=0, allow_small_or_imprecise_dtypes=True)
            nc.gpsimd.iota(posn, pattern=[[1, T]], base=0, channel_multiplier=0,
                           allow_small_or_imprecise_dtypes=True).then_inc(const_ready, 1)
            pool.wait_ge(fire_act, 5)
            pool.wait_ge(fire_dve, 3)
            rel3 = rel.rearrange("p (i j) -> p i j", j=T)
            nc.gpsimd.tensor_tensor(rel3, rel3, posn.unsqueeze(2).broadcast_to([NF, T, T]), ALU.mult)\
                .then_inc(fire_pool, 1)
            pool.wait_ge(stat_dve, 7)
            nc.gpsimd.partition_all_reduce(gstats[:, 0:6], stats[:, 0:6], P, bass.bass_isa.ReduceOp.max)\
                .then_inc(stat_all, 1)

            def stage_b(name, use, t, r):
                at = counter(PH_B, r)
                if name == "spread":
                    spread(PH_B, at, use, t)
                if name in ("shift0", "shift1"):
                    n = int(name[-1])
                    pool.wait_ge(S["shift"][t], at("shift", 0, f"max{n}"))
                    pv = P_(t)[:, n * 512:(n + 1) * 512].rearrange("p (h k) -> p h k", k=T)
                    nc.gpsimd.tensor_tensor(pv, pv, rmax[:, t, 8 * n:8 * n + 8].unsqueeze(2).broadcast_to([P, 8, T]),
                                            ALU.subtract)\
                        .then_inc(S["pool_x"][t], 1)

            run(pool, "pool", PH_B, stage_b)
            pool.wait_ge(stat_dve, STAT_Y)
            nc.gpsimd.partition_all_reduce(gstats[:, 6:8], stats[:, 6:8], P, bass.bass_isa.ReduceOp.max)\
                .then_inc(stat_all, 1)
            attentions(PH_C)
            gather(PH_O, moe[PH_M1], K1)

        @block.scalar
        def _(act):
            act.wait_ge(w_attn0, 16 * len(attn0))
            act.wait_ge(const_ready, 1)
            def evict_rows(at, use, t, scale, shift, dst=hT):
                act.wait_ge(S["rows_ps"][t], at("rows_ps", use))
                if scale is None:
                    ins = nc.scalar.activation(dst[:, t], hi(t)[:, 0:P], ACT.Copy)
                else:
                    ins = nc.scalar.activation(dst[:, t], hi(t)[:, 0:P], ACT.Identity, scale=scale[:, :],
                                               bias=0.0 if shift is None else shift[:, :])
                ins.then_inc(S["rows_T"][t], 1)

            def norm_eps(at, use, t):
                act.wait_ge(S["ln"][t], at("ln", use, "mean"))
                nc.scalar.activation(veps[:, t:t + 1], mv[:, t, 1:2], ACT.Identity, bias=eps[:, :])\
                    .then_inc(S["veps"][t], 1)

            def collect(phase, r):
                for lane in range(G):
                    act.wait_ge(S["ln"][lane], counter(phase, r)("ln", 5 if phase == PH_A else 3, "done"))
                if phase == PH_C:
                    act.wait_ge(scattered, r * (16 * G * K1) + 16 * NT * K0)
                elif not (isinstance(r, int) and r == 0):
                    act.wait_ge(scattered, r * (16 * G * K0))
                nc.scalar.activation(rows_out[:, :, :], hx[:, :, :], ACT.Copy).then_inc(collected, 1)

            def attention_stage(phase, name, use, t, at, rows_use):
                aw = att[phase, use]
                heads = aw["heads"]
                half = heads * 32
                quantised = phase == PH_B
                roped = (phase, use) == (PH_C, 1)
                if name == "rows":
                    if aw["kv"] is ctxT:
                        act.wait_ge(S["ctx_ps"][t], at("ctx_ps"))
                        nc.scalar.activation(ctxT[:, t], lo(t)[:, 0:P], ACT.Copy).then_inc(S["ctx_T"][t], 1)
                    evict_rows(at, rows_use, t, *aw["norm"])
                if name == "project" and not roped:
                    act.wait_ge(S["att_ps"][t], at("att_ps", use, "proj"))
                    for i, b_ in ((0, aw["bq"]), (1, aw["bk"])):
                        if b_ is None:
                            ins = nc.scalar.activation(qk[:, t, i], lo(t)[:, i * P:(i + 1) * P], ACT.Copy)
                        else:
                            ins = nc.scalar.activation(qk[:, t, i], lo(t)[:, i * P:(i + 1) * P],
                                                       ACT.Identity, bias=b_[:, :])
                    ins.then_inc(S["qk"][t], 1)
                n = name[-1]
                mine = slice(half * (n == "1"), half * (n == "1") + half)
                if name in ("softmax0", "softmax1"):
                    if quantised:
                        act.wait_ge(S["pool_x"][t], at("pool_x", 0, n))
                    else:
                        act.wait_ge(S["shift"][t], at("shift", use, "shifted" + n))
                    nc.scalar.activation(P_(t)[:, mine], P_(t)[:, mine], ACT.Exp,
                                         scale=1.0 if quantised else float(C // heads) ** -0.5)\
                        .then_inc(S["probs"][t], 1)
                if name in ("normalise0", "normalise1"):
                    act.wait_ge(S["soft"][t], at("soft", 0, "normed" + n))
                    nc.scalar.activation(P_(t)[:, mine], P_(t)[:, mine], ACT.Copy, bias=MAGIC)\
                        .then_inc(S["rounded"][t], 1)
                if name in ("turn0", "turn1"):
                    act.wait_ge(S["att_ps"][t], at("att_ps", use, "pT" + n))
                    nc.scalar.activation(PT(t)[:, mine], (lo if n == "0" else hi)(t)[:, 0:half], ACT.Copy,
                                         bias=-MAGIC if quantised else 0.0).then_inc(S["pT"][t], 1)
                if name == "turn_o":
                    act.wait_ge(S["out_ps"][t], at("out_ps", use, "oT"))
                    nc.scalar.activation(oT[:, t], hi(t)[:, 0:P], ACT.Copy).then_inc(S["oT"][t], 1)

            def stage_a(name, use, t, r):
                at = counter(PH_A, r)
                if (PH_A, use) in att:
                    attention_stage(PH_A, name, use, t, at, use)
                if name == "stats":
                    norm_eps(at, use, t)
                if name == "router_rows":
                    evict_rows(at, 3, t, w["f0_g2"], None)
                if name == "collect":
                    collect(PH_A, r)
                if name == "ranks":
                    act.wait_ge(route, route_at(PH_A, r, 6))
                    nc.scalar.activation(e2[:, :], top[:, :, 1], ACT.Exp).then_inc(route_exp, 1)

            def slots(phase):
                m = moe[phase]

                def stage(name, use, t, r):
                    at = counter(phase, r)
                    if name == "rows":
                        act.wait_ge(S["slot_ps"][t], at("slot_ps", 0, "rows"))
                        nc.scalar.activation(hT[:, t], hi(t)[:, 0:P], ACT.Identity, scale=m["scale"][:, :],
                                             bias=0.0 if m["shift"] is None else m["shift"][:, :])\
                            .then_inc(S["slot_act"][t], 1)
                    if name == "up":
                        act.wait_ge(S["slot_ps"][t], at("slot_ps", 0, "up"))
                        nc.scalar.activation(big[:, t, 0:m["F"]], lo(t)[:, 0:m["F"]],
                                             ACT.Gelu if phase == PH_M0 else ACT.Silu).then_inc(S["slot_act"][t], 1)
                    if name == "hid":
                        act.wait_ge(S["slot_ps"][t], at("slot_ps", 0, "hid"))
                        nc.scalar.activation(big[:, t, 1024:1024 + m["F"]], lo(t)[:, 0:m["F"]], ACT.Copy)\
                            .then_inc(S["slot_act"][t], 1)

                run(act, "act", phase, stage)

            def stage_q(name, use, t, r):
                at = counter(PH_Q, r)
                if name == "stats":
                    norm_eps(at, 0, t)
                if name == "rows":
                    evict_rows(at, 0, t, None, None)
                if name == "project":
                    act.wait_ge(S["att_ps"][t], at("att_ps", 0, "proj"))
                    nc.scalar.activation(qkv[:, 2, bass.ds(r * (G * P) + t * P, P)], hi(t)[:, 0:P], ACT.Copy)\
                        .then_inc(S["rows_T"][t], 1)

            def stage_b(name, use, t, r):
                at = counter(PH_B, r)
                if name == "quantise":
                    for i in range(3):
                        nc.scalar.activation(qkvq[:, t, i], qkv[:, i, bass.ds(r * (G * P) + t * P, P)], ACT.Identity,
                                             scale=qinv[:, i:i + 1], bias=magic[:, :]).then_inc(S["quant"][t], 1)
                if name == "centre":
                    act.wait_ge(S["quant"][t], at("quant", 2, "b"))
                    for i in range(3):
                        nc.scalar.activation(qkvq[:, t, i], qkvq[:, t, i], ACT.Copy, bias=-MAGIC)\
                            .then_inc(S["quant"][t], 1)
                if name == "values":
                    act.wait_ge(S["att_ps"][t], at("att_ps", 0, "proj"))
                    for odd in range(2):
                        half = slice(64 * odd, 64 * odd + 64)
                        ins = nc.scalar.activation(
                            vblocks(t, 16)[half, :, :, 9 * odd:9 * odd + 8],
                            hi(t)[half, 2 * P:3 * P].rearrange("p (b j d) -> p b j d", b=2, d=8), ACT.Copy)
                    ins.then_inc(S["v"][t], 1)
                attention_stage(PH_B, name, use, t, at, None)

            def stage_c(name, use, t, r):
                at = counter(PH_C, r)
                if name == "y_rows":
                    evict_rows(at, 0, t, None, None)
                if (PH_C, use) in att:
                    attention_stage(PH_C, name, use, t, at, 1)
                if name == "stats":
                    norm_eps(at, use, t)
                if name == "conv_rows":
                    evict_rows(at, 2, t, *att[PH_C, 1]["norm"], dst=oT)
                if name == "router_rows":
                    evict_rows(at, 3, t, w["f1_g2"], w["f1_b2"])
                if name == "collect":
                    collect(PH_C, r)

            run(act, "act", PH_A, stage_a)
            slots(PH_M0)
            run(act, "act", PH_Q, stage_q)
            act.wait_ge(const_ready, 2)
            nc.scalar.activation(w["fire_L"][:, :], w["fire_L"][:, :], ACT.Abs).then_inc(fire_act, 1)
            act.wait_ge(fire_dve, 1)
            nc.scalar.activation(posn, posn, ACT.Abs, scale=w["fire_c"][:, :]).then_inc(fire_act, 1)
            act.wait_ge(fire_act, 2)
            nc.scalar.activation(posn, posn, ACT.Ln, bias=1.0).then_inc(fire_act, 1)
            nc.scalar.activation(rel, rel, ACT.Abs, scale=w["fire_c"][:, :]).then_inc(fire_act, 1)
            act.wait_ge(fire_act, 4)
            nc.scalar.activation(rel, rel, ACT.Ln, bias=1.0).then_inc(fire_act, 1)
            act.wait_ge(fire_pool, 1)
            nc.scalar.activation(rel, rel, ACT.Relu, bias=w["fire_b1"][:, :], scale=w["fire_w1"][:, :])\
                .then_inc(fire_act, 1)
            act.wait_ge(stat_dve, STAT_Y - 3)
            run(act, "act", PH_B, stage_b)
            act.wait_ge(w_layer1, 16 * len(layer1))
            run(act, "act", PH_C, stage_c)
            slots(PH_M1)

        @block.tensor
        def _(pe):
            pe.wait_ge(w_attn0, 16 * len(attn0))
            pe.wait_ge(const_ready, 1)
            def transpose_rows(at, use, t, src):
                nc.tensor.transpose(hi(t)[:, 0:P], src[:, t], ident[:, :]).then_inc(S["rows_ps"][t], 1)

            def values(t, dst, wv, kvsrc, heads):
                wv2 = wv.rearrange("p (j two d) -> p two j d", two=2, d=C // heads)
                for b in range(2):
                    for odd in range(2):
                        last = nc.tensor.matmul(dst[64 * odd:64 * odd + 64, 64 * b:64 * b + 64],
                                                kvsrc[:, 64 * b:64 * b + 64], wv2[:, odd], start=True, stop=True)
                return last

            def attention_stage(phase, name, use, t, at, rows_use):
                aw = att[phase, use]
                heads = aw["heads"]
                half = heads * 32
                pairs = heads // 2
                roped = (phase, use) == (PH_C, 1)
                if name == "rows":
                    if aw["kv"] is ctxT:
                        pe.wait_ge(S["x_added"][t], at("x_added", 0))
                        pe.wait_ge(S["loaded"][t], at("loaded", 1))
                        nc.tensor.transpose(lo(t)[:, 0:P], ctxin[:, t], ident[:, :]).then_inc(S["ctx_ps"][t], 1)
                    pe.wait_ge(S["ln"][t], at("ln", aw["ln"], "done"))
                    transpose_rows(at, rows_use, t, h2)
                if name == "project" and not roped:
                    if aw["kv"] is ctxT:
                        pe.wait_ge(S["ctx_T"][t], at("ctx_T"))
                    pe.wait_ge(S["rows_T"][t], at("rows_T", rows_use))
                    kv = aw["kv"][:, t]
                    nc.tensor.matmul(lo(t)[:, 0:P], aw["q"], hT[:, t], start=True, stop=True)
                    nc.tensor.matmul(lo(t)[:, P:2 * P], aw["k"], kv, start=True, stop=True)
                    values(t, hi(t)[:, 2 * P:3 * P], aw["v"], kv, heads).then_inc(S["att_ps"][t], 1)
                if name in ("scores0", "scores1"):
                    n = int(name[-1])
                    q = qkvq[:, t, 0] if phase == PH_B else qk[:, t, 0]
                    pe.wait_ge(S["kblk"][t], at("kblk", use))
                    pe.wait_ge(S["v"][t], at("v", use, "v" if phase == PH_B else "spread"))
                    kb = big[:, t, 0:heads * P].rearrange("p (b n) -> p b n", b=2)
                    if aw["causal"]:
                        nc.tensor.matmul(bank[2 * t + n][:, 0:half], ident_bf[:, :],
                                         causal_bf[:, :].unsqueeze(1).broadcast_to([P, heads // 2, T]),
                                         start=True, stop=False, skip_group_check=True)
                    for b in range(2):
                        last = nc.tensor.matmul(bank[2 * t + n][64 * b:64 * b + 64, 0:half],
                                                q[:, 64 * b:64 * b + 64], kb[:, b, n * half:(n + 1) * half],
                                                start=not aw["causal"], stop=True,
                                                skip_group_check=aw["causal"])
                    last.then_inc(S["att_ps"][t], 1)
                if name in ("turn0", "turn1"):
                    n = int(name[-1])
                    if phase == PH_B:
                        pe.wait_ge(S["rounded"][t], at("rounded", 0, str(n)))
                    else:
                        pe.wait_ge(S["probs"][t], at("probs", use, str(n)))
                    for c in range(pairs // 2):
                        j = n * (pairs // 2) + c
                        last = nc.tensor.transpose(bank[2 * t + n][:, c * P:(c + 1) * P],
                                                   P_(t)[:, j * P:(j + 1) * P], ident[:, :])
                    last.then_inc(S["att_ps"][t], 1)
                if name == "weigh":
                    pe.wait_ge(S["pT"][t], at("pT", use, "1"))
                    W = 2 * (C // heads + 1)
                    vb = vblocks(t, heads)
                    for j in range(pairs):
                        for b in range(2):
                            last = nc.tensor.matmul(lo(t)[64 * b:64 * b + 64, j * W:(j + 1) * W],
                                                    PT(t)[:, j * P + 64 * b:j * P + 64 * b + 64], vb[:, b, j],
                                                    start=True, stop=True)
                    last.then_inc(S["att_ps"][t], 1)
                if name == "turn_o":
                    pe.wait_ge(S["o"][t], at("o", use, "done"))
                    nc.tensor.transpose(hi(t)[:, 0:P], o[:, t], ident[:, :]).then_inc(S["out_ps"][t], 1)
                if name == "output":
                    pe.wait_ge(S["oT"][t], at("oT", use if phase == PH_A else 0))
                    nc.tensor.matmul(hi(t)[:, P:2 * P], oT[:, t], aw["o"][:, :], start=True, stop=True)\
                        .then_inc(S["out_ps"][t], 1)

            def router(phase, name, at, t, wr, ln_use):
                if name == "router_rows":
                    pe.wait_ge(S["ln"][t], at("ln", ln_use, "done"))
                    transpose_rows(at, 3, t, hx)
                if name == "router":
                    pe.wait_ge(S["rows_T"][t], at("rows_T", 3))
                    nc.tensor.matmul(lo(t)[:, 0:routed[phase][1]], hT[:, t], wr, start=True, stop=True)\
                        .then_inc(S["logit_ps"][t], 1)

            def ranks(phase, r):
                E = routed[phase][1]
                pe.wait_ge(route, route_at(phase, r, CHOSEN[phase]))
                for lane in range(G):
                    dst = lo(G - 1)[:, lane * E:(lane + 1) * E]
                    nc.tensor.matmul(dst, before_bf[:, :], chosen[:, lane, 0:E], start=True, stop=False)
                    for b in range(lane):
                        nc.tensor.matmul(dst, ones_bf[:, :], chosen[:, b, 0:E], start=False, stop=False)
                    last = nc.tensor.matmul(dst, ones_bf[:, :], taken_bf[:, 0:E], start=False, stop=True)
                last.then_inc(rank_ps, 1)

            def stage_a(name, use, t, r):
                at = counter(PH_A, r)
                if (PH_A, use) in att:
                    attention_stage(PH_A, name, use, t, at, use)
                router(PH_A, name, at, t, w["f0_wr"][:, :], 5)
                if name == "ranks":
                    ranks(PH_A, r)
                if name == "ranked":
                    pe.wait_ge(route, route_at(PH_A, r, RANKED[PH_A]))

            def counts(phase):
                pe.wait_ge(route, route_at(phase, R - 1, ROUTE[phase] - 1))
                nc.tensor.matmul(lo(0)[:, 0:routed[phase][1]], ones_bf[:, :], taken_bf[:, 0:routed[phase][1]],
                                 start=True, stop=True).then_inc(count_ps, 1)

            def slots(phase):
                m = moe[phase]
                F, up = m["F"], m["up"]
                pe.wait_ge(table, TABLE[phase])

                def stage(name, use, t, r):
                    at = counter(phase, r)
                    if name == "rows":
                        pe.wait_ge(S["slot_in"][t], at("slot_in"))
                        if not (isinstance(r, int) and r == 0):
                            pe.wait_ge(S["slot_y"][t], counter(phase, r - 1)("slot_y", 0, "y"))
                        nc.tensor.transpose(hi(t)[:, 0:P], h[:, t], ident[:, :]).then_inc(S["slot_ps"][t], 1)
                    if name == "up":
                        pe.wait_ge(S["slot_y"][t], at("slot_y", 0, "weights"))
                        pe.wait_ge(S["slot_act"][t], at("slot_act", 0, "rows"))
                        for i in range(up // min(up, 512)):
                            n = min(up, 512)
                            last = nc.tensor.matmul(bank[2 * t + i][:, 0:n], hT[:, t],
                                                    expert_w[:, t, i * n:(i + 1) * n], start=True, stop=True)
                        last.then_inc(S["slot_ps"][t], 1)
                    if name == "hid":
                        if phase == PH_M1:
                            pe.wait_ge(S["slot_y"][t], at("slot_y", 0, "hid"))
                        else:
                            pe.wait_ge(S["slot_act"][t], at("slot_act", 0, "act"))
                        for i in range(F // P):
                            last = nc.tensor.transpose(lo(t)[:, i * P:(i + 1) * P], big[:, t, i * P:(i + 1) * P],
                                                       ident[:, :])
                        last.then_inc(S["slot_ps"][t], 1)
                    if name == "down":
                        pe.wait_ge(S["slot_act"][t], at("slot_act", 0, "hid"))
                        for i in range(F // P):
                            last = nc.tensor.matmul(hi(t)[:, 0:C], big[:, t, 1024 + i * P:1024 + (i + 1) * P],
                                                    expert_w[:, t, up + i * P:up + (i + 1) * P],
                                                    start=(i == 0), stop=(i == F // P - 1))
                        last.then_inc(S["slot_ps"][t], 1)

                run(pe, "pe", phase, stage)

            def stage_q(name, use, t, r):
                at = counter(PH_Q, r)
                if name == "rows":
                    pe.wait_ge(S["ln"][t], at("ln", 0, "done"))
                    if not (isinstance(r, int) and r == 0):
                        pe.wait_ge(S["rows_T"][t], counter(PH_Q, r - 1)("rows_T", 1))
                    transpose_rows(at, 0, t, h2)
                if name == "project":
                    if not (isinstance(r, int) and r == 0):
                        pe.wait_ge(S["rope"][t], counter(PH_Q, r - 1)("rope", 0, "done"))
                    pe.wait_ge(S["rows_T"][t], at("rows_T", 0))
                    for i, n in enumerate(("a1_wq", "a1_wk", "a1_wqs", "a1_wks")):
                        nc.tensor.matmul(lo(t)[:, i * P:(i + 1) * P], w[n][:, :], hT[:, t], start=True, stop=True)
                    nc.tensor.matmul(hi(t)[:, 0:P], w["a1_wv"][:, :], hT[:, t], start=True, stop=True)\
                        .then_inc(S["att_ps"][t], 1)

            def stage_b(name, use, t, r):
                at = counter(PH_B, r)
                if name == "values":
                    pe.wait_ge(S["quant"][t], at("quant", 2, "c"))
                    values(t, hi(t)[:, 2 * P:3 * P], ident[:, :], qkvq[:, t, 2], 16).then_inc(S["att_ps"][t], 1)
                else:
                    attention_stage(PH_B, name, use, t, at, None)

            def stage_c(name, use, t, r):
                at = counter(PH_C, r)
                if name == "y_rows":
                    pe.wait_ge(S["quant"][t], at("quant", 0, "c"))
                    transpose_rows(at, 0, t, h2)
                if name == "y_out":
                    pe.wait_ge(S["rows_T"][t], at("rows_T", 0))
                    nc.tensor.matmul(hi(t)[:, P:2 * P], hT[:, t], w["a1_wo"][:, :], start=True, stop=True)\
                        .then_inc(S["out_ps"][t], 1)
                if (PH_C, use) in att:
                    attention_stage(PH_C, name, use, t, at, 1)
                if name == "conv_rows":
                    pe.wait_ge(S["ln"][t], at("ln", 2, "done"))
                    transpose_rows(at, 2, t, h2)
                if name == "project" and use == 1:
                    pe.wait_ge(S["conv"][t], at("conv", 2))
                    for i, n in enumerate(("f1_wq", "f1_wk", "f1_wqs", "f1_wks")):
                        nc.tensor.matmul(lo(t)[:, i * P:(i + 1) * P], w[n][:, :], hT[:, t], start=True, stop=True)
                    values(t, hi(t)[:, 2 * P:3 * P], w["f1_wv"][:, :], hT[:, t], 16).then_inc(S["att_ps"][t], 1)
                router(PH_C, name, at, t, w["f1_wr"][:, :], 3)
                if name == "ranks":
                    ranks(PH_C, r)
                if name == "ranked":
                    pe.wait_ge(route, route_at(PH_C, r, RANKED[PH_C]))

            run(pe, "pe", PH_A, stage_a)
            counts(PH_A)
            slots(PH_M0)
            pe.wait_ge(w_layer1, 16 * len(layer1))
            phase_over(pe, PH_M0)
            run(pe, "pe", PH_Q, stage_q)
            phase_over(pe, PH_Q)
            pe.wait_ge(fire_act, 6)
            fh = rel.rearrange("p (i j) -> p i j", j=T)
            for j in range(T):
                for half in (0, 64):
                    last = nc.tensor.matmul(bank[j // 32][half:half + 64, (j % 32) * 16:(j % 32) * 16 + 16],
                                            fh[:, :, j], w["fire_w2"][:, :], start=True, stop=True)
            last.then_inc(fire_pe, 1)
            pe.wait_ge(fire_dve, 4)
            run(pe, "pe", PH_B, stage_b)
            phase_over(pe, PH_B)
            run(pe, "pe", PH_C, stage_c)
            counts(PH_C)
            slots(PH_M1)

        @block.vector
        def _(v):
            v.wait_ge(w_attn0, 16 * len(attn0))
            v.wait_ge(const_ready, 1)
            layer_norms = {
                (PH_A, 0): (xin, h, ("loaded", 1, None)), (PH_A, 1): (h, h2, ("ln", 0, "done")),
                (PH_A, 2): (x, h2, ("x_added", 0, None)), (PH_A, 3): (x, h, ("x_added", 1, None)),
                (PH_A, 4): (h, h2, ("ln", 3, "done")), (PH_A, 5): (h, hx, ("x_added", 2, None)),
                (PH_Q, 0): (x, h2, ("x_added", K0 - 1, None)),
                (PH_C, 0): (x, h2, ("x_added", 0, None)), (PH_C, 1): (x, h, ("x_added", 1, None)),
                (PH_C, 2): (h, h2, ("ln", 1, "done")), (PH_C, 3): (h, hx, ("x_added", 2, None)),
            }

            def layer_norm(phase, name, use, t, r):
                at = counter(phase, r)
                src, dst, rows_there = layer_norms[phase, use]
                if name == "stats":
                    v.wait_ge(S[rows_there[0]][t], at(*rows_there))
                    nc.vector.bn_stats(st6[:, t], src[:, t]).then_inc(S["ln"][t], 1)
                    v.wait_ge(S["ln"][t], at("ln", use, "stats"))
                    nc.vector.memset(unused[:, t:t + 1], 0.0)
                    nc.vector.bn_aggr(mv[:, t], st6[:, t]).then_inc(S["ln"][t], 1)
                else:
                    if dst is hx and not (isinstance(r, int) and r == 0):
                        v.wait_ge(collected, r + R if phase == PH_C else r)
                    v.wait_ge(S["rstd"][t], at("rstd", use))
                    nc.vector.tensor_scalar(dst[:, t], src[:, t], mv[:, t, 0:1], rstd[:, t:t + 1],
                                            ALU.subtract, ALU.mult).then_inc(S["ln"][t], 1)

            def attention_stage(phase, name, use, t, at):
                aw = att[phase, use]
                heads = aw["heads"]
                D = C // heads
                hh = heads // 2
                if name == "project":
                    v.wait_ge(S["att_ps"][t], at("att_ps", use, "proj"))
                    bv = aw.get("bv")
                    for odd in range(2):
                        rows = slice(64 * odd, 64 * odd + 64)
                        dst = vblocks(t, heads)[rows, :, :, odd * (D + 1):odd * (D + 1) + D]
                        src = hi(t)[rows, 2 * P:3 * P].rearrange("p (b j d) -> p b j d", b=2, d=D)
                        if bv is None:
                            last = nc.vector.tensor_copy(dst, src)
                        else:
                            bb = bv[rows, :].rearrange("p (j two d) -> p two j d", two=2, d=D)[:, odd]
                            last = nc.vector.tensor_tensor(
                                dst, src, bb.unsqueeze(1).broadcast_to([64, 2, heads // 2, D]), ALU.add)
                    last.then_inc(S["v"][t], 1)
                if name == "spread" and phase != PH_B:
                    if (phase, use) == (PH_C, 1):
                        v.wait_ge(S["rope"][t], at("rope", 0, "done"))
                    else:
                        v.wait_ge(S["qk"][t], at("qk", use))
                    nc.vector.tensor_tensor(*spread_of(t, qk[:, t, 1], heads, heads - VECTOR_HEADS[phase, use], heads),
                                            ALU.mult).then_inc(S["v"][t], 1)
                if name in ("shift0", "shift1"):
                    n = int(name[-1])
                    v.wait_ge(S["att_ps"][t], at("att_ps", use, f"scores{n}"))
                    most = rmax[:, t, n * hh:(n + 1) * hh]
                    ps = bank[2 * t + n][:, 0:hh * T].rearrange("p (h k) -> p h k", k=T)
                    mine = P_(t)[:, n * hh * T:(n + 1) * hh * T].rearrange("p (h k) -> p h k", k=T)
                    if phase == PH_B:
                        nc.vector.scalar_tensor_tensor(mine, ps, sS[:, :], bias[:, 8 * n:8 * n + 8, :],
                                                       ALU.mult, ALU.add).then_inc(S["soft"][t], 1)
                        v.wait_ge(S["soft"][t], at("soft", 0, f"biased{n}"))
                        nc.vector.tensor_reduce(most, mine, AX.X, ALU.max).then_inc(S["shift"][t], 1)
                    else:
                        nc.vector.tensor_reduce(most, ps, AX.X, ALU.max).then_inc(S["shift"][t], 1)
                        v.wait_ge(S["shift"][t], at("shift", use, f"max{n}"))
                        nc.vector.tensor_tensor(mine, ps, most.unsqueeze(2).broadcast_to([P, hh, T]), ALU.subtract)\
                            .then_inc(S["shift"][t], 1)
                if name == "weigh" and phase != PH_B:
                    v.wait_ge(S["att_ps"][t], at("att_ps", use, "o"))
                    ov = lo(t)[:, 0:heads * (D + 1)].rearrange("p (h d) -> p h d", d=D + 1)
                    nc.vector.reciprocal(rinv[:, t, 0:heads].unsqueeze(2), ov[:, :, D:D + 1]).then_inc(S["o"][t], 1)
                    v.wait_ge(S["o"][t], at("o", use, "inv"))
                    nc.vector.tensor_tensor(o[:, t].rearrange("p (h d) -> p h d", d=D), ov[:, :, 0:D],
                                            rinv[:, t, 0:heads].unsqueeze(2).broadcast_to([P, heads, D]), ALU.mult)\
                        .then_inc(S["o"][t], 1)

            def add_output(at, use, t, dst):
                v.wait_ge(S["out_ps"][t], at("out_ps", use, "out"))
                nc.vector.tensor_tensor(dst[:, t], hi(t)[:, P:2 * P], dst[:, t], ALU.add)\
                    .then_inc(S["x_added"][t], 1)

            def rope(at, t, dst):
                def n64(ap):
                    return ap.rearrange("p (n k) -> p n k", k=T)

                cos = w["cosT"][:, :].unsqueeze(1).broadcast_to([P, 4, T])
                sin = w["sinT"][:, :].unsqueeze(1).broadcast_to([P, 4, T])
                nc.vector.tensor_tensor(n64(P_(t)[:, 512:768]), n64(lo(t)[:, 0:256]), cos, ALU.mult)\
                    .then_inc(S["rope"][t], 1)
                nc.vector.tensor_tensor(n64(P_(t)[:, 768:1024]), n64(lo(t)[:, 256:512]), sin, ALU.mult)\
                    .then_inc(S["rope"][t], 1)
                v.wait_ge(S["rope"][t], at("rope", 0, "sin"))
                nc.vector.tensor_tensor(dst, P_(t)[:, 512:768].rearrange("p (n k) -> p n k", n=2),
                                        P_(t)[:, 768:1024].rearrange("p (n k) -> p n k", n=2), ALU.add)\
                    .then_inc(S["rope"][t], 1)

            def keep_logits(phase, at, t):
                E = routed[phase][1]
                v.wait_ge(S["logit_ps"][t], at("logit_ps"))
                nc.vector.tensor_copy(lg[:, t, 0:E], lo(t)[:, 0:E]).then_inc(S["logits"][t], 1)

            def routing(phase, r, name):
                _, E, K = routed[phase]
                n = [{"choose": 0, "ranked": RANKED[phase], "places": RANKED[phase] + 1}[name]]

                def link(ins):
                    ins.then_inc(route, 1)
                    v.wait_ge(route, route_at(phase, r, n[0]))
                    n[0] += 1

                L, K_ = lr[:, :, 0:E], key[:, :, 0:E]
                sl = [s_[:, :, 0:E] for s_ in sel]
                ch = chosen[:, :, 0:E]
                if name == "choose":
                    f8 = first8[:, 0:E].unsqueeze(1).broadcast_to([P, G, E])
                    for lane in range(G):
                        v.wait_ge(S["logits"][lane], counter(phase, r)("logits"))
                    src = lg[:, :, 0:E]
                    for s_ in range(K):
                        most = top[:, :, s_:s_ + 1]
                        link(nc.vector.tensor_reduce(most, src, AX.X, ALU.max))
                        link(nc.vector.tensor_tensor(L, src, most.broadcast_to([P, G, E]), ALU.subtract))
                        link(nc.vector.scalar_tensor_tensor(K_, L, 0.0, f8, ALU.is_ge, ALU.mult))
                        link(nc.vector.tensor_reduce(first[:, :, :], K_, AX.X, ALU.max))
                        link(nc.vector.tensor_tensor(sl[s_], K_, first[:, :, :].broadcast_to([P, G, E]), ALU.is_ge))
                        if s_ + 1 < K:
                            link(nc.vector.scalar_tensor_tensor(L, sl[s_], -3e38, L, ALU.mult, ALU.add))
                            src = L
                    if K == 2:
                        link(nc.vector.tensor_tensor(ch, sl[0], sl[1], ALU.add))
                    else:
                        link(nc.vector.tensor_copy(ch, sl[0]))
                    assert n[0] == CHOSEN[phase] + 1 == RANKED[phase]
                    return
                if name == "ranked":
                    v.wait_ge(rank_ps, r + (1 if phase == PH_A else R + 1))
                    link(nc.vector.tensor_tensor(row[:, :, 0:E],
                                                 lo(G - 1)[:, 0:G * E].rearrange("p (g e) -> p g e", e=E),
                                                 ecap[:, 0:E].unsqueeze(1).broadcast_to([P, G, E]), ALU.add))
                    return
                v.wait_ge(collected, r + (R + 1 if phase == PH_C else 1))
                if K == 2:
                    v.wait_ge(route_exp, r + 1)
                    link(nc.vector.tensor_scalar(e2[:, :], e2[:, :], 1.0, None, ALU.add))
                    link(nc.vector.reciprocal(w12[:, :, 0], e2[:, :]))
                    link(nc.vector.tensor_scalar(w12[:, :, 1], w12[:, :, 0], -1.0, 1.0, ALU.mult, ALU.add))
                    link(nc.vector.tensor_copy(w_all[:, bass.ds(r * G, G), :], w12[:, :, :]))
                for s_ in range(K):
                    link(nc.vector.tensor_tensor(K_, sl[s_], row[:, :, 0:E], ALU.mult))
                    link(nc.vector.tensor_reduce(row12[:, :, s_:s_ + 1], K_, AX.X, ALU.add))
                link(nc.vector.tensor_copy(row_all[:, bass.ds(r * G, G), 0:K], row12[:, :, 0:K]))
                link(nc.vector.tensor_reduce(key[:, 0, 0:E].unsqueeze(2), ch.rearrange("p g e -> p e g"), AX.X, ALU.add))
                link(nc.vector.tensor_tensor(taken[:, 0:E], taken[:, 0:E], key[:, 0, 0:E], ALU.add))
                nc.vector.tensor_copy(taken_bf[:, 0:E], taken[:, 0:E])
                link(nc.vector.tensor_copy(row_idx[:, :, 0:K], row12[:, :, 0:K]))
                assert n[0] == ROUTE[phase], (phase, n[0])

            def slot_table(phase, first):
                m, E, K = routed[phase]
                ns = m["ns"]
                n = [first]

                def link(ins):
                    n[0] += 1
                    ins.then_inc(table, 1)
                    v.wait_ge(table, n[0])

                v.wait_ge(count_ps, 1 if phase == PH_A else 2)
                link(nc.vector.tensor_copy(cnt[:, 0:E], lo(0)[:, 0:E]))
                link(nc.vector.tensor_copy(cnt_i[:, 0:E], cnt[:, 0:E]))
                nb = nblk[:, 0:E]
                link(nc.vector.tensor_scalar(nb, cnt[:, 0:E], 1.0 / P, (P - 1 - (P - 1) / 2) / P, ALU.mult, ALU.add))
                link(nc.vector.tensor_scalar(nb, nb, MAGIC, None, ALU.add))
                link(nc.vector.tensor_scalar(nb, nb, MAGIC, None, ALU.subtract))
                link(nc.vector.memset(cblk[:, 0:1], 0.0))
                for e in range(E):
                    link(nc.vector.tensor_tensor(cblk[:, e + 1:e + 2], cblk[:, e:e + 1], nblk[:, e:e + 1], ALU.add))
                link(nc.vector.scalar_tensor_tensor(delta[:, 0:E], cblk[:, 0:E], -float(P), ecap[:, 0:E],
                                                    ALU.mult, ALU.add))
                link(nc.vector.memset(delta[:, E:E + 1], float(E * CAP)))
                sz = ns * (E + 1)
                reached = big[:, 0, 0:sz].rearrange("p (j e) -> p j e", e=E + 1)
                owner = big[:, 1, 0:sz].rearrange("p (j e) -> p j e", e=E + 1)
                term = big[:, 2, 0:sz].rearrange("p (j e) -> p j e", e=E + 1)
                num = slot_f[:, 0:ns, 2]

                def per_e(ap):
                    return ap[:, 0:E + 1].unsqueeze(1).broadcast_to([P, ns, E + 1])

                link(nc.vector.tensor_tensor(reached, num.unsqueeze(2).broadcast_to([P, ns, E + 1]), per_e(cblk),
                                             ALU.is_ge))
                link(nc.vector.tensor_tensor(owner[:, :, 0:E], reached[:, :, 0:E], reached[:, :, 1:E + 1],
                                             ALU.subtract))
                link(nc.vector.tensor_copy(owner[:, :, E:E + 1], reached[:, :, E:E + 1]))
                link(nc.vector.tensor_tensor(term, owner, per_e(delta), ALU.mult))
                link(nc.vector.tensor_reduce(slot_f[:, 0:ns, 0:1], term, AX.X, ALU.add))
                link(nc.vector.tensor_scalar(term[:, :, 0], owner[:, :, E], -float(P), float(P), ALU.mult, ALU.add))
                link(nc.vector.tensor_tensor(term[:, :, 0], term[:, :, 0], num, ALU.mult))
                link(nc.vector.tensor_tensor(slot_f[:, 0:ns, 0], slot_f[:, 0:ns, 0], term[:, :, 0], ALU.add))
                link(nc.vector.tensor_tensor(term, owner, per_e(eid), ALU.mult))
                link(nc.vector.tensor_reduce(slot_f[:, 0:ns, 1:2], term, AX.X, ALU.add))
                link(nc.vector.tensor_scalar(slot_f[:, 0:ns, 1], slot_f[:, 0:ns, 1], float(E - 1), None, ALU.min))
                link(nc.vector.tensor_copy(slot_i[:, 0:ns, :], slot_f[:, 0:ns, 0:2]))
                assert n[0] == TABLE[phase_of_moe(phase)], n[0]
                link(nc.vector.tensor_copy(ddelta[:, 0:1], delta[:, 0:1]))
                link(nc.vector.tensor_tensor(ddelta[:, 1:E], delta[:, 1:E], delta[:, 0:E - 1], ALU.subtract))
                rows = row_all[:, :, 0:K]
                room = qkvq[:, :, :, :].rearrange("p g i k -> p (g i k)")
                at_least = room[:, 0:NT * K * E].rearrange("p (n k e) -> p n k e", k=K, e=E)
                less = room[:, NT * K * E:NT * K * (E + 1)].rearrange("p (n k) -> p n k", k=K)
                link(nc.vector.tensor_tensor(at_least, rows.unsqueeze(3).broadcast_to([P, NT, K, E]),
                                             ecap[:, 0:E].unsqueeze(1).unsqueeze(1).broadcast_to([P, NT, K, E]),
                                             ALU.is_ge))
                link(nc.vector.tensor_tensor(at_least, at_least,
                                             ddelta[:, 0:E].unsqueeze(1).unsqueeze(1).broadcast_to([P, NT, K, E]),
                                             ALU.mult))
                link(nc.vector.tensor_reduce(less.unsqueeze(3), at_least, AX.X, ALU.add))
                link(nc.vector.tensor_tensor(less, rows, less, ALU.subtract))
                link(nc.vector.tensor_copy(pos_idx[:, :, 0:K], less))
                link(nc.vector.memset(taken[:, :], 0.0))
                link(nc.vector.memset(taken_bf[:, :], 0.0))
                assert n[0] == TABLE_POS[PH_Q if phase == PH_A else PH_O], n[0]

            def slots(phase):
                m = moe[phase]
                up, F = m["up"], m["F"]

                def stage(name, use, t, r):
                    at = counter(phase, r)
                    if name == "weights":
                        e = v.value_load(slot_i[0:1, bass.ds(r * G + t, 1), 1], min_val=0, max_val=m["E"] - 1)
                        if not (isinstance(r, int) and r == 0):
                            v.wait_ge(S["slot_ps"][t], counter(phase, r - 1)("slot_ps", 0, "y"))
                        nc.vector.tensor_copy(expert_w[:, t, 0:up], m["w1"][:, bass.ds(e * up, up)])
                        nc.vector.tensor_copy(expert_w[:, t, up:up + F], m["w2"][:, bass.ds(e * F, F)])\
                            .then_inc(S["slot_y"][t], 1)
                    if name == "up" and phase == PH_M1:
                        v.wait_ge(S["slot_act"][t], at("slot_act", 0, "act"))
                        nc.vector.tensor_tensor(big[:, t, 0:F1], hi(t)[:, :], big[:, t, 0:F1], ALU.mult)\
                            .then_inc(S["slot_y"][t], 1)
                    if name == "down":
                        if not (isinstance(r, int) and r == 0):
                            v.wait_ge(S["slot_out"][t], counter(phase, r - 1)("slot_out"))
                        v.wait_ge(S["slot_ps"][t], at("slot_ps", 0, "y"))
                        nc.vector.tensor_copy(o[:, t], hi(t)[:, 0:C]).then_inc(S["slot_y"][t], 1)

                run(v, "dve", phase, stage)

            def quantise(at, event, i, t, src, dst, col):
                if event == "a":
                    ins = nc.vector.tensor_scalar(dst, src, qinv[:, col:col + 1], MAGIC, ALU.mult, ALU.add)
                elif event == "b":
                    v.wait_ge(S["quant"][t], at("quant", i, "a"))
                    ins = nc.vector.tensor_scalar(dst, dst, qmagic[:, col:col + 1], 0.0, ALU.subtract, ALU.max)
                else:
                    v.wait_ge(S["quant"][t], at("quant", i, "b"))
                    ins = nc.vector.tensor_scalar(dst, dst, QMAX, qzero[:, col:col + 1], ALU.min, ALU.subtract)
                ins.then_inc(S["quant"][t], 1)

            def stage_a(name, use, t, r):
                at = counter(PH_A, r)
                if name in ("stats", "norm"):
                    layer_norm(PH_A, name, use, t, r)
                if (PH_A, use) in att:
                    attention_stage(PH_A, name, use, t, at)
                if name == "output":
                    if use < 2:
                        v.wait_ge(S["pool_x"][t], at("pool_x", use + 1))
                    add_output(at, use, t, x if use < 2 else h)
                if name == "router":
                    keep_logits(PH_A, at, t)
                if name in ("choose", "ranked", "places"):
                    routing(PH_A, r, name)

            run(v, "dve", PH_A, stage_a)
            slot_table(PH_A, 0)
            v.wait_ge(w_moe0, 16 * len(moe0))
            slots(PH_M0)
            v.wait_ge(w_layer1, 16 * len(layer1))
            phase_over(v, PH_M0)

            def stage_q(name, use, t, r):
                at = counter(PH_Q, r)
                if name == "combine":
                    if not (isinstance(r, int) and r == 0):
                        v.wait_ge(S["stored"][t], counter(PH_Q, r - 1)("stored"))
                    v.wait_ge(S["loaded"][t], at("loaded", 0))
                    v.wait_ge(S["gathered"][t], at("gathered", K0 - 1))
                    wt = w_t[:, t]
                    nc.vector.tensor_copy(wt, w_all[:, bass.ds(r * G + t, 1), :].rearrange("p a k -> p (a k)"))\
                        .then_inc(S["logits"][t], 1)
                    v.wait_ge(S["logits"][t], at("logits"))
                    for s_ in range(K0):
                        if s_ == 1:
                            v.wait_ge(S["x_added"][t], at("x_added", 0))
                        nc.vector.scalar_tensor_tensor(x[:, t], big[:, t, s_ * C:(s_ + 1) * C], wt[:, s_:s_ + 1],
                                                       xin[:, t] if s_ == 0 else x[:, t], ALU.mult, ALU.add)\
                            .then_inc(S["x_added"][t], 1)
                if name in ("stats", "norm"):
                    layer_norm(PH_Q, name, 0, t, r)
                if name == "rope":
                    v.wait_ge(S["att_ps"][t], at("att_ps", 0, "proj"))
                    rope(at, t, qkv[:, 0:2, bass.ds(r * (G * P) + t * P, P)])

            run(v, "dve", PH_Q, stage_q)

            n = [0]

            def link(ins):
                n[0] += 1
                ins.then_inc(stat_dve, 1)
                v.wait_ge(stat_dve, n[0])

            def ranges(src, count, most, least):
                for i in range(count):
                    link(nc.vector.tensor_reduce(stats[:, most + i:most + i + 1], src(i), AX.X, ALU.max))
                    link(nc.vector.tensor_reduce(stats[:, least + i:least + i + 1], src(i), AX.X, ALU.min))
                link(nc.vector.tensor_scalar(stats[:, least:least + count], stats[:, least:least + count],
                                             -1.0, None, ALU.mult))

            def quantisers(col, count, most, least):
                c = slice(col, col + count)
                link(nc.vector.tensor_tensor(qstep[:, c], gstats[:, most:most + count],
                                             gstats[:, least:least + count], ALU.add))
                link(nc.vector.tensor_scalar(qstep[:, c], qstep[:, c], 1.0 / QMAX, 1e-12, ALU.mult, ALU.add))
                link(nc.vector.reciprocal(qinv[:, c], qstep[:, c]))
                link(nc.vector.tensor_tensor(qzero[:, c], gstats[:, least:least + count], qinv[:, c], ALU.mult))
                link(nc.vector.tensor_scalar(qzero[:, c], qzero[:, c], MAGIC, None, ALU.add))
                link(nc.vector.tensor_scalar(qzero[:, c], qzero[:, c], MAGIC, None, ALU.subtract))
                link(nc.vector.tensor_scalar(qmagic[:, c], qzero[:, c], -1.0, MAGIC, ALU.mult, ALU.add))
                link(nc.vector.tensor_scalar(qhigh[:, c], qmagic[:, c], QMAX, None, ALU.add))

            phase_over(v, PH_Q)
            v.wait_ge(const_ready, 2)
            v.wait_ge(fire_act, 1)
            nc.vector.tensor_scalar(posn, posn, w["fire_L"][:, :], None, ALU.max).then_inc(fire_dve, 1)
            v.wait_ge(fire_act, 3)
            nc.vector.tensor_scalar(posn, posn, 1e-6, None, ALU.add).then_inc(fire_dve, 1)
            v.wait_ge(fire_dve, 2)
            nc.vector.reciprocal(posn, posn).then_inc(fire_dve, 1)
            ranges(lambda i: qkv[:, i, :], 3, 0, 3)
            v.wait_ge(fire_pe, 1)
            for n_ in range(2):
                last = nc.vector.tensor_tensor(bias[:, :, 32 * n_:32 * n_ + 32],
                                               bank[n_][:, :].rearrange("p (j h) -> p h j", h=16),
                                               w["fire_b2"][:, :].unsqueeze(2).broadcast_to([P, 16, 32]), ALU.add)
            last.then_inc(fire_dve, 1)
            v.wait_ge(fire_dve, 4)
            nc.vector.tensor_tensor(bias[:, :, :], bias[:, :, :],
                                    causal[:, :].unsqueeze(1).broadcast_to([P, 16, T]), ALU.add)\
                .then_inc(fire_dve, 1)
            v.wait_ge(fire_dve, 5)
            v.wait_ge(stat_all, 1)
            quantisers(0, 3, 0, 3)
            link(nc.vector.scalar_tensor_tensor(sS[:, :], qstep[:, 0:1], 8.0 ** -0.5, qstep[:, 1:2],
                                                ALU.mult, ALU.mult))
            assert n[0] == STAT_Y - 3

            def stage_b(name, use, t, r):
                at = counter(PH_B, r)
                if name == "quantise":
                    v.wait_ge(S["quant"][t], at("quant", 2, "a"))
                    for i in range(3):
                        nc.vector.tensor_scalar(qkvq[:, t, i], qkvq[:, t, i], qmagic[:, i:i + 1], qhigh[:, i:i + 1],
                                                ALU.max, ALU.min).then_inc(S["quant"][t], 1)
                attention_stage(PH_B, name, use, t, at)
                if name in ("normalise0", "normalise1"):
                    n = name[-1]
                    heads = slice(8 * int(n), 8 * int(n) + 8)
                    v.wait_ge(S["probs"][t], at("probs", 0, n))
                    pv = P_(t).rearrange("p (h k) -> p h k", k=T)[:, heads]
                    nc.vector.tensor_reduce(rsum[:, t, heads], pv, AX.X, ALU.add).then_inc(S["soft"][t], 1)
                    v.wait_ge(S["soft"][t], at("soft", 0, "sum" + n))
                    nc.vector.reciprocal(rinv[:, t, heads], rsum[:, t, heads]).then_inc(S["soft"][t], 1)
                    v.wait_ge(S["soft"][t], at("soft", 0, "inv" + n))
                    nc.vector.scalar_tensor_tensor(pv, pv, QMAX, rinv[:, t, heads].unsqueeze(2)
                                                   .broadcast_to([P, 8, T]), ALU.mult, ALU.mult)\
                        .then_inc(S["soft"][t], 1)
                if name == "weigh":
                    v.wait_ge(S["att_ps"][t], at("att_ps", 0, "o"))
                    nc.vector.tensor_scalar(
                        qkv[:, 0, bass.ds(r * (G * P) + t * P, P)].rearrange("p (h d) -> p h d", d=8),
                        lo(t)[:, 0:144].rearrange("p (h d) -> p h d", d=9)[:, :, 0:8],
                        qstep[:, 2:3], 1.0 / QMAX, ALU.mult, ALU.mult).then_inc(S["o"][t], 1)

            run(v, "dve", PH_B, stage_b)

            phase_over(v, PH_B)
            ranges(lambda i: qkv[:, 0, :], 1, 6, 7)
            assert n[0] == STAT_Y
            v.wait_ge(stat_all, 2)
            quantisers(3, 1, 6, 7)

            def stage_c(name, use, t, r):
                at = counter(PH_C, r)
                if name == "quantise":
                    for event in "abc":
                        quantise(at, event, 0, t, qkv[:, 0, bass.ds(r * (G * P) + t * P, P)], h2[:, t], 3)
                if name == "y_out":
                    v.wait_ge(S["loaded"][t], at("loaded", 1))
                    if not (isinstance(r, int) and r == 0):
                        v.wait_ge(S["stored"][t], counter(PH_C, r - 1)("stored"))
                    v.wait_ge(S["out_ps"][t], at("out_ps", 0, "out"))
                    nc.vector.scalar_tensor_tensor(x[:, t], hi(t)[:, P:2 * P], qstep[:, 3:4], xin[:, t],
                                                   ALU.mult, ALU.add).then_inc(S["x_added"][t], 1)
                if name in ("stats", "norm"):
                    layer_norm(PH_C, name, use, t, r)
                if (PH_C, use) in att:
                    attention_stage(PH_C, name, use, t, at)
                if name == "weigh" and use == 0:
                    v.wait_ge(S["o"][t], at("o", 0, "done"))
                    nc.vector.tensor_tensor(x[:, t], x[:, t], o[:, t], ALU.add).then_inc(S["x_added"][t], 1)
                if name == "convolve":
                    v.wait_ge(S["rows_T"][t], at("rows_T", 2))
                    nc.vector.tensor_scalar(hT[:, t], oT[:, t], w["f1_conv"][:, 2:3], None, ALU.mult)\
                        .then_inc(S["conv"][t], 1)
                    for back in (1, 2):
                        v.wait_ge(S["conv"][t], at("conv", back - 1))
                        rows = hT[:, t].rearrange("p (b k) -> p b k", b=2)[:, :, back:T]
                        before = oT[:, t].rearrange("p (b k) -> p b k", b=2)[:, :, 0:T - back]
                        nc.vector.scalar_tensor_tensor(rows, before, w["f1_conv"][:, 2 - back:3 - back], rows,
                                                       ALU.mult, ALU.add).then_inc(S["conv"][t], 1)
                if name == "rope":
                    rope(at, t, qk[:, t])
                if name == "output":
                    add_output(at, 1, t, h)
                if name == "router":
                    keep_logits(PH_C, at, t)
                if name in ("choose", "ranked", "places"):
                    routing(PH_C, r, name)

            run(v, "dve", PH_C, stage_c)
            slot_table(PH_C, TABLE_POS[PH_Q])
            slots(PH_M1)
            phase_over(v, PH_M1)

            def stage_o(name, use, t, r):
                at = counter(PH_O, r)
                if name == "combine":
                    if not (isinstance(r, int) and r == 0):
                        v.wait_ge(S["stored"][t], counter(PH_O, r - 1)("stored"))
                    v.wait_ge(S["loaded"][t], at("loaded", 0))
                    v.wait_ge(S["gathered"][t], at("gathered", 0))
                    nc.vector.tensor_tensor(x[:, t], xin[:, t], big[:, t, 0:C], ALU.add)\
                        .then_inc(S["x_added"][t], 1)

            run(v, "dve", PH_O, stage_o)


def kernel(**inputs):
    import numpy as np
    import concourse.bacc as bacc
    from concourse import mybir as mb
    from concourse.bass_utils import run_bass_kernel_spmd

    def g(name):
        return np.asarray(inputs[name])

    def col(v):
        return v.reshape(-1, 1)

    def rows(v, n=128):
        return np.tile(v.reshape(1, -1), (n, 1))

    def chunks(m):
        return m.reshape(-1, 128, 128).transpose(1, 0, 2)

    def swapped(m):
        return m.reshape(128, 16, 2, 4)[:, :, ::-1, :].reshape(128, 128)

    def spread(m):
        return np.repeat(m.reshape(128, 4, 1, 8), 4, axis=2).reshape(128, 128)

    freq = (1.0 / 10000.0 ** (np.arange(0, 8, 2, dtype=np.float32) / 8)).astype(np.float32)
    angle = (np.arange(64, dtype=np.float32)[None, :] * freq[:, None]).astype(np.float32)
    cos = np.tile(np.cos(angle), (32, 1)).astype(np.float32)
    sin = np.tile(np.concatenate([-np.sin(angle), np.sin(angle)]), (16, 1)).astype(np.float32)

    wqkv, bqkv, fqkv = g("L0_attn_w_qkv"), g("L0_attn_b_qkv"), g("L1_ffn_attn_w")
    wk1 = spread(g("L1_attn_Wk"))
    arrays = {
        "x": g("x").reshape(4096, 128), "ctx": g("ctx_1024").reshape(4096, 128),
        "fire_w1": col(g("L1_attn_fire_w1")), "fire_b1": col(g("L1_attn_fire_b1")), "fire_w2": g("L1_attn_fire_w2"),
        "fire_b2": rows(g("L1_attn_fire_b2")), "fire_c": rows(g("L1_attn_fire_c"), 32),
        "fire_L": rows(g("L1_attn_fire_L"), 32),
        "a0_g": col(g("L0_attn_ln_gamma")), "a0_b": col(g("L0_attn_ln_beta")), "a0_wqkv": wqkv,
        "a0_bq": col(bqkv[0:128]), "a0_bk": col(bqkv[128:256]), "a0_bv": rows(bqkv[256:384]),
        "a0_wout": g("L0_attn_w_out"), "a0_bout": rows(g("L0_attn_b_out")),
        "x0_wq": g("L0_xattn_Wq"), "x0_wk": g("L0_xattn_Wk"), "x0_wv": g("L0_xattn_Wv"), "x0_wo": g("L0_xattn_Wo"),
        "x0_bq": col(g("L0_xattn_bq")), "x0_bk": col(g("L0_xattn_bk")), "x0_bv": rows(g("L0_xattn_bv")),
        "x0_bo": rows(g("L0_xattn_bo")),
        "f0_g1": col(g("L0_ffn_ln1_w")), "f0_g2": col(g("L0_ffn_ln2_w")), "f0_wqkv": g("L0_ffn_c_attn_w"),
        "f0_wo": g("L0_ffn_c_proj_w"), "f0_wr": g("L0_ffn_router_w"),
        "f0_w1": g("L0_ffn_w1"), "f0_w2": chunks(g("L0_ffn_w2")),
        "cosT": cos, "sinT": sin,
        "a1_wq": g("L1_attn_Wq"), "a1_wqs": swapped(g("L1_attn_Wq")), "a1_wk": wk1, "a1_wks": swapped(wk1),
        "a1_wv": spread(g("L1_attn_Wv")), "a1_wo": g("L1_attn_Wproj"),
        "x1_wq": g("L1_xattn_Wq").T, "x1_wk": g("L1_xattn_Wk").T, "x1_wv": g("L1_xattn_Wv").T,
        "f1_g1": col(g("L1_ffn_ln1_w")), "f1_b1": col(g("L1_ffn_ln1_b")),
        "f1_g2": col(g("L1_ffn_ln2_w")), "f1_b2": col(g("L1_ffn_ln2_b")),
        "f1_conv": g("L1_ffn_conv_w").reshape(128, 3),
        "f1_wq": fqkv[:, 0:128], "f1_wqs": swapped(fqkv[:, 0:128]),
        "f1_wk": fqkv[:, 128:256], "f1_wks": swapped(fqkv[:, 128:256]), "f1_wv": fqkv[:, 256:384],
        "f1_wo": g("L1_ffn_proj_w"), "f1_wr": g("L1_ffn_router_w"),
        "f1_wv13": g("L1_ffn_expert_wv").transpose(1, 0, 2), "f1_w2": chunks(g("L1_ffn_expert_proj")),
    }
    arrays = {"in_" + n: np.ascontiguousarray(v) for n, v in arrays.items()}
    nc = bacc.Bacc("TRN2", target_bir_lowering=False, num_devices=1)
    aps = {n[3:]: nc.dram_tensor(n, v.shape, mb.dt.from_np(v.dtype), kind="ExternalInput").ap()
           for n, v in arrays.items()}
    for n, rows_ in (("_mid", N), ("_mid2", N), ("_rows0", E0 * CAP + P), ("_rows1", E1 * CAP + P),
                     ("_out0", NS0 * P), ("_out1", NS1 * P)):
        aps[n] = nc.dram_tensor("scratch" + n, (rows_, 128), mb.dt.float32, kind="Internal").ap()
    out = nc.dram_tensor("out", (4096, 128), mb.dt.float32, kind="ExternalOutput").ap()
    decoder_kernel(nc, aps, out)
    r = run_bass_kernel_spmd(nc, [arrays], core_ids=[0])
    return r.results[0]["out"].reshape(64, 64, 128)
```
